# Optimizing a Trainium2 kernel written in Bass

```python
import numpy as np
import jax
import jax.numpy as jnp

def _softmax(x, axis=-1):
    return jax.nn.softmax(x, axis=axis)

def _gelu(x):
    return jax.nn.gelu(x, approximate=True)

def _silu(x):
    return jax.nn.silu(x)

def _sigmoid(x):
    return jax.nn.sigmoid(x)

def _layernorm(x, axis=-1, eps=1e-05):
    m = jnp.mean(x, axis=axis, keepdims=True)
    v = jnp.var(x, axis=axis, keepdims=True)
    return (x - m) / jnp.sqrt(v + eps)

def _scatter_add(tgt, idx, src, axis=0):
    return tgt.at[idx].add(src)

def _segment_sum(src, seg, n):
    return jax.ops.segment_sum(src, seg, n)
kernel_name = 'mk_gnn_ffn_d1_gnn_r8_5dc0b3'

def setup_inputs(seed: int=0):
    np.random.seed(seed)
    _w = jnp.asarray

    def _rec_inputs():
        import jax
        import jax.numpy as jnp
        _gk = jax.random.key(seed)
        x = -0.0002117 + 1 * jax.random.normal(jax.random.fold_in(_gk, 1), (6250, 512), jnp.float32)
        _s = jax.random.randint(jax.random.fold_in(_gk, 2), (50000,), 0, 6250, jnp.int32)
        _d = jax.random.randint(jax.random.fold_in(_gk, 3), (50000,), 0, 6250, jnp.int32)
        _loop = jnp.arange(6250, dtype=jnp.int32)
        src = jnp.concatenate([_s, _d, _loop])
        dst = jnp.concatenate([_d, _s, _loop])
        _o = jnp.argsort(dst, stable=True)
        src = src[_o]
        dst = dst[_o]
        return (x, src, dst)
    x, src, dst = _rec_inputs()

    def _L0_gnn_setup():
        import jax, jax.numpy as jnp
        import numpy as np
        N = 6250
        E = 80000
        IN_DIM = 512
        H = 4
        HD = 128
        OD = H * HD
        NEG_SLOPE = 0.2
        EPS = 1e-05

        def _segment_softmax(logits, seg, num_segments):
            m = jax.ops.segment_max(logits, seg, num_segments=num_segments)
            ex = jnp.exp(logits - m[seg])
            s = jax.ops.segment_sum(ex, seg, num_segments=num_segments)
            return ex / (s[seg] + 1e-16)
        key = jax.random.key(seed)
        ks = jax.random.split(key, 8)
        x = jax.random.normal(ks[0], (N, IN_DIM), jnp.float32)
        edge_index = jax.random.randint(ks[1], (2, E), 0, N)
        Wh = jax.random.normal(ks[2], (H, IN_DIM, HD), jnp.float32) / np.sqrt(IN_DIM).astype(np.float32)
        att_src = jax.random.normal(ks[3], (H, HD), jnp.float32) / np.sqrt(HD).astype(np.float32)
        att_dst = jax.random.normal(ks[4], (H, HD), jnp.float32) / np.sqrt(HD).astype(np.float32)
        bias_h = jnp.zeros((H, HD), jnp.float32)
        W_out = jax.random.normal(ks[5], (OD, OD), jnp.float32) / np.sqrt(OD).astype(np.float32)
        b_out = jnp.zeros((OD,), jnp.float32)
        gamma = jnp.ones((OD,), jnp.float32)
        beta = jnp.zeros((OD,), jnp.float32)
        return dict(x=x, edge_index=edge_index, Wh=Wh, att_src=att_src, att_dst=att_dst, bias_h=bias_h, W_out=W_out, b_out=b_out, gamma=gamma, beta=beta)
    _L0_gnn_all = _L0_gnn_setup()
    _L0_gnn_in = {k: v for k, v in _L0_gnn_all.items() if k in ('Wh', 'att_src', 'att_dst', 'bias_h', 'W_out', 'b_out', 'gamma', 'beta')}
    del _L0_gnn_all

    def _L0_ffn_setup():
        import math
        import jax, jax.numpy as jnp
        import numpy as np
        B, T, D, FF, E = (32, 1024, 512, 256, 8)
        CAPACITY_FACTOR = 1.25
        CAP = int(math.ceil(CAPACITY_FACTOR * B * T / E))

        def _bank_residual(x2, Wr, br, W1, b1, W2, b2):
            N, d = x2.shape
            e = Wr.shape[1]
            logits = x2 @ Wr + br
            probs = jax.nn.softmax(logits, axis=-1)
            expert = jnp.argmax(probs, axis=-1)
            gate = jnp.take_along_axis(probs, expert[:, None], axis=-1)[:, 0]
            oneh = jax.nn.one_hot(expert, e, dtype=x2.dtype)
            pos = (jnp.cumsum(oneh, axis=0) * oneh).sum(-1).astype(jnp.int32) - 1
            keep = pos < CAP
            slot = expert.astype(jnp.int32) * CAP + jnp.minimum(pos, CAP - 1)
            xd = jnp.where(keep[:, None], x2, 0.0)
            buf = jnp.zeros((e * CAP, d), x2.dtype).at[slot].add(xd)
            buf = buf.reshape(e, CAP, d)
            h = jax.nn.gelu(jnp.einsum('ecd,edf->ecf', buf, W1) + b1[:, None, :], approximate=False)
            out = jnp.einsum('ecf,efd->ecd', h, W2) + b2[:, None, :]
            y = out.reshape(e * CAP, d)[slot]
            return y * (gate * keep.astype(x2.dtype))[:, None]
        key = jax.random.key(seed)
        ks = jax.random.split(key, 18)
        s = 0.02
        inp = {'x': jax.random.normal(ks[0], (B, T, D), dtype=jnp.float32), 'Wr_sp': jax.random.normal(ks[1], (D, E)) * s, 'br_sp': jnp.zeros((E,), jnp.float32), 'Wr_fq': jax.random.normal(ks[2], (D, E)) * s, 'br_fq': jnp.zeros((E,), jnp.float32), 'Ws1': jax.random.normal(ks[3], (D, FF)) * s, 'bs1': jnp.zeros((FF,), jnp.float32), 'Ws2': jax.random.normal(ks[4], (FF, D)) * s, 'bs2': jnp.zeros((D,), jnp.float32), 'W1_sp': jax.random.normal(ks[5], (E, D, FF)) * s, 'b1_sp': jnp.zeros((E, FF), jnp.float32), 'W2_sp': jax.random.normal(ks[6], (E, FF, D)) * s, 'b2_sp': jnp.zeros((E, D), jnp.float32), 'W1_fq': jax.random.normal(ks[7], (E, D, FF)) * s, 'b1_fq': jnp.zeros((E, FF), jnp.float32), 'W2_fq': jax.random.normal(ks[8], (E, FF, D)) * s, 'b2_fq': jnp.zeros((E, D), jnp.float32)}
        return inp
    _L0_ffn_all = _L0_ffn_setup()
    _L0_ffn_in = {k: v for k, v in _L0_ffn_all.items() if k in ('Wr_sp', 'br_sp', 'Wr_fq', 'br_fq', 'Ws1', 'bs1', 'Ws2', 'bs2', 'W1_sp', 'b1_sp', 'W2_sp', 'b2_sp', 'W1_fq', 'b1_fq', 'W2_fq', 'b2_fq')}
    del _L0_ffn_all
    return {'x': x, 'src': src, 'dst': dst, 'L0_gnn_Wh': _L0_gnn_in['Wh'], 'L0_gnn_att_src': _L0_gnn_in['att_src'], 'L0_gnn_att_dst': _L0_gnn_in['att_dst'], 'L0_gnn_bias_h': _L0_gnn_in['bias_h'], 'L0_gnn_W_out': _L0_gnn_in['W_out'], 'L0_gnn_b_out': _L0_gnn_in['b_out'], 'L0_gnn_gamma': _L0_gnn_in['gamma'], 'L0_gnn_beta': _L0_gnn_in['beta'], 'L0_ffn_Wr_sp': _L0_ffn_in['Wr_sp'], 'L0_ffn_br_sp': _L0_ffn_in['br_sp'], 'L0_ffn_Wr_fq': _L0_ffn_in['Wr_fq'], 'L0_ffn_br_fq': _L0_ffn_in['br_fq'], 'L0_ffn_Ws1': _L0_ffn_in['Ws1'], 'L0_ffn_bs1': _L0_ffn_in['bs1'], 'L0_ffn_Ws2': _L0_ffn_in['Ws2'], 'L0_ffn_bs2': _L0_ffn_in['bs2'], 'L0_ffn_W1_sp': _L0_ffn_in['W1_sp'], 'L0_ffn_b1_sp': _L0_ffn_in['b1_sp'], 'L0_ffn_W2_sp': _L0_ffn_in['W2_sp'], 'L0_ffn_b2_sp': _L0_ffn_in['b2_sp'], 'L0_ffn_W1_fq': _L0_ffn_in['W1_fq'], 'L0_ffn_b1_fq': _L0_ffn_in['b1_fq'], 'L0_ffn_W2_fq': _L0_ffn_in['W2_fq'], 'L0_ffn_b2_fq': _L0_ffn_in['b2_fq']}

def reference(x, src, dst, L0_gnn_Wh, L0_gnn_att_src, L0_gnn_att_dst, L0_gnn_bias_h, L0_gnn_W_out, L0_gnn_b_out, L0_gnn_gamma, L0_gnn_beta, L0_ffn_Wr_sp, L0_ffn_br_sp, L0_ffn_Wr_fq, L0_ffn_br_fq, L0_ffn_Ws1, L0_ffn_bs1, L0_ffn_Ws2, L0_ffn_bs2, L0_ffn_W1_sp, L0_ffn_b1_sp, L0_ffn_W2_sp, L0_ffn_b2_sp, L0_ffn_W1_fq, L0_ffn_b1_fq, L0_ffn_W2_fq, L0_ffn_b2_fq):
    import jax
    import jax.numpy as jnp

    def _L0_gnn_ref(x, edge_index, Wh, att_src, att_dst, bias_h, W_out, b_out, gamma, beta):
        import jax, jax.numpy as jnp
        import numpy as np
        N = 6250
        E = 80000
        IN_DIM = 512
        H = 4
        HD = 128
        OD = H * HD
        NEG_SLOPE = 0.2
        EPS = 1e-05

        def _segment_softmax(logits, seg, num_segments):
            m = jax.ops.segment_max(logits, seg, num_segments=num_segments)
            ex = jnp.exp(logits - m[seg])
            s = jax.ops.segment_sum(ex, seg, num_segments=num_segments)
            return ex / (s[seg] + 1e-16)
        loop = jnp.arange(N)
        src = jnp.concatenate([edge_index[0], loop])
        dst = jnp.concatenate([edge_index[1], loop])
        xp = jnp.einsum('ni,hio->hno', x, Wh)
        a_src = jnp.einsum('hno,ho->hn', xp, att_src)
        a_dst = jnp.einsum('hno,ho->hn', xp, att_dst)
        e = a_src[:, src] + a_dst[:, dst]
        e = jnp.where(e > 0, e, NEG_SLOPE * e)
        alpha = jax.vmap(lambda l: _segment_softmax(l, dst, N))(e)
        msgs = xp[:, src]
        out_h = jax.vmap(lambda a, m: jax.ops.segment_sum(a[:, None] * m, dst, num_segments=N))(alpha, msgs)
        out_h = out_h + bias_h[:, None, :]
        h = jnp.transpose(out_h, (1, 0, 2)).reshape(N, OD)
        y = h @ W_out.T + b_out
        mu = jnp.mean(y, axis=-1, keepdims=True)
        var = jnp.mean((y - mu) ** 2, axis=-1, keepdims=True)
        return (y - mu) / jnp.sqrt(var + EPS) * gamma + beta

    def _L0_ffn_ref(x, Wr_sp, br_sp, Wr_fq, br_fq, Ws1, bs1, Ws2, bs2, W1_sp, b1_sp, W2_sp, b2_sp, W1_fq, b1_fq, W2_fq, b2_fq):
        import math
        import jax, jax.numpy as jnp
        import numpy as np
        B, T, D, FF, E = (32, 1024, 512, 256, 8)
        CAPACITY_FACTOR = 1.25
        CAP = int(math.ceil(CAPACITY_FACTOR * B * T / E))

        def _bank_residual(x2, Wr, br, W1, b1, W2, b2):
            N, d = x2.shape
            e = Wr.shape[1]
            logits = x2 @ Wr + br
            probs = jax.nn.softmax(logits, axis=-1)
            expert = jnp.argmax(probs, axis=-1)
            gate = jnp.take_along_axis(probs, expert[:, None], axis=-1)[:, 0]
            oneh = jax.nn.one_hot(expert, e, dtype=x2.dtype)
            pos = (jnp.cumsum(oneh, axis=0) * oneh).sum(-1).astype(jnp.int32) - 1
            keep = pos < CAP
            slot = expert.astype(jnp.int32) * CAP + jnp.minimum(pos, CAP - 1)
            xd = jnp.where(keep[:, None], x2, 0.0)
            buf = jnp.zeros((e * CAP, d), x2.dtype).at[slot].add(xd)
            buf = buf.reshape(e, CAP, d)
            h = jax.nn.gelu(jnp.einsum('ecd,edf->ecf', buf, W1) + b1[:, None, :], approximate=False)
            out = jnp.einsum('ecf,efd->ecd', h, W2) + b2[:, None, :]
            y = out.reshape(e * CAP, d)[slot]
            return y * (gate * keep.astype(x2.dtype))[:, None]
        b, t, d = x.shape
        x2 = x.reshape(b * t, d)
        shared = jax.nn.gelu(x2 @ Ws1 + bs1, approximate=False) @ Ws2 + bs2
        y = shared
        y = y + _bank_residual(x2, Wr_sp, br_sp, W1_sp, b1_sp, W2_sp, b2_sp)
        y = y + _bank_residual(x2, Wr_fq, br_fq, W1_fq, b1_fq, W2_fq, b2_fq)
        return y.reshape(b, t, d)
    edge_index = jnp.stack([src, dst])
    x = x + _L0_gnn_ref(_layernorm(x, axis=-1), edge_index, L0_gnn_Wh, L0_gnn_att_src, L0_gnn_att_dst, L0_gnn_bias_h, L0_gnn_W_out, L0_gnn_b_out, L0_gnn_gamma, L0_gnn_beta)
    x = x + _L0_ffn_ref(_layernorm(x, axis=-1)[None], L0_ffn_Wr_sp, L0_ffn_br_sp, L0_ffn_Wr_fq, L0_ffn_br_fq, L0_ffn_Ws1, L0_ffn_bs1, L0_ffn_Ws2, L0_ffn_bs2, L0_ffn_W1_sp, L0_ffn_b1_sp, L0_ffn_W2_sp, L0_ffn_b2_sp, L0_ffn_W1_fq, L0_ffn_b1_fq, L0_ffn_W2_fq, L0_ffn_b2_fq)[0]
    return x

_drawn_inputs = setup_inputs


def setup_inputs(seed=0):
    import zlib

    import numpy as np

    out = dict(_drawn_inputs(seed))
    spreads = {'L0_gnn_bias_h': (0.0, 0.1),
     'L0_gnn_b_out': (0.0, 0.1),
     'L0_gnn_gamma': (1.0, 0.2),
     'L0_gnn_beta': (0.0, 0.1),
     'L0_ffn_br_sp': (0.0, 0.726),
     'L0_ffn_br_fq': (0.0, 0.8),
     'L0_ffn_bs1': (0.0, 0.613),
     'L0_ffn_bs2': (0.0, 0.1),
     'L0_ffn_b1_sp': (0.0, 0.8),
     'L0_ffn_b2_sp': (0.0, 0.503),
     'L0_ffn_b1_fq': (0.0, 0.8),
     'L0_ffn_b2_fq': (0.0, 0.505)}
    factors = {'L0_ffn_Wr_sp': 2.86,
     'L0_ffn_Wr_fq': 2.963,
     'L0_ffn_W1_sp': 4.544,
     'L0_ffn_W2_sp': 4.282,
     'L0_ffn_W1_fq': 4.579,
     'L0_ffn_W2_fq': 4.326}
    for name, (base, spread) in spreads.items():
        noise = np.random.default_rng([zlib.crc32(name.encode()), seed]).standard_normal(out[name].shape)
        drawn = base * np.exp(spread * noise) if base else spread * noise
        out[name] = jnp.asarray(drawn.astype(out[name].dtype))
    for name, factor in factors.items():
        out[name] = (out[name] * factor).astype(out[name].dtype)
    return out
```

```python
from contextlib import ExitStack

import concourse.bass as bass
from concourse import mybir

F32 = mybir.dt.float32
BF16 = mybir.dt.bfloat16
I32 = mybir.dt.int32
ALU = mybir.AluOpType
ACT = mybir.ActivationFunctionType
AX_X = mybir.AxisListType.X

P = 128
N = 6250
D = 512
KD = D // P
H = 4
HD = D // H
E = 106250
NT = (N + P - 1) // P
NP = NT * P
LAST = N - (NT - 1) * P
GE = 256
NG = (E + GE - 1) // GE
PAD = NG * GE - E
U = NG + NT - 1
CP = 116
NC = U // CP
TU = 2 * U
SLOPE = 0.2
EPS = 1e-5
BIG = 1.0e30
FF = 256
NE = 8
CAP = 5120
ET = NT + NE - 1
assert NC * CP == U


def build(nc, a, out, scratch="Internal", phases=9):
    with ExitStack() as ctx:
        ctx.enter_context(nc.allow_non_contiguous_dma(reason="small columns and index rows"))

        def dram(name, shape, dt=F32):
            if scratch == "Internal":
                return nc.dram_tensor(name, shape, dt).ap()
            return nc.dram_tensor("dbg_" + name, shape, dt, kind=scratch).ap()

        held = []

        def sem(name):
            held.append(nc.alloc_semaphore(name))
            return held[-1]

        def phase(run, *args):
            run(*args)
            nc.clear_and_free_semaphores(list(held))
            held.clear()
            nc.all_engine_barrier()

        def sems(name, n):
            return [sem(f"{name}{i}") for i in range(n)]

        def reused(eng, semaphore, value, n):
            if not isinstance(n, int) or n:
                eng.wait_ge(semaphore, value)

        def sb(stack, name, shape, dt=F32):
            return stack.enter_context(nc.sbuf_tensor(name, shape, dt))

        def ps(stack, name, shape, dt=F32):
            return stack.enter_context(nc.psum_tensor(name, shape, dt))

        xp_d = dram("xp_d", [NP, D])
        as_d = dram("as_d", [NP, H])
        ads_d = dram("ads_d", [NP, 2 * H])
        src_d = dram("src_d", [NG, GE], I32)
        dst_d = dram("dst_d", [NG, GE], I32)
        tile_d = dram("tile_d", [U], I32)
        row_d = dram("row_d", [10, U])
        car_d = dram("car_d", [9, U])

        ident = sb(ctx, "ident", [P, P])
        halfneg = sb(ctx, "halfneg", [P, 1])
        lg = sb(ctx, "lg", [P, NT, 2 * NE])
        sums, edges = ExitStack(), ExitStack()
        acc = sb(sums, "acc", [P, NT * D])
        accs = sb(sums, "accs", [P, NT, 9])
        srcE = sb(edges, "srcE", [P, TU], I32)
        dlE = sb(edges, "dlE", [P, TU])
        trow = sb(edges, "trow", [1, U], I32)
        x9E = sb(edges, "x9E", [P, TU, 9])

        def constants():
            cz, ci = sem("cz"), sem("ci")
            with nc.Block() as block:
                @block.gpsimd
                def _(pool):
                    nc.gpsimd.memset(ident[:], 0.0).then_inc(cz, 1)
                    nc.gpsimd.memset(halfneg[:], -0.5).then_inc(ci, 1)
                    pool.wait_ge(cz, 1)
                    nc.gpsimd.affine_select(out=ident[:], in_=ident[:], compare_op=ALU.not_equal, fill=1.0,
                                            base=0, pattern=[[-1, P]], channel_multiplier=1).then_inc(ci, 1)
                    pool.wait_ge(ci, 2)

        def project_nodes():
            with ExitStack() as c:
                wc = sb(c, "wc", [P, KD, H, HD])
                att = sb(c, "att", [P, 2, H, HD])
                wa = sb(c, "wa", [P, KD, 2 * H])
                wtmp = sb(c, "wtmp", [P, 2, H, HD])
                xin = sb(c, "xin", [P, 2, D])
                xl = sb(c, "xl", [P, 2, D])
                xT = sb(c, "xT", [P, 2, D])
                xp = sb(c, "xp", [P, 2, D])
                a8 = sb(c, "a8", [P, 2, 2 * H])
                st = sb(c, "st", [P, 2, 6])
                mv = sb(c, "mv", [P, 2, 2])
                ve = sb(c, "ve", [P, 2, 1])
                rstd = sb(c, "rstd", [P, 2, 1])
                psT = ps(c, "psT", [P, 2, D])
                psX = ps(c, "psX", [P, 2, D])
                psA = ps(c, "psA", [P, 2, D])
                w_in, tmp_ready, wa_ready = sem("w_in"), sem("tmp_ready"), sem("wa_ready")
                x_in, x_zero = sems("x_in", 2), sem("x_zero")
                st_ready, mv_ready = sems("st_ready", 2), sems("mv_ready", 2)
                ve_ready, rstd_ready = sems("ve_ready", 2), sems("rstd_ready", 2)
                xl_ready, xlT_ready, xT_ready = sems("xl_ready", 2), sems("xlT_ready", 2), sems("xT_ready", 2)
                proj_ready, xp_ready, stored = sems("proj_ready", 2), sems("xp_ready", 2), sems("stored", 2)
                passed = sem("passedA")
                HALF = NT // 2

                def loop(eng, steps):
                    steps(0, (0, 1))
                    with eng.Fori(1, HALF) as i:
                        steps(i, (0, 1))
                    steps(HALF, (0,))

                with nc.Block() as block:
                    @block.sync
                    def _(sp):
                        for h in range(H):
                            sp.dma_start(wc[:, :, h], a["Wh"][h].rearrange("(k p) o -> p k o", p=P)).then_inc(w_in, 16)
                        for s, name in ((0, "att_src"), (1, "att_dst")):
                            sp.dma_start(att[:, s], a[name].partition_broadcast(P)).then_inc(w_in, 16)

                        def steps(n, slots):
                            for j in slots:
                                if len(slots) == 2:
                                    reused(sp, xl_ready[j], n, n)
                                    sp.dma_start(xin[:, j], a["x"][bass.ts(n * 2 + j, P), :]).then_inc(x_in[j], 16)
                                else:
                                    sp.wait_ge(x_zero, 1)
                                    sp.dma_start(xin[0:LAST, j], a["x"][(NT - 1) * P:N, :]).then_inc(x_in[j], 16)
                        loop(sp, steps)

                    @block.vector
                    def _(dve):
                        dve.wait_ge(w_in, 16 * (H + 2))
                        for k in range(KD):
                            if k:
                                dve.wait_ge(wa_ready, k)
                            for s in range(2):
                                nc.vector.tensor_tensor(wtmp[:, s], wc[:, k], att[:, s], ALU.mult).then_inc(tmp_ready, 1)
                            dve.wait_ge(tmp_ready, 2 * k + 2)
                            nc.vector.tensor_reduce(wa[:, k], wtmp[:].rearrange("p s h o -> p (s h) o"), AX_X,
                                                    ALU.add).then_inc(wa_ready, 1)

                        def steps(n, slots):
                            if len(slots) == 1:
                                reused(dve, xl_ready[0], n, n)
                                nc.vector.memset(xin[:, 0], 0.0).then_inc(x_zero, 1)
                            for j in slots:
                                dve.wait_ge(x_in[j], n * 16 + 16)
                                nc.vector.bn_stats(st[:, j], xin[:, j]).then_inc(st_ready[j], 1)
                            for j in slots:
                                dve.wait_ge(st_ready[j], n + 1)
                                dve.sem_inc(passed, 1)
                                nc.vector.bn_aggr(mv[:, j], st[:, j]).then_inc(mv_ready[j], 1)
                            for j in slots:
                                dve.wait_ge(mv_ready[j], n + 1)
                                nc.vector.tensor_scalar_add(ve[:, j], mv[:, j, 1:2], EPS).then_inc(ve_ready[j], 1)
                            for j in slots:
                                dve.wait_ge(rstd_ready[j], n + 1)
                                reused(dve, xlT_ready[j], n, n)
                                nc.vector.tensor_scalar(xl[:, j], xin[:, j], mv[:, j, 0:1], rstd[:, j, 0:1],
                                                        ALU.subtract, ALU.mult).then_inc(xl_ready[j], 1)
                            for j in slots:
                                dve.wait_ge(proj_ready[j], n + 1)
                                reused(dve, stored[j], n * 48, n)
                                nc.vector.tensor_copy(a8[:, j], psA[:, j, 0:2 * H]).then_inc(xp_ready[j], 1)
                                nc.vector.tensor_copy(xp[:, j], psX[:, j]).then_inc(xp_ready[j], 1)
                        loop(dve, steps)

                    @block.gpsimd
                    def _(pool):
                        def steps(n, slots):
                            for j in slots:
                                pool.wait_ge(ve_ready[j], n + 1)
                                nc.gpsimd.tensor_tensor(rstd[:, j], ve[:, j], halfneg[:], ALU.pow).then_inc(rstd_ready[j], 1)
                        loop(pool, steps)

                    @block.tensor
                    def _(pe):
                        pe.wait_ge(wa_ready, KD)

                        def steps(n, slots):
                            for j in slots:
                                pe.wait_ge(xl_ready[j], n + 1)
                                reused(pe, xT_ready[j], n, n)
                                for k in range(KD):
                                    last = nc.tensor.transpose(psT[:, j, k * P:(k + 1) * P], xl[:, j, k * P:(k + 1) * P], ident[:])
                                last.then_inc(xlT_ready[j], 1)
                            for j in slots:
                                pe.wait_ge(xT_ready[j], n + 1)
                                reused(pe, xp_ready[j], n * 2, n)
                                for k in range(KD):
                                    xTk = xT[:, j, k * P:(k + 1) * P]
                                    nc.tensor.matmul(psX[:, j], xTk, wc[:, k].rearrange("p h o -> p (h o)"),
                                                     start=(k == 0), stop=(k == KD - 1))
                                    last = nc.tensor.matmul(psA[:, j, 0:2 * H], xTk, wa[:, k], start=(k == 0), stop=(k == KD - 1))
                                last.then_inc(proj_ready[j], 1)
                        loop(pe, steps)

                    @block.scalar
                    def _(act):
                        def steps(n, slots):
                            for j in slots:
                                act.wait_ge(xlT_ready[j], n + 1)
                                reused(act, proj_ready[j], n, n)
                                nc.scalar.copy(xT[:, j], psT[:, j]).then_inc(xT_ready[j], 1)
                            for j in slots:
                                act.wait_ge(xp_ready[j], n * 2 + 2)
                                row = bass.ts(n * 2 + j, P)
                                act.dma_start(xp_d[row, :], xp[:, j]).then_inc(stored[j], 16)
                                act.dma_start(as_d[row, :], a8[:, j, 0:H]).then_inc(stored[j], 16)
                                act.dma_start(ads_d[row, :], a8[:, j]).then_inc(stored[j], 16)
                        loop(act, steps)
                        act.wait_ge(stored[0], (HALF + 1) * 48)
                        act.wait_ge(stored[1], HALF * 48)

        def plan_units():
            with ExitStack() as c:
                padv = sb(c, "padv", [1, 2, PAD], I32)
                hi = sb(c, "hi", [1, NG], I32)
                hs = sb(c, "hs", [1, NG], I32)
                gi = sb(c, "gi", [1, NG], I32)
                gf = sb(c, "gf", [1, 2, NG])
                key1 = sb(c, "key1", [1, NG])
                key = sb(c, "key", [P, NG])
                lt = sb(c, "lt", [CP, NC, NG])
                ui = sb(c, "ui", [CP, NC], I32)
                uf = sb(c, "uf", [CP, NC])
                gu = sb(c, "gu", [CP, NC])
                tu = sb(c, "tu", [CP, NC])
                ti = sb(c, "ti", [CP, NC], I32)
                gc = sb(c, "gc", [CP, NC], I32)
                pad_set, edges_in, hi_in, iotas = sem("pad_set"), sem("edges_in"), sem("hi_in"), sem("iotas")
                b1, key_b, gidx, rows_in, rows_f, tile_out, tile_in = (
                    sem("b1"), sem("key_b"), sem("gidx"), sem("rows_in"), sem("rows_f"), sem("tile_out"), sem("tile_in"))

                with nc.Block() as block:
                    @block.sync
                    def _(sp):
                        for k, (to, name) in enumerate(((src_d, "src"), (dst_d, "dst"))):
                            flat = to.rearrange("g e -> (g e)")
                            sp.dma_start(flat[0:E], a[name]).then_inc(edges_in, 16)
                        sp.wait_ge(pad_set, 2)
                        for k, to in enumerate((src_d, dst_d)):
                            flat = to.rearrange("g e -> (g e)")
                            sp.dma_start(flat[E:NG * GE].rearrange("(a e) -> a e", a=1), padv[:, k]).then_inc(edges_in, 16)
                        sp.wait_ge(edges_in, 64)
                        sp.dma_start(hi[:], dst_d[:, GE - 1:GE].rearrange("g e -> e g")).then_inc(hi_in, 16)
                        sp.wait_ge(gidx, 1)
                        sp.dma_start(tile_d.rearrange("(c p) -> p c", p=CP), ti[:]).then_inc(tile_out, 16)
                        sp.wait_ge(tile_out, 16)
                        sp.dma_start(trow[:], tile_d.rearrange("(a u) -> a u", a=1)).then_inc(tile_in, 16)
                        sp.wait_ge(tile_in, 16)

                    @block.gpsimd
                    def _(pool):
                        nc.gpsimd.memset(padv[:, 0], 0).then_inc(pad_set, 1)
                        nc.gpsimd.memset(padv[:, 1], NP - 1).then_inc(pad_set, 1)
                        nc.gpsimd.iota(gi[:], [[1, NG]], base=0, channel_multiplier=0).then_inc(iotas, 1)
                        nc.gpsimd.iota(ui[:], [[CP, NC]], base=0, channel_multiplier=1).then_inc(iotas, 1)
                        pool.wait_ge(b1, 4)
                        nc.gpsimd.partition_broadcast(key[:], key1[:], P).then_inc(key_b, 1)
                        pool.wait_ge(gidx, 2)
                        for k, (rows, table) in enumerate(((srcRi, src_d), (dstRi, dst_d))):
                            for q in range(NC):
                                pool.indirect_dma_start(rows[:, q, :], None, table, bass.IndirectOffsetOnAxis(ap=gc[:, q:q + 1], axis=0)
                                                        ).then_inc(rows_in, 16)
                        pool.wait_ge(rows_in, 32 * NC)

                    @block.vector
                    def _(dve):
                        dve.wait_ge(hi_in, 16)
                        dve.wait_ge(iotas, 2)
                        nc.vector.tensor_scalar(hs[:], hi[:], 7, None, ALU.arith_shift_right).then_inc(b1, 1)
                        nc.vector.tensor_copy(gf[:, 1], gi[:]).then_inc(b1, 1)
                        dve.wait_ge(b1, 2)
                        nc.vector.tensor_copy(gf[:, 0], hs[:]).then_inc(b1, 1)
                        nc.vector.tensor_copy(uf[:], ui[:])
                        dve.wait_ge(b1, 3)
                        nc.vector.tensor_tensor(key1[:], gf[:, 0], gf[:, 1], ALU.add).then_inc(b1, 1)
                        dve.wait_ge(key_b, 1)
                        for q in range(NC):
                            nc.vector.tensor_scalar(lt[:, q], key[0:CP], uf[:, q:q + 1], None, ALU.is_lt).then_inc(b1, 1)
                        dve.wait_ge(b1, 4 + NC)
                        nc.vector.tensor_reduce(gu[:], lt[:], AX_X, ALU.add).then_inc(b1, 1)
                        dve.wait_ge(b1, 5 + NC)
                        nc.vector.tensor_tensor(tu[:], uf[:], gu[:], ALU.subtract).then_inc(b1, 1)
                        dve.wait_ge(b1, 6 + NC)
                        nc.vector.tensor_copy(ti[:], tu[:]).then_inc(gidx, 1)
                        nc.vector.tensor_scalar(gc[:], gu[:], float(NG - 1), None, ALU.min).then_inc(gidx, 1)
                        nc.vector.tensor_scalar(tbase[:], tu[:], float(P), None, ALU.mult).then_inc(b1, 1)
                        dve.wait_ge(b1, 7 + NC)
                        dve.wait_ge(rows_in, 32 * NC)
                        nc.vector.tensor_copy(srcR[:], srcRi[:]).then_inc(rows_f, 1)
                        nc.vector.tensor_copy(dstR[:], dstRi[:]).then_inc(rows_f, 1)
                        dve.wait_ge(rows_f, 2)
                        for q in range(NC):
                            nc.vector.tensor_scalar(dlR[:, q], dstR[:, q], tbase[:, q:q + 1], None, ALU.subtract).then_inc(rows_f, 1)
                        dve.wait_ge(rows_f, 2 + NC)

        def rows_to_edges(pairs, tag):
            with ExitStack() as c:
                pt = ps(c, "pt" + tag, [P, 2, D])
                turned, copied = sem("turned" + tag), sem("copied" + tag)
                jobs = [(rows, to, k) for rows, to in pairs for k in range(2)]
                with nc.Block() as block:
                    @block.tensor
                    def _(pe):
                        for n, (rows, to, k) in enumerate(jobs):
                            if n >= 2:
                                pe.wait_ge(copied, n - 1)
                            for q in range(NC):
                                last = nc.tensor.transpose(pt[:, n % 2, q * CP:(q + 1) * CP], rows[:, q, k * P:(k + 1) * P],
                                                           ident[0:CP, 0:CP])
                            last.then_inc(turned, 1)

                    @block.vector
                    def _(dve):
                        for n, (rows, to, k) in enumerate(jobs):
                            dve.wait_ge(turned, n + 1)
                            nc.vector.tensor_copy(to.rearrange("p (u k) -> p k u", k=2)[:, k], pt[:, n % 2, 0:U]).then_inc(copied, 1)
                        dve.wait_ge(copied, len(jobs))

        def gather_logits():
            B = 8
            ROUNDS = TU // (2 * B)
            with ExitStack() as c:
                ixs = sb(c, "ixs", [P, 2, B], I32)
                ixd = sb(c, "ixd", [P, 2, B], I32)
                gs = sb(c, "gs", [P, 2, B, H])
                gd = sb(c, "gd", [P, 2, B, 2 * H])
                passed = sem("passedC")
                index_ready, gathered, kept = sems("index_ready", 2), sems("gathered", 2), sems("kept", 2)

                def loop(eng, steps):
                    steps(0)
                    with eng.Fori(1, ROUNDS) as i:
                        steps(i)

                with nc.Block() as block:
                    @block.vector
                    def _(dve):
                        def steps(n):
                            for s in range(2):
                                reused(dve, gathered[s], n * 32 * B, n)
                                tiles = bass.ds(n * 2 * B + s * B, B)
                                nc.vector.tensor_copy(ixs[:, s], srcE[:, tiles]).then_inc(index_ready[s], 1)
                                nc.vector.tensor_copy(ixd[:, s], dstE[:, tiles]).then_inc(index_ready[s], 1)
                        loop(dve, steps)

                    @block.gpsimd
                    def _(pool):
                        def steps(n):
                            for s in range(2):
                                pool.wait_ge(index_ready[s], n * 2 + 2)
                                reused(pool, kept[s], n * 2, n)
                                pool.sem_inc(passed, 1)
                                for b in range(B):
                                    pool.indirect_dma_start(gs[:, s, b], None, as_d, bass.IndirectOffsetOnAxis(
                                        ap=ixs[:, s, b:b + 1], axis=0)).then_inc(gathered[s], 16)
                                    pool.indirect_dma_start(gd[:, s, b], None, ads_d, bass.IndirectOffsetOnAxis(
                                        ap=ixd[:, s, b:b + 1], axis=0)).then_inc(gathered[s], 16)
                        loop(pool, steps)

                    @block.scalar
                    def _(act):
                        def steps(n):
                            for s in range(2):
                                act.wait_ge(gathered[s], n * 32 * B + 32 * B)
                                tiles = bass.ds(n * 2 * B + s * B, B)
                                nc.scalar.copy(aE[:, tiles, 0:H], gs[:, s]).then_inc(kept[s], 1)
                                nc.scalar.copy(aE[:, tiles, H:3 * H], gd[:, s]).then_inc(kept[s], 1)
                        loop(act, steps)
                        for s in range(2):
                            act.wait_ge(kept[s], ROUNDS * 2)

        def edges_to_rows():
            with ExitStack() as c:
                pt = ps(c, "ptC", [CP, 2, NC, P])
                turned, copied = sem("turnedC"), sem("copiedC")
                jobs = [(j, k) for j in range(3 * H) for k in range(2)]
                columns = aE.rearrange("p (q u k) j -> p q k j u", q=NC, k=2)
                with nc.Block() as block:
                    @block.tensor
                    def _(pe):
                        for n, (j, k) in enumerate(jobs):
                            if n >= 2:
                                pe.wait_ge(copied, n - 1)
                            for q in range(NC):
                                last = nc.tensor.transpose(pt[:, n % 2, q], columns[:, q, k, j], ident[:])
                            last.then_inc(turned, 1)

                    @block.vector
                    def _(dve):
                        for n, (j, k) in enumerate(jobs):
                            dve.wait_ge(turned, n + 1)
                            nc.vector.tensor_copy(aR[:, j, :, k * P:(k + 1) * P], pt[:, n % 2]).then_inc(copied, 1)
                        dve.wait_ge(copied, len(jobs))

        def edge_softmax():
            with ExitStack() as c:
                sm = sb(c, "sm", [CP, 10, NC])
                car = sb(c, "car", [CP, 9, NC])
                rl = sb(c, "rl", [H, 2, U])
                rd = sb(c, "rd", [H, 2, U])
                cont = sb(c, "cont", [H, U + 1])
                full = sb(c, "full", [H, U])
                pen2 = sb(c, "pen2", [H, 2, U])
                penc = sb(c, "penc", [H, U + 1])
                run2 = sb(c, "run2", [H, 2, U + 1])
                carry = sb(c, "carry", [H, 2, U])
                d1, rows_out, rows_back, car_out, car_back = (sem("d1"), sem("rows_out"), sem("rows_back"),
                                                              sem("car_out"), sem("car_back"))
                small_ready, carry_ready, logits_ready, exp_ready = sem("small_ready"), sem("carry_ready"), sem("logits_ready"), sem("exp_ready")
                asv, aself, adst = aR[:, 0:H], aR[:, H:2 * H], aR[:, 2 * H:3 * H]

                with nc.Block() as block:
                    @block.vector
                    def _(dve):
                        count = [0]

                        def link(ins):
                            count[0] += 1
                            ins.then_inc(d1, 1)
                            dve.wait_ge(d1, count[0])

                        def flat(ap):
                            return ap.rearrange("p q e -> p (q e)")

                        link(nc.vector.tensor_scalar(penv, dlR[:], 0.0, None, ALU.is_ge))
                        link(nc.vector.scalar_tensor_tensor(penf, dlR[:], float(P), penv, ALU.is_lt, ALU.mult))
                        link(nc.vector.tensor_scalar(penv, penf, -1.0, BIG, ALU.add, ALU.mult))
                        for h in range(H):
                            link(nc.vector.tensor_tensor(asv[:, h], asv[:, h], penv, ALU.add))
                        link(nc.vector.memset(last1[:, :, GE - 1:GE], 1.0))
                        link(nc.vector.tensor_tensor(last1[:, :, 0:GE - 1], dstR[:, :, 1:GE], dstR[:, :, 0:GE - 1], ALU.not_equal))
                        link(nc.vector.tensor_scalar(penb, last1, -BIG, None, ALU.mult))
                        link(nc.vector.memset(penf[:, :, 0:1], -BIG))
                        link(nc.vector.tensor_copy(penf[:, :, 1:GE], penb[:, :, 0:GE - 1]))
                        for h in range(H):
                            link(nc.vector.tensor_tensor_scan(flat(fwd[:, h]), flat(penf), flat(asv[:, h]), 0.0, ALU.add, ALU.max))
                            link(nc.vector.tensor_tensor_scan(flat(bwd[:, h])[:, ::-1], flat(penb)[:, ::-1],
                                                              flat(asv[:, h])[:, ::-1], 0.0, ALU.add, ALU.max))
                        link(nc.vector.tensor_copy(sm[:, 0:H], fwd[:, :, :, GE - 1]))
                        link(nc.vector.tensor_copy(sm[:, H:2 * H], bwd[:, :, :, 0]))
                        link(nc.vector.tensor_copy(sm[:, 8], dstR[:, :, 0]))
                        nc.vector.tensor_copy(sm[:, 9], dstR[:, :, GE - 1]).then_inc(small_ready, 1)
                        dve.wait_ge(small_ready, 1)
                        for q in range(NC):
                            link(nc.vector.tensor_scalar(penf[:, q], dstR[:, q], sm[:, 8, q:q + 1], -BIG, ALU.not_equal, ALU.mult))
                            link(nc.vector.tensor_scalar(penb[:, q], dstR[:, q], sm[:, 9, q:q + 1], -BIG, ALU.not_equal, ALU.mult))
                        for h in range(H):
                            link(nc.vector.tensor_tensor(fwd[:, h], fwd[:, h], bwd[:, h], ALU.max))
                        dve.wait_ge(rows_back, 64)
                        link(nc.vector.memset(cont[:], 0.0))
                        link(nc.vector.tensor_tensor(cont[:, 1:U], rd[:, 0, 1:U], rd[:, 1, 0:U - 1], ALU.is_equal))
                        link(nc.vector.tensor_tensor(full[:], rd[:, 0], rd[:, 1], ALU.is_equal))
                        link(nc.vector.tensor_tensor(pen2[:, 0], full[:], cont[:, 0:U], ALU.mult))
                        link(nc.vector.tensor_tensor(pen2[:, 1], full[:], cont[:, 1:U + 1], ALU.mult))
                        link(nc.vector.tensor_scalar(pen2[:], pen2[:], -1.0, BIG, ALU.add, ALU.mult))
                        link(nc.vector.tensor_scalar(penc[:], cont[:], -1.0, BIG, ALU.add, ALU.mult))
                        link(nc.vector.memset(run2[:], 0.0))
                        link(nc.vector.tensor_tensor_scan(run2[:, 0, 1:U + 1], pen2[:, 0], rl[:, 0], -BIG, ALU.add, ALU.max))
                        link(nc.vector.tensor_tensor_scan(run2[:, 1, 0:U][:, ::-1], pen2[:, 1][:, ::-1], rl[:, 1][:, ::-1],
                                                          -BIG, ALU.add, ALU.max))
                        link(nc.vector.tensor_tensor(carry[:, 0], run2[:, 0, 0:U], penc[:, 0:U], ALU.add))
                        nc.vector.tensor_tensor(carry[:, 1], run2[:, 1, 1:U + 1], penc[:, 1:U + 1], ALU.add).then_inc(carry_ready, 1)
                        dve.wait_ge(car_back, 16 * (2 * NC + 1))
                        for h in range(H):
                            for q in range(NC):
                                link(nc.vector.scalar_tensor_tensor(fwd[:, h, q], penf[:, q], car[:, h, q:q + 1], fwd[:, h, q], ALU.add, ALU.max))
                                link(nc.vector.scalar_tensor_tensor(fwd[:, h, q], penb[:, q], car[:, H + h, q:q + 1], fwd[:, h, q], ALU.add, ALU.max))
                        link(nc.vector.tensor_scalar(last1[:, :, GE - 1], car[:, 8], -1.0, 1.0, ALU.mult, ALU.add))
                        for h in range(H):
                            link(nc.vector.tensor_tensor(fwd[:, h], fwd[:, h], aself[:, h], ALU.max))
                            link(nc.vector.tensor_tensor(fwd[:, h], fwd[:, h], adst[:, h], ALU.add))
                            link(nc.vector.scalar_tensor_tensor(fwd[:, h], fwd[:, h], SLOPE, fwd[:, h], ALU.mult, ALU.max))
                            for part in (asv, aself):
                                link(nc.vector.tensor_tensor(part[:, h], part[:, h], adst[:, h], ALU.add))
                                link(nc.vector.scalar_tensor_tensor(part[:, h], part[:, h], SLOPE, part[:, h], ALU.mult, ALU.max))
                                nc.vector.tensor_tensor(part[:, h], part[:, h], fwd[:, h], ALU.subtract).then_inc(logits_ready, 1)
                        for h in range(H):
                            dve.wait_ge(exp_ready, 2 * h + 2)
                            link(nc.vector.tensor_tensor(aself[:, h], aself[:, h], last1, ALU.mult))

                    @block.scalar
                    def _(act):
                        for h in range(H):
                            act.wait_ge(logits_ready, 2 * h + 2)
                            for part in (asv, aself):
                                nc.scalar.activation(part[:, h], part[:, h], ACT.Exp).then_inc(exp_ready, 1)
                        act.wait_ge(exp_ready, 2 * H)

                    @block.sync
                    def _(sp):
                        sp.wait_ge(small_ready, 1)
                        for q in range(NC):
                            sp.dma_start(row_d[:, q * CP:(q + 1) * CP].rearrange("j p -> p j"), sm[:, :, q]).then_inc(rows_out, 16)
                        sp.wait_ge(rows_out, 16 * NC)
                        sp.dma_start(rl[:, 0], row_d[0:H]).then_inc(rows_back, 16)
                        sp.dma_start(rl[:, 1], row_d[H:2 * H]).then_inc(rows_back, 16)
                        sp.dma_start(rd[:, 0], row_d[8].partition_broadcast(H)).then_inc(rows_back, 16)
                        sp.dma_start(rd[:, 1], row_d[9].partition_broadcast(H)).then_inc(rows_back, 16)
                        sp.wait_ge(carry_ready, 1)
                        for k in range(2):
                            sp.dma_start(car_d[k * H:(k + 1) * H], carry[:, k]).then_inc(car_out, 16)
                        sp.dma_start(car_d[8:9], cont[0:1, 1:U + 1]).then_inc(car_out, 16)
                        sp.wait_ge(car_out, 48)
                        for q in range(NC):
                            cols = slice(q * CP, (q + 1) * CP)
                            for k in range(2):
                                sp.dma_start(car[:, k * H:(k + 1) * H, q], car_d[k * H:(k + 1) * H, cols].rearrange("j p -> p j")).then_inc(car_back, 16)
                        sp.dma_start(car[:, 8], car_d[8].rearrange("(q p) -> p q", p=CP)).then_inc(car_back, 16)
                        sp.wait_ge(car_back, 16 * (2 * NC + 1))

        def aggregate():
            SEGS, SU = 4, 2
            ST = 2 * SU
            ROUNDS = U // (SEGS * SU)
            assert ROUNDS * SEGS * SU == U
            with ExitStack() as c:
                ix = sb(c, "ix", [P, SEGS, ST], I32)
                g = sb(c, "g", [P, SEGS, ST, H, HD])
                x9 = sb(c, "x9", [P, SEGS, ST, 9])
                dl = sb(c, "dl", [P, SEGS, ST])
                onehot = sb(c, "onehot", [P, SEGS, ST, P])
                nodei = sb(c, "nodei", [P, P], I32)
                nodef = sb(c, "nodef", [P, P])
                psO = ps(c, "psO", [P, 2, SU, D])
                psS = ps(c, "psS", [P, 2, D])
                acc_zero, node_iota, node_row = sem("acc_zero"), sem("node_iota"), sem("node_row")
                ix_in, g_in = sems("ix_in", SEGS), sems("g_in", SEGS * ST)
                weights_in, onehot_ready = sems("weights_in", SEGS), sems("onehot_ready", SEGS)
                scaled_act, scaled_dve = sems("scaled_act", SEGS), sems("scaled_dve", SEGS)
                summed, added, passed = sems("summed", SEGS), sem("added"), sem("passedE")

                def loop(eng, steps):
                    steps(0)
                    with eng.Fori(1, ROUNDS) as i:
                        steps(i)

                def tiles(n, s):
                    return bass.ds(n * (SEGS * ST) + s * ST, ST)

                with nc.Block() as block:
                    @block.sync
                    def _(sp):
                        def steps(n):
                            for s in range(SEGS):
                                for k in range(ST):
                                    reused(sp, g_in[s * ST + k], n * 16, n)
                                sp.dma_start(ix[:, s], srcE[:, tiles(n, s)]).then_inc(ix_in[s], 16)
                        loop(sp, steps)

                    @block.gpsimd
                    def _(pool):
                        nc.gpsimd.iota(nodei[:], [[1, P]], base=0, channel_multiplier=0).then_inc(node_iota, 1)

                        def steps(n):
                            for s in range(SEGS):
                                pool.wait_ge(ix_in[s], n * 16 + 16)
                                reused(pool, summed[s], n, n)
                                pool.sem_inc(passed, 1)
                                for k in range(ST):
                                    pool.indirect_dma_start(g[:, s, k].rearrange("p h o -> p (h o)"), None, xp_d,
                                                            bass.IndirectOffsetOnAxis(ap=ix[:, s, k:k + 1], axis=0)
                                                            ).then_inc(g_in[s * ST + k], 16)
                        loop(pool, steps)

                    @block.vector
                    def _(dve):
                        nc.vector.memset(acc, 0.0).then_inc(acc_zero, 1)
                        nc.vector.memset(accs[:], 0.0).then_inc(acc_zero, 1)
                        dve.wait_ge(node_iota, 1)
                        nc.vector.tensor_copy(nodef[:], nodei[:]).then_inc(node_row, 1)
                        dve.wait_ge(node_row, 1)
                        dve.wait_ge(acc_zero, 2)

                        def add(n, s, slots):
                            dve.wait_ge(summed[s], n + 1)
                            for m in range(SU):
                                order = (n * (SEGS * SU) + s * SU + m) * 2
                                if not (isinstance(n, int) and n * SEGS * SU + s * SU + m == 0):
                                    dve.wait_ge(added, order)
                                t = slots[s * SU + m]
                                nc.vector.tensor_tensor(acc[:, t], acc[:, t], psO[:, s % 2, m], ALU.add).then_inc(added, 1)
                                nc.vector.tensor_tensor(accs[:, t], accs[:, t], psS[:, s % 2, m * 9:m * 9 + 9],
                                                        ALU.add).then_inc(added, 1)

                        def slots_of(n):
                            return nc.values_load_multi_w_load_instructions(
                                trow[0:1, bass.ds(n * (SEGS * SU), SEGS * SU)], [dve.engine], min_val=0, max_val=NT - 1,
                                skip_runtime_bounds_check_because="a unit's tile is its index less its group, within 0..NT-1")[1]

                        def steps(n):
                            slots = slots_of(n)
                            for s in range(SEGS):
                                reused(dve, summed[s], n, n)
                                nc.vector.tensor_copy(x9[:, s], x9E[:, tiles(n, s)]).then_inc(weights_in[s], 1)
                                nc.vector.tensor_copy(dl[:, s], dlE[:, tiles(n, s)]).then_inc(weights_in[s], 1)
                                dve.wait_ge(weights_in[s], n * 2 + 2)
                                for k in range(ST):
                                    nc.vector.tensor_scalar(onehot[:, s, k], nodef[:], dl[:, s, k:k + 1], None,
                                                            ALU.is_equal).then_inc(onehot_ready[s], 1)
                                for k in range(ST):
                                    dve.wait_ge(g_in[s * ST + k], n * 16 + 16)
                                    for h in range(2, H):
                                        nc.vector.tensor_scalar(g[:, s, k, h], g[:, s, k, h], x9[:, s, k, h:h + 1], None,
                                                                ALU.mult).then_inc(scaled_dve[s], 1)
                                if s:
                                    add(n, s - 1, slots)
                            add(n, SEGS - 1, slots)
                        loop(dve, steps)

                    @block.scalar
                    def _(act):
                        def steps(n):
                            for s in range(SEGS):
                                act.wait_ge(weights_in[s], n * 2 + 2)
                                for k in range(ST):
                                    act.wait_ge(g_in[s * ST + k], n * 16 + 16)
                                    for h in range(2):
                                        nc.scalar.activation(g[:, s, k, h], g[:, s, k, h], ACT.Copy,
                                                             scale=x9[:, s, k, h:h + 1]).then_inc(scaled_act[s], 1)
                        loop(act, steps)

                    @block.tensor
                    def _(pe):
                        def steps(n):
                            for s in range(SEGS):
                                if not (isinstance(n, int) and n == 0 and s < 2):
                                    pe.wait_ge(added, (n * SEGS + s - 1) * (SU * 2))
                                pe.wait_ge(onehot_ready[s], (n + 1) * ST)
                                for m in range(SU):
                                    for k in range(2):
                                        kk = m * 2 + k
                                        pe.wait_ge(scaled_act[s], n * (2 * ST) + (kk + 1) * 2)
                                        pe.wait_ge(scaled_dve[s], n * (2 * ST) + (kk + 1) * 2)
                                        nc.tensor.matmul(psO[:, s % 2, m], onehot[:, s, kk], g[:, s, kk].rearrange("p h o -> p (h o)"),
                                                         start=(k == 0), stop=(k == 1))
                                        last = nc.tensor.matmul(psS[:, s % 2, m * 9:m * 9 + 9], onehot[:, s, kk], x9[:, s, kk],
                                                                start=(k == 0), stop=(k == 1))
                                last.then_inc(summed[s], 1)
                        loop(pe, steps)

        def finish_nodes():
            HALF = NT // 2
            with ExitStack() as c:
                wo = sb(c, "wo", [P, KD, D])
                woT = sb(c, "woT", [P, KD, D])
                ws1 = sb(c, "ws1", [P, KD, FF])
                ws2 = sb(c, "ws2", [P, FF // P, D])
                wr = sb(c, "wr", [P, KD, 2 * NE])
                bs1 = sb(c, "bs1", [P, FF // P])
                row = {name: sb(c, "row_" + name, [P, D]) for name in ("bias_h", "b_out", "gamma", "beta", "bs2")}
                br = sb(c, "br", [P, 2 * NE])
                eself = sb(c, "eself", [P, NT, H])
                rsum = sb(c, "rsum", [P, NT, H])
                xp = sb(c, "xpF", [P, 2, D])
                xin = sb(c, "xinF", [P, 2, D])
                hh = sb(c, "hh", [P, 2, D])
                rT = sb(c, "rT", [P, 2, D])
                y = sb(c, "y", [P, 2, D])
                xb = sb(c, "xb", [P, 2, D])
                x1 = sb(c, "x1", [P, 2, D])
                x1b = sb(c, "x1b", [P, 2, D])
                xl = sb(c, "xlF", [P, 2, D])
                x2T = sb(c, "x2T", [P, 2, D])
                hsT = sb(c, "hsT", [P, 2, FF])
                z = sb(c, "z", [P, 2, D])
                st = sb(c, "stF", [P, 2, 2, 6])
                mv = sb(c, "mvF", [P, 2, 2, 2])
                ve = sb(c, "veF", [P, 2, 2])
                rstd = sb(c, "rstdF", [P, 2, 2])
                psT = ps(c, "psTF", [P, 2, D])
                psY = ps(c, "psYF", [P, 2, D])
                psU = ps(c, "psUF", [P, 2, D])
                psD = ps(c, "psDF", [P, 2, D])
                w_in, wT_turned, wT_ready, sums_ready = sem("w_inF"), sem("wT_turned"), sem("wT_ready"), sem("sums_ready")
                x_in, x_zero, passed = sems("x_inF", 2), sem("x_zeroF"), sem("passedF")
                self_added, hh_ready, hT_turned, hT_ready = sems("self_added", 2), sems("hh_ready", 2), sems("hT_turned", 2), sems("hT_ready", 2)
                y_summed, y_ready, st_ready, mv_ready = sems("y_summed", 2), sems("y_readyF", 2), sems("st_readyF", 2), sems("mv_readyF", 2)
                ve_ready, rstd_ready, norm_steps = sems("ve_readyF", 2), sems("rstd_readyF", 2), sems("norm_steps", 2)
                xb_ready, x1_ready, x1b_ready = sems("xb_ready", 2), sems("x1_ready", 2), sems("x1b_ready", 2)
                xl_ready, xl_turned, x2T_ready = sems("xl_readyF", 2), sems("xl_turned", 2), sems("x2T_ready", 2)
                up_summed, hs_ready, down_summed = sems("up_summed", 2), sems("hs_ready", 2), sems("down_summed", 2)
                logits_ready, z_ready, xl_stored, z_stored = sems("logits_readyF", 2), sems("z_ready", 2), sems("xl_stored", 2), sems("z_stored", 2)

                def loop(eng, steps):
                    steps(0, (0, 1))
                    with eng.Fori(1, HALF) as i:
                        steps(i, (0, 1))
                    steps(HALF, (0,))

                with nc.Block() as block:
                    @block.sync
                    def _(sp):
                        sp.dma_start(wo[:], a["W_out"].rearrange("(k p) i -> p k i", p=P)).then_inc(w_in, 16)
                        sp.dma_start(ws1[:], a["Ws1"].rearrange("(k p) f -> p k f", p=P)).then_inc(w_in, 16)
                        sp.dma_start(ws2[:], a["Ws2"].rearrange("(k p) o -> p k o", p=P)).then_inc(w_in, 16)
                        sp.dma_start(bs1[:], a["bs1"].rearrange("(f p) -> p f", p=P)).then_inc(w_in, 16)
                        for b, bank in enumerate(("sp", "fq")):
                            sp.dma_start(wr[:, :, b * NE:(b + 1) * NE], a["Wr_" + bank].rearrange("(k p) e -> p k e", p=P)).then_inc(w_in, 16)
                            sp.dma_start(br[:, b * NE:(b + 1) * NE], a["br_" + bank].partition_broadcast(P)).then_inc(w_in, 16)
                        for name, to in row.items():
                            v = a[name].rearrange("h o -> (h o)") if name == "bias_h" else a[name]
                            sp.dma_start(to[:], v.partition_broadcast(P)).then_inc(w_in, 16)

                        def steps(n, slots):
                            for j in slots:
                                reused(sp, x1_ready[j], n, n)
                                tile = bass.ts(n * 2 + j, P)
                                sp.dma_start(xp[:, j], xp_d[tile, :]).then_inc(x_in[j], 16)
                                if len(slots) == 2:
                                    sp.dma_start(xin[:, j], a["x"][tile, :]).then_inc(x_in[j], 16)
                                else:
                                    sp.wait_ge(x_zero, 1)
                                    sp.dma_start(xin[0:LAST, j], a["x"][(NT - 1) * P:N, :]).then_inc(x_in[j], 16)
                        loop(sp, steps)

                    @block.gpsimd
                    def _(pool):
                        pool.wait_ge(w_in, 16 * 13)

                        def steps(n, slots):
                            for j in slots:
                                pool.wait_ge(x_in[j], n * 32 + 32)
                                reused(pool, x1_ready[j], n, n)
                                nc.gpsimd.tensor_tensor(xb[:, j], xin[:, j], row["beta"][:], ALU.add).then_inc(xb_ready[j], 1)
                            for j in slots:
                                pool.wait_ge(ve_ready[j], n * 2 + 1)
                                nc.gpsimd.tensor_tensor(rstd[:, j, 0:1], ve[:, j, 0:1], halfneg[:], ALU.pow).then_inc(rstd_ready[j], 1)
                            for j in slots:
                                pool.wait_ge(ve_ready[j], n * 2 + 2)
                                nc.gpsimd.tensor_tensor(rstd[:, j, 1:2], ve[:, j, 1:2], halfneg[:], ALU.pow).then_inc(rstd_ready[j], 1)
                            for j in slots:
                                pool.wait_ge(x1_ready[j], n + 1)
                                reused(pool, z_ready[j], n, n)
                                nc.gpsimd.tensor_tensor(x1b[:, j], x1[:, j], row["bs2"][:], ALU.add).then_inc(x1b_ready[j], 1)
                        loop(pool, steps)

                    @block.vector
                    def _(dve):
                        dve.wait_ge(w_in, 16 * 13)
                        for k in range(KD):
                            dve.wait_ge(wT_turned, k + 1)
                            nc.vector.tensor_copy(woT[:, k], psT[:, k % 2]).then_inc(wT_ready, 1)
                        nc.vector.tensor_scalar(rsum[:], accs[:, :, 8:9].to_broadcast([P, NT, H]), -1.0, 1.0, ALU.mult, ALU.add).then_inc(sums_ready, 1)
                        dve.wait_ge(sums_ready, 1)
                        nc.vector.tensor_tensor(eself[:], accs[:, :, H:2 * H], rsum[:], ALU.add).then_inc(sums_ready, 1)
                        dve.wait_ge(sums_ready, 2)
                        nc.vector.scalar_tensor_tensor(rsum[:], accs[:, :, 0:H], 1e-16, eself[:], ALU.add, ALU.add).then_inc(sums_ready, 1)
                        dve.wait_ge(sums_ready, 3)
                        nc.vector.reciprocal(rsum[:], rsum[:]).then_inc(sums_ready, 1)
                        dve.wait_ge(sums_ready, 4)

                        def steps(n, slots):
                            if len(slots) == 1:
                                dve.wait_ge(xb_ready[0], n)
                                nc.vector.memset(xin[:, 0], 0.0).then_inc(x_zero, 1)
                            for j in slots:
                                t = n * 2 + j
                                dve.wait_ge(x_in[j], n * 32 + 32)
                                reused(dve, hT_turned[j], n, n)
                                for h in range(H):
                                    cols = slice(h * HD, (h + 1) * HD)
                                    nc.vector.tensor_scalar(hh[:, j, cols], xp[:, j, cols], eself[:, bass.ds(t, 1), h], None,
                                                            ALU.mult).then_inc(self_added[j], 1)
                                dve.wait_ge(self_added[j], n * 9 + 4)
                                nc.vector.tensor_tensor(hh[:, j], hh[:, j], acc[:, bass.ds(t, 1)].rearrange("p a d -> p (a d)"),
                                                        ALU.add).then_inc(self_added[j], 1)
                                dve.wait_ge(self_added[j], n * 9 + 5)
                                for h in range(H):
                                    cols = slice(h * HD, (h + 1) * HD)
                                    nc.vector.tensor_scalar(hh[:, j, cols], hh[:, j, cols], rsum[:, bass.ds(t, 1), h], None,
                                                            ALU.mult).then_inc(self_added[j], 1)
                                dve.wait_ge(self_added[j], n * 9 + 9)
                                nc.vector.tensor_tensor(hh[:, j], hh[:, j], row["bias_h"][:], ALU.add).then_inc(hh_ready[j], 1)

                            def stats(v, which, j):
                                nc.vector.bn_stats(st[:, j, which], v).then_inc(st_ready[j], 1)
                                dve.wait_ge(st_ready[j], n * 2 + which + 1)
                                dve.sem_inc(passed, 1)
                                nc.vector.bn_aggr(mv[:, j, which], st[:, j, which]).then_inc(mv_ready[j], 1)
                                dve.wait_ge(mv_ready[j], n * 2 + which + 1)
                                nc.vector.tensor_scalar_add(ve[:, j, which:which + 1], mv[:, j, which, 1:2], EPS).then_inc(ve_ready[j], 1)

                            for j in slots:
                                dve.wait_ge(y_summed[j], n + 1)
                                nc.vector.tensor_tensor(y[:, j], psY[:, j], row["b_out"][:], ALU.add).then_inc(y_ready[j], 1)
                                dve.wait_ge(y_ready[j], n + 1)
                                dve.sem_inc(passed, 1)
                                stats(y[:, j], 0, j)
                            for j in slots:
                                dve.wait_ge(rstd_ready[j], n * 2 + 1)
                                nc.vector.tensor_scalar(y[:, j], y[:, j], mv[:, j, 0, 0:1], rstd[:, j, 0:1],
                                                        ALU.subtract, ALU.mult).then_inc(norm_steps[j], 1)
                                dve.wait_ge(norm_steps[j], n * 2 + 1)
                                nc.vector.tensor_tensor(y[:, j], y[:, j], row["gamma"][:], ALU.mult).then_inc(norm_steps[j], 1)
                                dve.wait_ge(norm_steps[j], n * 2 + 2)
                                dve.wait_ge(xb_ready[j], n + 1)
                                reused(dve, x1b_ready[j], n, n)
                                nc.vector.tensor_tensor(x1[:, j], y[:, j], xb[:, j], ALU.add).then_inc(x1_ready[j], 1)
                                dve.wait_ge(x1_ready[j], n + 1)
                                dve.sem_inc(passed, 1)
                                stats(x1[:, j], 1, j)
                            for j in slots:
                                dve.wait_ge(rstd_ready[j], n * 2 + 2)
                                reused(dve, xl_stored[j], n * 16, n)
                                reused(dve, xl_turned[j], n, n)
                                nc.vector.tensor_scalar(xl[:, j], x1[:, j], mv[:, j, 1, 0:1], rstd[:, j, 1:2],
                                                        ALU.subtract, ALU.mult).then_inc(xl_ready[j], 1)
                            for j in slots:
                                dve.wait_ge(up_summed[j], n + 1)
                                nc.vector.tensor_tensor(lg[:, bass.ds(n * 2 + j, 1)].rearrange("p a e -> p (a e)"), psY[:, j, 0:2 * NE], br[:],
                                                        ALU.add).then_inc(logits_ready[j], 1)
                            for j in slots:
                                dve.wait_ge(down_summed[j], n + 1)
                                dve.wait_ge(x1b_ready[j], n + 1)
                                reused(dve, z_stored[j], n * 16, n)
                                nc.vector.tensor_tensor(z[:, j], psD[:, j], x1b[:, j], ALU.add).then_inc(z_ready[j], 1)
                        loop(dve, steps)

                    @block.tensor
                    def _(pe):
                        pe.wait_ge(w_in, 16 * 13)
                        for k in range(KD):
                            if k >= 2:
                                pe.wait_ge(wT_ready, k - 1)
                            for o in range(KD):
                                last = nc.tensor.transpose(psT[:, k % 2, o * P:(o + 1) * P], wo[:, o, k * P:(k + 1) * P], ident[:])
                            last.then_inc(wT_turned, 1)
                        pe.wait_ge(wT_ready, KD)

                        def turn(to, rows):
                            for k in range(KD):
                                last = nc.tensor.transpose(to[:, k * P:(k + 1) * P], rows[:, k * P:(k + 1) * P], ident[:])
                            return last

                        def steps(n, slots):
                            for j in slots:
                                pe.wait_ge(hh_ready[j], n + 1)
                                reused(pe, x2T_ready[j], n, n)
                                turn(psT[:, j], hh[:, j]).then_inc(hT_turned[j], 1)
                            for j in slots:
                                pe.wait_ge(hT_ready[j], n + 1)
                                reused(pe, logits_ready[j], n, n)
                                for k in range(KD):
                                    last = nc.tensor.matmul(psY[:, j], rT[:, j, k * P:(k + 1) * P], woT[:, k], start=(k == 0), stop=(k == KD - 1))
                                last.then_inc(y_summed[j], 1)
                            for j in slots:
                                pe.wait_ge(xl_ready[j], n + 1)
                                turn(psT[:, j], xl[:, j]).then_inc(xl_turned[j], 1)
                            for j in slots:
                                pe.wait_ge(x2T_ready[j], n + 1)
                                pe.wait_ge(y_ready[j], n + 1)
                                reused(pe, hs_ready[j], n * 2, n)
                                for k in range(KD):
                                    nc.tensor.matmul(psY[:, j, 0:2 * NE], x2T[:, j, k * P:(k + 1) * P], wr[:, k], start=(k == 0), stop=(k == KD - 1))
                                for f in range(FF // P):
                                    for k in range(KD):
                                        last = nc.tensor.matmul(psU[:, j, f * P:(f + 1) * P], ws1[:, k, f * P:(f + 1) * P],
                                                                x2T[:, j, k * P:(k + 1) * P], start=(k == 0), stop=(k == KD - 1))
                                last.then_inc(up_summed[j], 1)
                            for j in slots:
                                pe.wait_ge(hs_ready[j], n * 2 + 2)
                                reused(pe, z_ready[j], n, n)
                                for f in range(FF // P):
                                    last = nc.tensor.matmul(psD[:, j], hsT[:, j, f * P:(f + 1) * P], ws2[:, f], start=(f == 0), stop=(f == FF // P - 1))
                                last.then_inc(down_summed[j], 1)
                        loop(pe, steps)

                    @block.scalar
                    def _(act):
                        act.wait_ge(w_in, 16 * 13)

                        def steps(n, slots):
                            for j in slots:
                                act.wait_ge(hT_turned[j], n + 1)
                                reused(act, y_summed[j], n, n)
                                nc.scalar.copy(rT[:, j], psT[:, j]).then_inc(hT_ready[j], 1)
                            for j in slots:
                                act.wait_ge(xl_turned[j], n + 1)
                                reused(act, up_summed[j], n, n)
                                nc.scalar.copy(x2T[:, j], psT[:, j]).then_inc(x2T_ready[j], 1)
                                act.wait_ge(xl_ready[j], n + 1)
                                act.dma_start(xl_d[bass.ts(n * 2 + j, P), :], xl[:, j]).then_inc(xl_stored[j], 16)
                            for j in slots:
                                act.wait_ge(up_summed[j], n + 1)
                                reused(act, down_summed[j], n, n)
                                for f in range(FF // P):
                                    cols = slice(f * P, (f + 1) * P)
                                    nc.scalar.activation(hsT[:, j, cols], psU[:, j, cols], ACT.Gelu, bias=bs1[:, f:f + 1]).then_inc(hs_ready[j], 1)
                            for j in slots:
                                act.wait_ge(z_ready[j], n + 1)
                                act.dma_start(z_d[bass.ts(n * 2 + j, P), :], z[:, j]).then_inc(z_stored[j], 16)
                        loop(act, steps)
                        for done in (xl_stored, z_stored):
                            act.wait_ge(done[0], 16 * (HALF + 1))
                            act.wait_ge(done[1], 16 * HALF)

        def route():
            B2 = 2 * NE
            with ExitStack() as c:
                iota8 = sb(c, "iota8", [P, B2], I32)
                iota8f = sb(c, "iota8f", [P, B2])
                prow = sb(c, "prow", [P, 1], I32)
                real = sb(c, "real", [P, 1])
                far = sb(c, "far", [P, 1])
                toki = sb(c, "toki", [P, NT], I32)
                jrow = sb(c, "jrow", [1, ET], I32)
                jrowf = sb(c, "jrowf", [1, ET])
                triu = sb(c, "triu", [P, P])
                ones = sb(c, "ones", [P, P])
                mx = sb(c, "mx", [P, 2 * NT])
                ex = sb(c, "ex", [P, NT, B2])
                oh = sb(c, "oh", [P, NT, B2])
                cum = sb(c, "cum", [P, NT, B2])
                tot = sb(c, "tot", [P, NT, B2])
                pre = sb(c, "pre", [P, NT, B2])
                cnt = sb(c, "cnt", [P, B2], I32)
                nt = sb(c, "nt", [P, B2])
                nti = sb(c, "nti", [P, B2], I32)
                ends = sb(c, "ends", [P, 2, NE])
                base = sb(c, "base", [P, B2])
                slotf = sb(c, "slotf", [P, 2 * NT])
                posf = sb(c, "posf", [P, 2 * NT])
                sci = sb(c, "sci", [P, 2 * NT], I32)
                ecmp = sb(c, "ecmp", [1, 2, ET, NE])
                ef = sb(c, "ef", [1, 2, ET])
                fill = sb(c, "fill", [P, 2 * ET], I32)
                psC = ps(c, "psC", [P, 2, D])
                psN = ps(c, "psN", [P, 2, D])
                SB = 7
                idx = sb(c, "idx", [P, SB, 2], I32)
                tok = sb(c, "tok", [P, SB], I32)
                g1, gz, g2, g3, g4, filled = sem("g1"), sem("gz"), sem("g2"), sem("g3"), sem("g4"), sem("filled")
                e_ready, e_done, staged, scattered, perm_in, passed = (sem("e_ready"), sem("e_done"), sem("staged"), sem("scattered"),
                                                                       sem("perm_in"), sem("passedG"))
                banks = "p t (b e) -> p (t b) e"
                halves = (slice(0, NT // 2), slice(NT // 2, NT))

                with nc.Block() as block:
                    @block.gpsimd
                    def _(pool):
                        nc.gpsimd.iota(iota8[:], [[0, 2], [1, NE]], base=0, channel_multiplier=0).then_inc(gz, 1)
                        nc.gpsimd.iota(prow[:], [[0, 1]], base=0, channel_multiplier=1).then_inc(gz, 1)
                        nc.gpsimd.iota(toki[:], [[P, NT]], base=0, channel_multiplier=1).then_inc(gz, 1)
                        nc.gpsimd.iota(jrow[:], [[1, ET]], base=0, channel_multiplier=0).then_inc(gz, 1)
                        nc.gpsimd.memset(ones[:], 1.0).then_inc(gz, 1)
                        nc.gpsimd.memset(fill[:], NP - 1).then_inc(gz, 1)
                        nc.gpsimd.memset(triu[:], 1.0).then_inc(gz, 1)
                        pool.wait_ge(gz, 7)
                        nc.gpsimd.affine_select(out=triu[:], in_=triu[:], compare_op=ALU.is_ge, fill=0.0,
                                                base=0, pattern=[[1, P]], channel_multiplier=-1).then_inc(gz, 1)
                        pool.wait_ge(filled, 16)

                        def steps(n):
                            pool.wait_ge(staged, n * 2 + 2)
                            pool.sem_inc(passed, 1)
                            for k in range(SB):
                                for b in range(2):
                                    pool.indirect_dma_start(perm_d, bass.IndirectOffsetOnAxis(ap=idx[:, k, b:b + 1], axis=0),
                                                            tok[:, k:k + 1], None, bounds_check=2 * ET * P - 1,
                                                            oob_is_err=False).then_inc(scattered, 16)
                        steps(0)
                        with pool.Fori(1, NT // SB) as i:
                            steps(i)
                        pool.wait_ge(scattered, NT * 32)

                    @block.sync
                    def _(sp):
                        sp.wait_ge(gz, 8)
                        sp.dma_start(perm_d.rearrange("(p j) a -> p (j a)", p=P), fill[:]).then_inc(filled, 16)
                        for b, bank in enumerate(("sp", "fq")):
                            for e in range(NE):
                                sp.dma_start(w1[:, b * NE + e], a["W1_" + bank][e].rearrange("(k p) f -> p k f", p=P)).then_inc(banks_in, 16)
                                sp.dma_start(w2[:, b * NE + e], a["W2_" + bank][e].rearrange("(k p) o -> p k o", p=P)).then_inc(banks_in, 16)
                            sp.dma_start(b1[:, b * NE:(b + 1) * NE], a["b1_" + bank].partition_broadcast(P)).then_inc(banks_in, 16)
                            sp.dma_start(b2[:, b * NE:(b + 1) * NE], a["b2_" + bank].partition_broadcast(P)).then_inc(banks_in, 16)
                        sp.wait_ge(scattered, NT * 32)
                        sp.dma_start(perm[:], perm_d.rearrange("(j p) a -> p (j a)", p=P)).then_inc(perm_in, 16)
                        sp.wait_ge(perm_in, 16)

                    @block.scalar
                    def _(act):
                        act.wait_ge(e_ready, 1)
                        nc.scalar.activation(ex[:], ex[:], ACT.Exp).then_inc(e_done, 1)

                    @block.tensor
                    def _(pe):
                        pe.wait_ge(gz, 8)
                        pe.wait_ge(g2, 1)
                        for m, w in enumerate(halves):
                            cols = (w.stop - w.start) * B2
                            nc.tensor.matmul(psC[:, m, 0:cols], triu[:], oh[:, w].rearrange("p t e -> p (t e)"), start=True, stop=True)
                            nc.tensor.matmul(psN[:, m, 0:cols], ones[:], oh[:, w].rearrange("p t e -> p (t e)"), start=True, stop=True).then_inc(g3, 1)

                    @block.vector
                    def _(dve):
                        count = [0]

                        def link(ins):
                            count[0] += 1
                            ins.then_inc(g1, 1)
                            dve.wait_ge(g1, count[0])

                        dve.wait_ge(gz, 8)
                        link(nc.vector.tensor_copy(iota8f[:], iota8[:]))
                        link(nc.vector.tensor_copy(far[:], prow[:]))
                        link(nc.vector.tensor_scalar(real[:], far[:], float(LAST), None, ALU.is_lt))
                        link(nc.vector.tensor_scalar(far[:], real[:], -30000.0, 30000.0, ALU.mult, ALU.add))
                        lgb, exb, ohb = lg[:].rearrange(banks, b=2), ex[:].rearrange(banks, b=2), oh[:].rearrange(banks, b=2)
                        link(nc.vector.tensor_reduce(mx[:], lgb, AX_X, ALU.max))
                        link(nc.vector.tensor_tensor(ohb, lgb, mx[:].unsqueeze(2).to_broadcast([P, 2 * NT, NE]), ALU.subtract))
                        link(nc.vector.tensor_copy(ex[:], oh[:]))
                        nc.vector.memset(slotf[:], 0.0).then_inc(e_ready, 1)
                        link(nc.vector.tensor_scalar(oh[:], oh[:], 0.0, -float(NE), ALU.is_equal, ALU.mult))
                        link(nc.vector.tensor_tensor(oh[:], oh[:], iota8f[:].unsqueeze(1).to_broadcast([P, NT, B2]), ALU.add))
                        link(nc.vector.tensor_reduce(mx[:], ohb, AX_X, ALU.min))
                        link(nc.vector.tensor_tensor(ohb, ohb, mx[:].unsqueeze(2).to_broadcast([P, 2 * NT, NE]), ALU.is_equal))
                        nc.vector.tensor_scalar(oh[:, NT - 1], oh[:, NT - 1], real[:, 0:1], None, ALU.mult).then_inc(g2, 1)
                        dve.wait_ge(e_done, 1)
                        link(nc.vector.tensor_reduce(gate[:], exb, AX_X, ALU.add))
                        link(nc.vector.reciprocal(gate[:], gate[:]))
                        dve.wait_ge(g3, 2)
                        for m, w in enumerate(halves):
                            cols = (w.stop - w.start) * B2
                            link(nc.vector.tensor_copy(cum[:, w].rearrange("p t e -> p (t e)"), psC[:, m, 0:cols]))
                            link(nc.vector.tensor_copy(tot[:, w].rearrange("p t e -> p (t e)"), psN[:, m, 0:cols]))
                        for k in range(B2):
                            link(nc.vector.tensor_tensor_scan(pre[:, :, k], ones[:, 0:NT], tot[:, :, k], 0.0, ALU.mult, ALU.add))
                        link(nc.vector.tensor_scalar(nt[:], pre[:, NT - 1], float(P - 1), None, ALU.add))
                        link(nc.vector.tensor_tensor(cum[:], cum[:], pre[:], ALU.add))
                        link(nc.vector.scalar_tensor_tensor(cum[:], cum[:], -1.0, tot[:], ALU.add, ALU.subtract))
                        link(nc.vector.tensor_copy(cnt[:], nt[:]))
                        link(nc.vector.tensor_scalar(nti[:], cnt[:], 7, None, ALU.arith_shift_right))
                        link(nc.vector.tensor_copy(nt[:], nti[:]))
                        for b in range(2):
                            link(nc.vector.tensor_tensor_scan(ends[:, b], ones[:, 0:NE], nt[:, b * NE:(b + 1) * NE], 0.0, ALU.mult, ALU.add))
                            link(nc.vector.tensor_tensor(base[:, b * NE:(b + 1) * NE], ends[:, b], nt[:, b * NE:(b + 1) * NE], ALU.subtract))
                            link(nc.vector.tensor_scalar(base[:, b * NE:(b + 1) * NE], base[:, b * NE:(b + 1) * NE], float(P), float(b * ET * P),
                                                         ALU.mult, ALU.add))
                        cumb = cum[:].rearrange(banks, b=2)
                        link(nc.vector.tensor_tensor(tot[:], cum[:], oh[:], ALU.mult))
                        link(nc.vector.tensor_reduce(posf[:], tot[:].rearrange(banks, b=2), AX_X, ALU.add))
                        link(nc.vector.tensor_tensor(cum[:], cum[:], base[:].unsqueeze(1).to_broadcast([P, NT, B2]), ALU.add))
                        link(nc.vector.tensor_tensor(cum[:], cum[:], oh[:], ALU.mult))
                        link(nc.vector.tensor_reduce(slotf[:], cumb, AX_X, ALU.add))
                        link(nc.vector.tensor_copy(slot[:].rearrange("p t b -> p (t b)"), slotf[:]))
                        link(nc.vector.tensor_scalar(slotf[:, 2 * NT - 2:2 * NT], slotf[:, 2 * NT - 2:2 * NT], far[:, 0:1], None, ALU.add))
                        link(nc.vector.tensor_copy(sci[:], slotf[:]))
                        link(nc.vector.scalar_tensor_tensor(gate[:], posf[:], float(CAP), gate[:], ALU.is_lt, ALU.mult))
                        link(nc.vector.tensor_copy(jrowf[:], jrow[:]))
                        for b in range(2):
                            link(nc.vector.tensor_tensor(ecmp[:, b], ends[0:1, b].unsqueeze(1).to_broadcast([1, ET, NE]),
                                                         jrowf[:].unsqueeze(2).to_broadcast([1, ET, NE]), ALU.is_le))
                            link(nc.vector.tensor_reduce(ef[:, b], ecmp[:, b], AX_X, ALU.add))
                            link(nc.vector.tensor_scalar(ef[:, b], ef[:, b], float(NE - 1), float(b * NE), ALU.min, ALU.add))
                        link(nc.vector.tensor_copy(erow[:], ef[:].rearrange("a b j -> a (b j)")))

                        def steps(n):
                            reused(dve, scattered, n * (SB * 32), n)
                            nc.vector.tensor_copy(idx[:].rearrange("p k b -> p (k b)"), sci[:, bass.ds(n * (2 * SB), 2 * SB)]).then_inc(staged, 1)
                            nc.vector.tensor_copy(tok[:], toki[:, bass.ds(n * SB, SB)]).then_inc(staged, 1)
                        steps(0)
                        with dve.Fori(1, NT // SB) as i:
                            steps(i)

        def experts():
            S = 4
            ROUNDS = 2 * ET // S
            with ExitStack() as c:
                ix = sb(c, "ixH", [P, S], I32)
                xr = sb(c, "xr", [P, S, D])
                xT = sb(c, "xTH", [P, 2, D])
                hp = sb(c, "hp", [P, 2, FF])
                hr = sb(c, "hr", [P, 2, FF])
                hT = sb(c, "hT", [P, 2, FF])
                y = sb(c, "yH", [P, 2, D])
                psT = ps(c, "psTH", [P, 2, D])
                psU = ps(c, "psUH", [P, 2, D])
                psH = ps(c, "psHH", [P, 2, D])
                psD = ps(c, "psDH", [P, 2, D])
                ix_ready, x_in, x_turned, xT_ready = sems("ix_readyH", S), sems("x_inH", S), sems("x_turnedH", S), sems("xT_readyH", S)
                up_summed, h_biased, h_ready, h_turned = sems("up_summedH", S), sems("h_biased", S), sems("h_readyH", S), sems("h_turned", S)
                hT_ready, down_summed, y_ready, y_stored = sems("hT_readyH", S), sems("down_summedH", S), sems("y_readyH", S), sems("y_storedH", S)
                passed = sem("passedH")

                def loop(eng, steps):
                    steps(0)
                    with eng.Fori(1, ROUNDS) as i:
                        steps(i)

                def before(eng, semaphores, n, s, back=2, each=1):
                    if s >= back:
                        eng.wait_ge(semaphores[s - back], (n + 1) * each)
                    elif not isinstance(n, int) or n:
                        eng.wait_ge(semaphores[s - back + S], n * each)

                def expert_of(eng, n):
                    return nc.values_load_multi_w_load_instructions(
                        erow[0:1, bass.ds(n * S, S)], [eng.engine], min_val=0, max_val=2 * NE - 1,
                        skip_runtime_bounds_check_because="a count of ends, held to the bank's experts")[1]

                with nc.Block() as block:
                    @block.gpsimd
                    def _(pool):
                        def steps(n):
                            for s in range(S):
                                pool.wait_ge(ix_ready[s], n + 1)
                                reused(pool, x_turned[s], n, n)
                                pool.sem_inc(passed, 1)
                                pool.indirect_dma_start(xr[:, s], None, xl_d, bass.IndirectOffsetOnAxis(ap=ix[:, s:s + 1], axis=0)
                                                        ).then_inc(x_in[s], 16)
                        loop(pool, steps)

                    @block.tensor
                    def _(pe):
                        pe.wait_ge(banks_in, 16 * BANK_LOADS)

                        def turn_x(n, s):
                            pe.wait_ge(x_in[s], n * 16 + 16)
                            before(pe, xT_ready, n, s)
                            for k in range(KD):
                                last = nc.tensor.transpose(psT[:, s % 2, k * P:(k + 1) * P], xr[:, s, k * P:(k + 1) * P], ident[:])
                            last.then_inc(x_turned[s], 1)

                        def up(n, s, e):
                            pe.wait_ge(xT_ready[s], n + 1)
                            before(pe, h_biased, n, s)
                            for k in range(KD):
                                last = nc.tensor.matmul(psU[:, s % 2, 0:FF], xT[:, s % 2, k * P:(k + 1) * P], w1[:, e, k],
                                                        start=(k == 0), stop=(k == KD - 1))
                            last.then_inc(up_summed[s], 1)

                        def down(n, s, e):
                            pe.wait_ge(h_ready[s], n + 1)
                            before(pe, hT_ready, n, s)
                            for f in range(FF // P):
                                last = nc.tensor.transpose(psH[:, s % 2, f * P:(f + 1) * P], hr[:, s % 2, f * P:(f + 1) * P], ident[:])
                            last.then_inc(h_turned[s], 1)

                        def down2(n, s, e):
                            pe.wait_ge(hT_ready[s], n + 1)
                            before(pe, y_ready, n, s)
                            for f in range(FF // P):
                                last = nc.tensor.matmul(psD[:, s % 2], hT[:, s % 2, f * P:(f + 1) * P], w2[:, e, f],
                                                        start=(f == 0), stop=(f == FF // P - 1))
                            last.then_inc(down_summed[s], 1)

                        def steps(n):
                            e = expert_of(pe, n)
                            for s0 in range(0, S, 2):
                                for part in (turn_x, up, down, down2):
                                    for s in (s0, s0 + 1):
                                        part(n, s, e[s]) if part is not turn_x else part(n, s)
                        loop(pe, steps)

                    @block.scalar
                    def _(act):
                        def steps(n):
                            for s0 in range(0, S, 2):
                                for s in (s0, s0 + 1):
                                    act.wait_ge(x_turned[s], n + 1)
                                    before(act, up_summed, n, s)
                                    nc.scalar.copy(xT[:, s % 2], psT[:, s % 2]).then_inc(xT_ready[s], 1)
                                for s in (s0, s0 + 1):
                                    act.wait_ge(h_biased[s], n + 1)
                                    before(act, h_turned, n, s)
                                    nc.scalar.activation(hr[:, s % 2], hp[:, s % 2], ACT.Gelu).then_inc(h_ready[s], 1)
                                for s in (s0, s0 + 1):
                                    act.wait_ge(y_ready[s], n + 1)
                                    act.dma_start(y_d[bass.ts(n * S + s, P), :], y[:, s % 2]).then_inc(y_stored[s], 16)
                        loop(act, steps)
                        for s in range(S):
                            act.wait_ge(y_stored[s], 16 * ROUNDS)

                    @block.vector
                    def _(dve):
                        dve.wait_ge(banks_in, 16 * BANK_LOADS)

                        def steps(n):
                            for s in range(S):
                                reused(dve, x_in[s], n * 16, n)
                                nc.vector.tensor_copy(ix[:, s:s + 1], perm[:, bass.ds(n * S + s, 1)]).then_inc(ix_ready[s], 1)
                            e = expert_of(dve, n)
                            for s0 in range(0, S, 2):
                                for s in (s0, s0 + 1):
                                    dve.wait_ge(up_summed[s], n + 1)
                                    before(dve, h_ready, n, s)
                                    nc.vector.tensor_tensor(hp[:, s % 2], psU[:, s % 2, 0:FF], b1[:, e[s]], ALU.add).then_inc(h_biased[s], 1)
                                for s in (s0, s0 + 1):
                                    dve.wait_ge(h_turned[s], n + 1)
                                    before(dve, down_summed, n, s)
                                    nc.vector.tensor_copy(hT[:, s % 2], psH[:, s % 2, 0:FF]).then_inc(hT_ready[s], 1)
                                for s in (s0, s0 + 1):
                                    dve.wait_ge(down_summed[s], n + 1)
                                    before(dve, y_stored, n, s, each=16)
                                    nc.vector.tensor_tensor(y[:, s % 2], psD[:, s % 2], b2[:, e[s]], ALU.add).then_inc(y_ready[s], 1)
                        loop(dve, steps)

        def combine():
            S = 6
            ROUNDS = NT // S
            assert ROUNDS * S == NT - 1
            with ExitStack() as c:
                ix = sb(c, "ixI", [P, S, 2], I32)
                yb = sb(c, "yb", [P, S, 2, D])
                z = sb(c, "zI", [P, S, D])
                ix_ready, y_in, z_in = sems("ix_readyI", S), sems("y_inI", S), sems("z_inI", S)
                part, o_ready, stored, passed = sems("partI", S), sems("o_ready", S), sems("storedI", S), sem("passedI")

                def loop(eng, steps):
                    steps(0, range(S))
                    with eng.Fori(1, ROUNDS) as i:
                        steps(i, range(S))
                    steps(ROUNDS, range(1))

                with nc.Block() as block:
                    @block.sync
                    def _(sp):
                        def steps(n, slots):
                            for s in slots:
                                reused(sp, stored[s], n * 16, n)
                                sp.dma_start(z[:, s], z_d[bass.ts(n * S + s, P), :]).then_inc(z_in[s], 16)
                        loop(sp, steps)

                    @block.gpsimd
                    def _(pool):
                        def steps(n, slots):
                            for s in slots:
                                pool.wait_ge(ix_ready[s], n + 1)
                                reused(pool, o_ready[s], n, n)
                                pool.sem_inc(passed, 1)
                                for b in range(2):
                                    pool.indirect_dma_start(yb[:, s, b], None, y_d, bass.IndirectOffsetOnAxis(ap=ix[:, s, b:b + 1], axis=0)
                                                            ).then_inc(y_in[s], 16)
                        loop(pool, steps)

                    @block.vector
                    def _(dve):
                        def steps(n, slots):
                            for s in slots:
                                reused(dve, y_in[s], n * 32, n)
                                nc.vector.tensor_copy(ix[:, s:s + 1], slot[:, bass.ds(n * S + s, 1)]).then_inc(ix_ready[s], 1)
                            for s in slots:
                                dve.wait_ge(z_in[s], n * 16 + 16)
                                dve.wait_ge(y_in[s], n * 32 + 32)
                                for b in range(2):
                                    g = gate[:, bass.ds((n * S + s) * 2 + b, 1)]
                                    ins = nc.vector.scalar_tensor_tensor(z[:, s], yb[:, s, b], g, z[:, s], ALU.mult, ALU.add)
                                    if b == 0:
                                        ins.then_inc(part[s], 1)
                                        dve.wait_ge(part[s], n + 1)
                                ins.then_inc(o_ready[s], 1)
                        loop(dve, steps)

                    @block.scalar
                    def _(act):
                        def steps(n, slots):
                            for s in slots:
                                act.wait_ge(o_ready[s], n + 1)
                                if len(slots) > 1:
                                    act.dma_start(out[bass.ts(n * S + s, P), :], z[:, s]).then_inc(stored[s], 16)
                                else:
                                    act.dma_start(out[(NT - 1) * P:N, :], z[0:LAST, s]).then_inc(stored[s], 16)
                        loop(act, steps)
                        for s in range(S):
                            act.wait_ge(stored[s], 16 * (ROUNDS + (s == 0)))

        phase(constants)
        phase(project_nodes)
        if phases >= 2:
            with ExitStack() as soft:
                srcR = sb(soft, "srcR", [CP, NC, GE])
                dstR = sb(soft, "dstR", [CP, NC, GE])
                dlR = sb(soft, "dlR", [CP, NC, GE])
                tbase = sb(soft, "tbase", [CP, NC])
                dstE = sb(soft, "dstE", [P, TU], I32)
                with ExitStack() as raw:
                    srcRi = sb(raw, "srcRi", [CP, NC, GE], I32)
                    dstRi = sb(raw, "dstRi", [CP, NC, GE], I32)
                    phase(plan_units)
                phase(rows_to_edges, ((srcR, srcE[:]), (dstR, dstE[:]), (dlR, dlE[:])), "B")
                aR, rest = acc[0:CP, 0:3 * H * NC * GE], acc[0:CP, 3 * H * NC * GE:]
                aR = aR.rearrange("p (j q e) -> p j q e", j=3 * H, q=NC)
                aE = acc[:, 3 * H * NC * GE:3 * H * NC * GE + TU * 3 * H].rearrange("p (t j) -> p t j", t=TU)
                phase(gather_logits)
                phase(edges_to_rows)
                parts = rest[:, 0:12 * NC * GE].rearrange("p (j q e) -> p j q e", j=12, q=NC)
                fwd, bwd, penv, last1, penf, penb = parts[:, 0:H], parts[:, H:2 * H], parts[:, 8], parts[:, 9], parts[:, 10], parts[:, 11]
                phase(edge_softmax)
                phase(rows_to_edges, [(aR[:, h], x9E[:, :, h]) for h in range(2 * H)] + [(last1, x9E[:, :, 8])], "D")
                if scratch != "Internal" and phases == 2:
                    x9_d = dram("x9_d", [P, TU, 9])
                    with nc.Block() as block:
                        @block.sync
                        def _(sp):
                            x9o = sem("x9o")
                            sp.dma_start(x9_d, x9E[:]).then_inc(x9o, 16)
                            sp.wait_ge(x9o, 16)
        if phases >= 3:
            xl_d = dram("xl_d", [NP, D])
            z_d = dram("z_d", [NP, D])
            y_d = dram("y_d", [2 * ET * P, D])
            perm_d = dram("perm_d", [2 * ET * P, 1], I32)
            with sums:
                with edges:
                    acc = acc[:].rearrange("p (t d) -> p t d", d=D)
                    phase(aggregate)
                if scratch != "Internal" and phases == 3:
                    acc_d, accs_d = dram("acc_d", [P, NT, D]), dram("accs_d", [P, NT, 9])
                    with nc.Block() as block:
                        @block.sync
                        def _(sp):
                            x9o = sem("x9o")
                            sp.dma_start(acc_d, acc).then_inc(x9o, 16)
                            sp.dma_start(accs_d, accs[:]).then_inc(x9o, 16)
                            sp.wait_ge(x9o, 32)
                if phases > 3:
                    phase(finish_nodes)
            if phases > 4:
                gate = sb(ctx, "gate", [P, 2 * NT])
                slot = sb(ctx, "slot", [P, NT, 2], I32)
                perm = sb(ctx, "perm", [P, 2 * ET], I32)
                erow = sb(ctx, "erow", [1, 2 * ET], I32)
                with ExitStack() as weights:
                    w1 = sb(weights, "w1", [P, 2 * NE, KD, FF])
                    w2 = sb(weights, "w2", [P, 2 * NE, FF // P, D])
                    b1 = sb(weights, "b1", [P, 2 * NE, FF])
                    b2 = sb(weights, "b2", [P, 2 * NE, D])
                    banks_in = ctx.enter_context(nc.semaphore("banks_in"))
                    BANK_LOADS = 4 * NE + 4
                    phase(route)
                    phase(experts)
                phase(combine)


_INS = {"x": "x", "src": "src", "dst": "dst", "Wh": "L0_gnn_Wh", "att_src": "L0_gnn_att_src", "att_dst": "L0_gnn_att_dst",
        "bias_h": "L0_gnn_bias_h", "W_out": "L0_gnn_W_out", "b_out": "L0_gnn_b_out", "gamma": "L0_gnn_gamma",
        "beta": "L0_gnn_beta", "Wr_sp": "L0_ffn_Wr_sp", "br_sp": "L0_ffn_br_sp", "Wr_fq": "L0_ffn_Wr_fq",
        "br_fq": "L0_ffn_br_fq", "Ws1": "L0_ffn_Ws1", "bs1": "L0_ffn_bs1", "Ws2": "L0_ffn_Ws2", "bs2": "L0_ffn_bs2",
        "W1_sp": "L0_ffn_W1_sp", "b1_sp": "L0_ffn_b1_sp", "W2_sp": "L0_ffn_W2_sp", "b2_sp": "L0_ffn_b2_sp",
        "W1_fq": "L0_ffn_W1_fq", "b1_fq": "L0_ffn_b1_fq", "W2_fq": "L0_ffn_W2_fq", "b2_fq": "L0_ffn_b2_fq"}
SCRATCH, PHASES = "Internal", 9


def kernel(**inputs):
    import numpy as np
    import concourse.bacc as bacc
    from concourse.bass_utils import run_bass_kernel_spmd as run

    nc = bacc.Bacc("TRN2", target_bir_lowering=False, num_devices=1)
    arrays, aps = {}, {}
    for short, name in _INS.items():
        arrays["in_" + short] = v = np.ascontiguousarray(inputs[name])
        aps[short] = nc.dram_tensor("in_" + short, v.shape, mybir.dt.from_np(v.dtype), kind="ExternalInput").ap()
    out = nc.dram_tensor("out_x", (N, D), F32, kind="ExternalOutput").ap()
    build(nc, aps, out, SCRATCH, PHASES)
    r = run(nc, [arrays], core_ids=[0])
    return r.results[0]["out_x"]
```

```python
from contextlib import ExitStack

import concourse.bass as bass
from concourse import mybir

F32 = mybir.dt.float32
BF16 = mybir.dt.bfloat16
I32 = mybir.dt.int32
ALU = mybir.AluOpType
ACT = mybir.ActivationFunctionType
AX_X = mybir.AxisListType.X

P = 128
N = 6250
D = 512
KD = D // P
H = 4
HD = D // H
E = 106250
NT = (N + P - 1) // P
NP = NT * P
LAST = N - (NT - 1) * P
GE = 256
NG = (E + GE - 1) // GE
PAD = NG * GE - E
U = NG + NT - 1
CP = 116
NC = U // CP
TU = 2 * U
SLOPE = 0.2
EPS = 1e-5
BIG = 1.0e30
FF = 256
NE = 8
CAP = 5120
ET = NT + NE - 1
assert NC * CP == U


def build(nc, a, out, scratch="Internal", phases=9):
    with ExitStack() as ctx:
        ctx.enter_context(nc.allow_non_contiguous_dma(reason="small columns and index rows"))

        def dram(name, shape, dt=F32):
            if scratch == "Internal":
                return nc.dram_tensor(name, shape, dt).ap()
            return nc.dram_tensor("dbg_" + name, shape, dt, kind=scratch).ap()

        held = []

        def sem(name):
            held.append(nc.alloc_semaphore(name))
            return held[-1]

        def phase(run, *args):
            run(*args)
            nc.clear_and_free_semaphores(list(held))
            held.clear()
            nc.all_engine_barrier()

        def sems(name, n):
            return [sem(f"{name}{i}") for i in range(n)]

        def reused(eng, semaphore, value, n):
            if not isinstance(n, int) or n:
                eng.wait_ge(semaphore, value)

        def pipeline(eng, slots, total, stages):
            rounds = total // slots

            def step(n, s):
                for lag, fn in stages:
                    if s >= lag:
                        fn(n, s - lag)
                    elif not isinstance(n, int) or n:
                        fn(n - 1, s - lag + slots)

            for n in range(2):
                for s in range(slots):
                    step(n, s)
            with eng.Fori(2, rounds) as i:
                for s in range(slots):
                    step(i, s)
            for t in range(rounds * slots, total + max(lag for lag, _ in stages)):
                for lag, fn in stages:
                    if t - lag < total:
                        fn((t - lag) // slots, (t - lag) % slots)

        def earlier(eng, semaphores, n, s, back, each=1):
            if s >= back:
                eng.wait_ge(semaphores[s - back], (n + 1) * each)
            elif not isinstance(n, int) or n:
                eng.wait_ge(semaphores[s - back + len(semaphores)], n * each)

        def sb(stack, name, shape, dt=F32):
            return stack.enter_context(nc.sbuf_tensor(name, shape, dt))

        def ps(stack, name, shape, dt=F32):
            return stack.enter_context(nc.psum_tensor(name, shape, dt))

        xp_d = dram("xp_d", [NP, D])
        as_d = dram("as_d", [NP, H])
        src_d = dram("src_d", [NG, GE], I32)
        dst_d = dram("dst_d", [NG, GE], I32)
        tile_d = dram("tile_d", [U], I32)
        dlb_d = dram("dlb_d", [U, GE], BF16)
        lob_d = dram("lob_d", [U, GE], BF16)
        row_d = dram("row_d", [10, U])
        car_d = dram("car_d", [9, U])

        ident = sb(ctx, "ident", [P, P])
        halfneg = sb(ctx, "halfneg", [P, 1])
        lg = sb(ctx, "lg", [P, NT, 2 * NE])
        sums, edges = ExitStack(), ExitStack()
        acc = sb(sums, "acc", [P, NT * D])
        accs = sb(sums, "accs", [P, NT, 9])
        srcE = sb(edges, "srcE", [P, TU], I32)
        dlE = sb(edges, "dlE", [P, TU])
        trow = sb(edges, "trow", [1, U + 8], I32)
        hiE = sb(edges, "hiE", [P, TU])
        trow0 = sb(edges, "trow0", [1, U], I32)
        x9E = sb(edges, "x9E", [P, TU, 9])

        def constants():
            cz, ci = sem("cz"), sem("ci")
            with nc.Block() as block:
                @block.gpsimd
                def _(pool):
                    nc.gpsimd.memset(ident[:], 0.0).then_inc(cz, 1)
                    nc.gpsimd.memset(halfneg[:], -0.5).then_inc(ci, 1)
                    pool.wait_ge(cz, 1)
                    nc.gpsimd.affine_select(out=ident[:], in_=ident[:], compare_op=ALU.not_equal, fill=1.0,
                                            base=0, pattern=[[-1, P]], channel_multiplier=1).then_inc(ci, 1)
                    pool.wait_ge(ci, 2)

        def project_nodes():
            S = 4
            with ExitStack() as c:
                wc = sb(c, "wc", [P, KD, H, HD])
                att = sb(c, "att", [P, 2, H, HD])
                wa = sb(c, "wa", [P, KD, 2 * H])
                wtmp = sb(c, "wtmp", [P, 2, H, HD])
                xin = sb(c, "xin", [P, S, D])
                xl = sb(c, "xl", [P, S, D])
                xT = sb(c, "xT", [P, S, D])
                xp = sb(c, "xp", [P, S, D])
                st = sb(c, "st", [P, S, 6])
                mv = sb(c, "mv", [P, S, 2])
                ve = sb(c, "ve", [P, S, 1])
                rstd = sb(c, "rstd", [P, S, 1])
                psT = ps(c, "psT", [P, 2, D])
                psX = ps(c, "psX", [P, 2, D])
                psA = ps(c, "psA", [P, 2, D])
                w_in, tmp_ready, wa_ready, x_zero, passed = sem("w_in"), sem("tmp_ready"), sem("wa_ready"), sem("x_zero"), sem("passedA")
                x_in, st_ready, mv_ready, ve_ready = sems("x_in", S), sems("st_ready", S), sems("mv_ready", S), sems("ve_ready", S)
                rstd_ready, xl_ready, xlT_ready, xT_ready = sems("rstd_ready", S), sems("xl_ready", S), sems("xlT_ready", S), sems("xT_ready", S)
                proj_ready, xp_ready, stored = sems("proj_ready", S), sems("xp_ready", S), sems("stored", S)

                def is_last(n, j):
                    return isinstance(n, int) and n * S + j == NT - 1

                with nc.Block() as block:
                    @block.sync
                    def _(sp):
                        for h in range(H):
                            sp.dma_start(wc[:, :, h], a["Wh"][h].rearrange("(k p) o -> p k o", p=P)).then_inc(w_in, 16)
                        for s, name in ((0, "att_src"), (1, "att_dst")):
                            sp.dma_start(att[:, s], a[name].partition_broadcast(P)).then_inc(w_in, 16)

                        def load(n, j):
                            if is_last(n, j):
                                sp.wait_ge(x_zero, 1)
                                sp.dma_start(xin[0:LAST, j], a["x"][(NT - 1) * P:N, :]).then_inc(x_in[j], 16)
                            else:
                                reused(sp, xl_ready[j], n, n)
                                sp.dma_start(xin[:, j], a["x"][bass.ts(n * S + j, P), :]).then_inc(x_in[j], 16)
                        pipeline(sp, S, NT, [(0, load)])

                    @block.vector
                    def _(dve):
                        dve.wait_ge(w_in, 16 * (H + 2))
                        for k in range(KD):
                            if k:
                                dve.wait_ge(wa_ready, k)
                            for s in range(2):
                                nc.vector.tensor_tensor(wtmp[:, s], wc[:, k], att[:, s], ALU.mult).then_inc(tmp_ready, 1)
                            dve.wait_ge(tmp_ready, 2 * k + 2)
                            nc.vector.tensor_reduce(wa[:, k], wtmp[:].rearrange("p s h o -> p (s h) o"), AX_X,
                                                    ALU.add).then_inc(wa_ready, 1)

                        def stats(n, j):
                            if is_last(n, j):
                                dve.wait_ge(xl_ready[j], n)
                                nc.vector.memset(xin[:, j], 0.0).then_inc(x_zero, 1)
                            dve.wait_ge(x_in[j], n * 16 + 16)
                            nc.vector.bn_stats(st[:, j], xin[:, j]).then_inc(st_ready[j], 1)
                            dve.wait_ge(st_ready[j], n + 1)
                            dve.sem_inc(passed, 1)
                            nc.vector.bn_aggr(mv[:, j], st[:, j]).then_inc(mv_ready[j], 1)
                            dve.wait_ge(mv_ready[j], n + 1)
                            nc.vector.tensor_scalar_add(ve[:, j], mv[:, j, 1:2], EPS).then_inc(ve_ready[j], 1)

                        def normalise(n, j):
                            dve.wait_ge(rstd_ready[j], n + 1)
                            reused(dve, xlT_ready[j], n, n)
                            nc.vector.tensor_scalar(xl[:, j], xin[:, j], mv[:, j, 0:1], rstd[:, j, 0:1],
                                                    ALU.subtract, ALU.mult).then_inc(xl_ready[j], 1)

                        def copy_out(n, j):
                            dve.wait_ge(proj_ready[j], n + 1)
                            reused(dve, stored[j], n * 32, n)
                            nc.vector.tensor_copy(aN[:, bass.ds(n * S + j, 1)].rearrange("p a e -> p (a e)"), psA[:, j % 2, 0:2 * H]
                                                  ).then_inc(xp_ready[j], 1)
                            nc.vector.tensor_copy(xp[:, j], psX[:, j % 2]).then_inc(xp_ready[j], 1)
                        pipeline(dve, S, NT, [(0, stats), (1, normalise), (3, copy_out)])

                    @block.gpsimd
                    def _(pool):
                        def deviation(n, j):
                            pool.wait_ge(ve_ready[j], n + 1)
                            nc.gpsimd.tensor_tensor(rstd[:, j], ve[:, j], halfneg[:], ALU.pow).then_inc(rstd_ready[j], 1)
                        pipeline(pool, S, NT, [(0, deviation)])

                    @block.tensor
                    def _(pe):
                        pe.wait_ge(wa_ready, KD)

                        def turn(n, j):
                            pe.wait_ge(xl_ready[j], n + 1)
                            earlier(pe, xT_ready, n, j, 2)
                            for k in range(KD):
                                last = nc.tensor.transpose(psT[:, j % 2, k * P:(k + 1) * P], xl[:, j, k * P:(k + 1) * P], ident[:])
                            last.then_inc(xlT_ready[j], 1)

                        def project(n, j):
                            pe.wait_ge(xT_ready[j], n + 1)
                            earlier(pe, xp_ready, n, j, 2, each=2)
                            for k in range(KD):
                                xTk = xT[:, j, k * P:(k + 1) * P]
                                nc.tensor.matmul(psX[:, j % 2], xTk, wc[:, k].rearrange("p h o -> p (h o)"),
                                                 start=(k == 0), stop=(k == KD - 1))
                                last = nc.tensor.matmul(psA[:, j % 2, 0:2 * H], xTk, wa[:, k], start=(k == 0), stop=(k == KD - 1))
                            last.then_inc(proj_ready[j], 1)
                        pipeline(pe, S, NT, [(0, turn), (1, project)])

                    @block.scalar
                    def _(act):
                        def copy_turned(n, j):
                            act.wait_ge(xlT_ready[j], n + 1)
                            reused(act, proj_ready[j], n, n)
                            nc.scalar.copy(xT[:, j], psT[:, j % 2]).then_inc(xT_ready[j], 1)

                        def store(n, j):
                            act.wait_ge(xp_ready[j], n * 2 + 2)
                            row = bass.ts(n * S + j, P)
                            act.dma_start(xp_d[row, :], xp[:, j]).then_inc(stored[j], 16)
                            act.dma_start(as_d[row, :], aN[:, bass.ds(n * S + j, 1), 0:H].rearrange("p a e -> p (a e)")).then_inc(stored[j], 16)
                        pipeline(act, S, NT, [(0, copy_turned), (2, store)])
                        for j in range(S):
                            act.wait_ge(stored[j], ((NT - 1 - j) // S + 1) * 32)

        def plan_units():
            with ExitStack() as c:
                padv = sb(c, "padv", [1, 2, PAD], I32)
                hi = sb(c, "hi", [1, NG], I32)
                hs = sb(c, "hs", [1, NG], I32)
                gi = sb(c, "gi", [1, NG], I32)
                gf = sb(c, "gf", [1, 2, NG])
                key1 = sb(c, "key1", [1, NG])
                key = sb(c, "key", [P, NG])
                lt = sb(c, "lt", [CP, NC, NG])
                ui = sb(c, "ui", [CP, NC], I32)
                uf = sb(c, "uf", [CP, NC])
                gu = sb(c, "gu", [CP, NC])
                tu = sb(c, "tu", [CP, NC])
                ti = sb(c, "ti", [CP, NC], I32)
                gc = sb(c, "gc", [CP, NC], I32)
                pad_set, edges_in, hi_in, iotas = sem("pad_set"), sem("edges_in"), sem("hi_in"), sem("iotas")
                rows_b, rows_out, lo_steps = sem("rows_b"), sem("rows_outB"), sem("lo_steps")
                loR = sb(c, "loR", [CP, NC, GE], I32)
                loRb = sb(c, "loRb", [CP, NC, GE], BF16)
                dlRb = sb(c, "dlRb", [CP, NC, GE], BF16)
                b1, key_b, gidx, rows_in, rows_f, tile_out, tile_in = (
                    sem("b1"), sem("key_b"), sem("gidx"), sem("rows_in"), sem("rows_f"), sem("tile_out"), sem("tile_in"))

                with nc.Block() as block:
                    @block.sync
                    def _(sp):
                        for k, (to, name) in enumerate(((src_d, "src"), (dst_d, "dst"))):
                            flat = to.rearrange("g e -> (g e)")
                            sp.dma_start(flat[0:E], a[name]).then_inc(edges_in, 16)
                        sp.wait_ge(pad_set, 2)
                        for k, to in enumerate((src_d, dst_d)):
                            flat = to.rearrange("g e -> (g e)")
                            sp.dma_start(flat[E:NG * GE].rearrange("(a e) -> a e", a=1), padv[:, k]).then_inc(edges_in, 16)
                        sp.wait_ge(edges_in, 64)
                        sp.dma_start(hi[:], dst_d[:, GE - 1:GE].rearrange("g e -> e g")).then_inc(hi_in, 16)
                        sp.wait_ge(gidx, 1)
                        sp.dma_start(tile_d.rearrange("(c p) -> p c", p=CP), ti[:]).then_inc(tile_out, 16)
                        sp.wait_ge(tile_out, 16)
                        sp.dma_start(trow[0:1, 3:3 + U], tile_d.rearrange("(a u) -> a u", a=1)).then_inc(tile_in, 16)
                        sp.dma_start(trow0[:], tile_d.rearrange("(a u) -> a u", a=1)).then_inc(tile_in, 16)
                        sp.wait_ge(tile_in, 32)
                        sp.wait_ge(rows_b, 2)
                        for q in range(NC):
                            units = slice(q * CP, (q + 1) * CP)
                            sp.dma_start(dlb_d[units, :], dlRb[:, q]).then_inc(rows_out, 16)
                            sp.dma_start(lob_d[units, :], loRb[:, q]).then_inc(rows_out, 16)
                        sp.wait_ge(rows_out, 32 * NC)

                    @block.gpsimd
                    def _(pool):
                        nc.gpsimd.memset(padv[:, 0], 0).then_inc(pad_set, 1)
                        nc.gpsimd.memset(padv[:, 1], NP - 1).then_inc(pad_set, 1)
                        nc.gpsimd.iota(gi[:], [[1, NG]], base=0, channel_multiplier=0).then_inc(iotas, 1)
                        nc.gpsimd.iota(ui[:], [[CP, NC]], base=0, channel_multiplier=1).then_inc(iotas, 1)
                        pool.wait_ge(b1, 4)
                        nc.gpsimd.partition_broadcast(key[:], key1[:], P).then_inc(key_b, 1)
                        pool.wait_ge(gidx, 2)
                        for k, (rows, table) in enumerate(((srcRi, src_d), (dstRi, dst_d))):
                            for q in range(NC):
                                pool.indirect_dma_start(rows[:, q, :], None, table, bass.IndirectOffsetOnAxis(ap=gc[:, q:q + 1], axis=0)
                                                        ).then_inc(rows_in, 16)
                        pool.wait_ge(rows_in, 32 * NC)

                    @block.vector
                    def _(dve):
                        dve.wait_ge(hi_in, 16)
                        dve.wait_ge(iotas, 2)
                        nc.vector.tensor_scalar(hs[:], hi[:], 7, None, ALU.arith_shift_right).then_inc(b1, 1)
                        nc.vector.tensor_copy(gf[:, 1], gi[:]).then_inc(b1, 1)
                        dve.wait_ge(b1, 2)
                        nc.vector.tensor_copy(gf[:, 0], hs[:]).then_inc(b1, 1)
                        nc.vector.tensor_copy(uf[:], ui[:])
                        dve.wait_ge(b1, 3)
                        nc.vector.tensor_tensor(key1[:], gf[:, 0], gf[:, 1], ALU.add).then_inc(b1, 1)
                        dve.wait_ge(key_b, 1)
                        for q in range(NC):
                            nc.vector.tensor_scalar(lt[:, q], key[0:CP], uf[:, q:q + 1], None, ALU.is_lt).then_inc(b1, 1)
                        dve.wait_ge(b1, 4 + NC)
                        nc.vector.tensor_reduce(gu[:], lt[:], AX_X, ALU.add).then_inc(b1, 1)
                        dve.wait_ge(b1, 5 + NC)
                        nc.vector.tensor_tensor(tu[:], uf[:], gu[:], ALU.subtract).then_inc(b1, 1)
                        dve.wait_ge(b1, 6 + NC)
                        nc.vector.tensor_copy(ti[:], tu[:]).then_inc(gidx, 1)
                        nc.vector.tensor_scalar(gc[:], gu[:], float(NG - 1), None, ALU.min).then_inc(gidx, 1)
                        nc.vector.tensor_scalar(tbase[:], tu[:], float(P), None, ALU.mult).then_inc(b1, 1)
                        dve.wait_ge(b1, 7 + NC)
                        dve.wait_ge(rows_in, 32 * NC)
                        nc.vector.tensor_copy(srcR[:], srcRi[:]).then_inc(rows_f, 1)
                        nc.vector.tensor_copy(dstR[:], dstRi[:]).then_inc(rows_f, 1)
                        dve.wait_ge(rows_f, 2)
                        for q in range(NC):
                            nc.vector.tensor_scalar(dlR[:, q], dstR[:, q], tbase[:, q:q + 1], None, ALU.subtract).then_inc(rows_f, 1)
                        dve.wait_ge(rows_f, 2 + NC)
                        nc.vector.tensor_copy(dlRb[:], dlR[:]).then_inc(rows_b, 1)
                        nc.vector.tensor_scalar(loR[:], srcRi[:], P - 1, None, ALU.bitwise_and).then_inc(lo_steps, 1)
                        dve.wait_ge(lo_steps, 1)
                        nc.vector.tensor_copy(loRb[:], loR[:]).then_inc(rows_b, 1)
                        dve.wait_ge(rows_b, 2)
                        nc.vector.tensor_scalar(loR[:], srcRi[:], 7, None, ALU.arith_shift_right).then_inc(lo_steps, 1)
                        dve.wait_ge(lo_steps, 2)
                        nc.vector.tensor_copy(hiR[:], loR[:]).then_inc(lo_steps, 1)
                        dve.wait_ge(lo_steps, 3)

        def rows_to_edges(pairs, tag):
            with ExitStack() as c:
                pt = ps(c, "pt" + tag, [P, 2, D])
                turned, copied = sem("turned" + tag), sem("copied" + tag)
                jobs = [(rows, to, k) for rows, to in pairs for k in range(2)]
                with nc.Block() as block:
                    @block.tensor
                    def _(pe):
                        for n, (rows, to, k) in enumerate(jobs):
                            if n >= 2:
                                pe.wait_ge(copied, n - 1)
                            for q in range(NC):
                                last = nc.tensor.transpose(pt[:, n % 2, q * CP:(q + 1) * CP], rows[:, q, k * P:(k + 1) * P],
                                                           ident[0:CP, 0:CP])
                            last.then_inc(turned, 1)

                    @block.vector
                    def _(dve):
                        for n, (rows, to, k) in enumerate(jobs):
                            dve.wait_ge(turned, n + 1)
                            nc.vector.tensor_copy(to.rearrange("p (u k) -> p k u", k=2)[:, k], pt[:, n % 2, 0:U]).then_inc(copied, 1)
                        dve.wait_ge(copied, len(jobs))

        def gather_logits():
            S, CU = 2, 8
            CT, VT = 2 * CU, 10
            CHUNKS = U // CU
            W = NT * H
            with ExitStack() as c:
                t3 = sb(c, "t3", [P, NT, 3, 2 * H], BF16)
                left = sb(c, "left", [P, 2, NT, 2 * H])
                pidx = sb(c, "pidx", [P, 1], I32)
                pcol = sb(c, "pcol", [P, 1])
                hidx = sb(c, "hidx", [P, NT, H], I32)
                hrow = sb(c, "hrow", [P, W])
                dlb = sb(c, "dlb", [P, S, CT * P], BF16)
                lob = sb(c, "lob", [P, S, VT * P], BF16)
                dstT = sb(c, "dstT", [P, S, CT * P], BF16)
                loT = sb(c, "loT", [P, S, VT * P], BF16)
                sel = sb(c, "sel", [P, VT, NT, H])
                ix = sb(c, "ixC", [P, S, CT - VT], I32)
                gs = sb(c, "gs", [P, S, CT - VT, H])
                psV = ps(c, "psV", [P, VT // 2, D])
                psW = ps(c, "psW", [P, S, D])
                iotas, prep, table_ready = sem("iotasC"), sem("prepC"), sem("table_ready")
                rows_in, ix_in, onehots = sems("rows_inC", S), sems("ix_inC", S), sems("onehots", S)
                picked, selected, dst_picked, dst_kept = sems("picked", VT // 2), sems("selected", VT // 2), sems("dst_picked", S), sems("dst_kept", S)
                sel_read, gathered, kept, passed = sem("sel_read"), sems("gathered", S), sems("kept", S), sem("passedC")

                with nc.Block() as block:
                    @block.sync
                    def _(sp):
                        def load(n, s):
                            reused(sp, onehots[s], n * 2, n)
                            units = bass.ds((n * S + s) * CU, CU)
                            sp.dma_start(dlb[:, s], dlb_d[units, :].rearrange("u e -> (u e)").partition_broadcast(P)).then_inc(rows_in[s], 16)
                            units = bass.ds((n * S + s) * CU, VT // 2)
                            sp.dma_start(lob[:, s], lob_d[units, :].rearrange("u e -> (u e)").partition_broadcast(P)).then_inc(rows_in[s], 16)
                            reused(sp, gathered[s], n * (16 * (CT - VT)), n)
                            sp.dma_start(ix[:, s], srcE[:, bass.ds((n * S + s) * CT + VT, CT - VT)]).then_inc(ix_in[s], 16)
                        pipeline(sp, S, CHUNKS, [(0, load)])

                    @block.gpsimd
                    def _(pool):
                        nc.gpsimd.iota(pidx[:], [[0, 1]], base=0, channel_multiplier=1).then_inc(iotas, 1)
                        nc.gpsimd.iota(hidx[:], [[1, NT], [0, H]], base=0, channel_multiplier=0).then_inc(iotas, 1)

                        def gather(n, s):
                            pool.wait_ge(ix_in[s], n * 16 + 16)
                            reused(pool, kept[s], n, n)
                            pool.sem_inc(passed, 1)
                            for k in range(CT - VT):
                                pool.indirect_dma_start(gs[:, s, k], None, as_d, bass.IndirectOffsetOnAxis(ap=ix[:, s, k:k + 1], axis=0)
                                                        ).then_inc(gathered[s], 16)
                        pipeline(pool, S, CHUNKS, [(0, gather)])

                    @block.vector
                    def _(dve):
                        count = [0]

                        def link(ins):
                            count[0] += 1
                            ins.then_inc(prep, 1)
                            dve.wait_ge(prep, count[0])

                        dve.wait_ge(iotas, 2)
                        link(nc.vector.tensor_copy(pcol[:], pidx[:]))
                        link(nc.vector.tensor_copy(hrow[:], hidx[:].rearrange("p t h -> p (t h)")))
                        link(nc.vector.tensor_copy(t3[:, :, 0], aN[:]))
                        link(nc.vector.tensor_tensor(left[:, 0], aN[:], t3[:, :, 0], ALU.subtract))
                        link(nc.vector.tensor_copy(t3[:, :, 1], left[:, 0]))
                        link(nc.vector.tensor_tensor(left[:, 1], left[:, 0], t3[:, :, 1], ALU.subtract))
                        nc.vector.tensor_copy(t3[:, :, 2], left[:, 1]).then_inc(table_ready, 1)

                        def onehot(n, s):
                            dve.wait_ge(rows_in[s], n * 32 + 32)
                            reused(dve, dst_picked[s], n, n)
                            nc.vector.tensor_scalar(loT[:, s], lob[:, s], pcol[:, 0:1], None, ALU.is_equal).then_inc(onehots[s], 1)
                            nc.vector.tensor_scalar(dstT[:, s], dlb[:, s], pcol[:, 0:1], None, ALU.is_equal).then_inc(onehots[s], 1)

                        def select(n, s):
                            chunk = n * S + s
                            if not (isinstance(chunk, int) and chunk == 0):
                                dve.wait_ge(sel_read, chunk)
                            for v in range(VT):
                                if v % 2 == 0:
                                    dve.wait_ge(picked[v // 2], chunk + 1)
                                nc.vector.scalar_tensor_tensor(sel[:, v].rearrange("p t h -> p (t h)"), hrow[:], hiE[:, bass.ds(chunk * CT + v, 1)],
                                                               psV[:, v // 2, (v % 2) * W:(v % 2 + 1) * W], ALU.is_equal, ALU.mult
                                                               ).then_inc(selected[v // 2], 1)
                            for m in range(VT // 2):
                                dve.wait_ge(selected[m], chunk * 2 + 2)
                            nc.vector.tensor_reduce(aE[:, bass.ds(chunk * CT, VT), 0:H], sel[:].rearrange("p v t h -> p v h t"), AX_X,
                                                    ALU.add).then_inc(sel_read, 1)
                            dve.wait_ge(dst_picked[s], n + 1)
                            nc.vector.tensor_reduce(aE[:, bass.ds(chunk * CT, CT), H:3 * H],
                                                    psW[:, s, 0:CT * 6 * H].rearrange("p (k s a) -> p k a s", k=CT, s=3), AX_X, ALU.add
                                                    ).then_inc(dst_kept[s], 1)
                        pipeline(dve, S, CHUNKS, [(0, onehot), (1, select)])
                        dve.wait_ge(sel_read, CHUNKS)
                        for s in range(S):
                            dve.wait_ge(dst_kept[s], CHUNKS // S)

                    @block.tensor
                    def _(pe):
                        pe.wait_ge(table_ready, 1)

                        def pick(n, s):
                            chunk = n * S + s
                            slots = nc.values_load_multi_w_load_instructions(
                                trow0[0:1, bass.ds(chunk * CU, CU)], [pe.engine], min_val=0, max_val=NT - 1,
                                skip_runtime_bounds_check_because="a unit's tile is its index less its group, within 0..NT-1")[1]
                            pe.wait_ge(onehots[s], n * 2 + 2)
                            for v in range(VT):
                                if v % 2 == 0 and not (isinstance(chunk, int) and chunk == 0):
                                    pe.wait_ge(selected[v // 2], chunk * 2)
                                for part in range(3):
                                    last = nc.tensor.matmul(psV[:, v // 2, (v % 2) * W:(v % 2 + 1) * W], loT[:, s, v * P:(v + 1) * P],
                                                            t3[:, :, part, 0:H], start=(part == 0), stop=(part == 2))
                                if v % 2:
                                    last.then_inc(picked[v // 2], 1)
                            reused(pe, dst_kept[s], n, n)
                            for k in range(CT):
                                last = nc.tensor.matmul(psW[:, s, k * 6 * H:(k + 1) * 6 * H], dstT[:, s, k * P:(k + 1) * P],
                                                        t3[:, slots[k // 2]].rearrange("p s a -> p (s a)"), start=True, stop=True)
                            last.then_inc(dst_picked[s], 1)
                        pipeline(pe, S, CHUNKS, [(0, pick)])

                    @block.scalar
                    def _(act):
                        def keep(n, s):
                            act.wait_ge(gathered[s], n * (16 * (CT - VT)) + 16 * (CT - VT))
                            nc.scalar.copy(aE[:, bass.ds((n * S + s) * CT + VT, CT - VT), 0:H], gs[:, s]).then_inc(kept[s], 1)
                        pipeline(act, S, CHUNKS, [(0, keep)])
                        for s in range(S):
                            act.wait_ge(kept[s], CHUNKS // S)

        def edges_to_rows():
            with ExitStack() as c:
                pt = ps(c, "ptC", [CP, 2, NC, P])
                turned, copied = sem("turnedC"), sem("copiedC")
                jobs = [(j, k) for j in range(3 * H) for k in range(2)]
                columns = aE.rearrange("p (q u k) j -> p q k j u", q=NC, k=2)
                with nc.Block() as block:
                    @block.tensor
                    def _(pe):
                        for n, (j, k) in enumerate(jobs):
                            if n >= 2:
                                pe.wait_ge(copied, n - 1)
                            for q in range(NC):
                                last = nc.tensor.transpose(pt[:, n % 2, q], columns[:, q, k, j], ident[:])
                            last.then_inc(turned, 1)

                    @block.vector
                    def _(dve):
                        for n, (j, k) in enumerate(jobs):
                            dve.wait_ge(turned, n + 1)
                            nc.vector.tensor_copy(aR[:, j, :, k * P:(k + 1) * P], pt[:, n % 2]).then_inc(copied, 1)
                        dve.wait_ge(copied, len(jobs))

        def edge_softmax():
            with ExitStack() as c:
                sm = sb(c, "sm", [CP, 10, NC])
                car = sb(c, "car", [CP, 9, NC])
                rl = sb(c, "rl", [H, 2, U])
                rd = sb(c, "rd", [H, 2, U])
                cont = sb(c, "cont", [H, U + 1])
                full = sb(c, "full", [H, U])
                pen2 = sb(c, "pen2", [H, 2, U])
                penc = sb(c, "penc", [H, U + 1])
                run2 = sb(c, "run2", [H, 2, U + 1])
                carry = sb(c, "carry", [H, 2, U])
                d1, rows_out, rows_back, car_out, car_back = (sem("d1"), sem("rows_out"), sem("rows_back"),
                                                              sem("car_out"), sem("car_back"))
                small_ready, carry_ready, logits_ready, exp_ready = sem("small_ready"), sem("carry_ready"), sem("logits_ready"), sem("exp_ready")
                asv, aself, adst = aR[:, 0:H], aR[:, H:2 * H], aR[:, 2 * H:3 * H]

                with nc.Block() as block:
                    @block.vector
                    def _(dve):
                        count = [0]

                        def link(ins):
                            count[0] += 1
                            ins.then_inc(d1, 1)
                            dve.wait_ge(d1, count[0])

                        def flat(ap):
                            return ap.rearrange("p q e -> p (q e)")

                        link(nc.vector.tensor_scalar(penv, dlR[:], 0.0, None, ALU.is_ge))
                        link(nc.vector.scalar_tensor_tensor(penf, dlR[:], float(P), penv, ALU.is_lt, ALU.mult))
                        link(nc.vector.tensor_scalar(penv, penf, -1.0, BIG, ALU.add, ALU.mult))
                        for h in range(H):
                            link(nc.vector.tensor_tensor(asv[:, h], asv[:, h], penv, ALU.add))
                        link(nc.vector.memset(last1[:, :, GE - 1:GE], 1.0))
                        link(nc.vector.tensor_tensor(last1[:, :, 0:GE - 1], dstR[:, :, 1:GE], dstR[:, :, 0:GE - 1], ALU.not_equal))
                        link(nc.vector.tensor_scalar(penb, last1, -BIG, None, ALU.mult))
                        link(nc.vector.memset(penf[:, :, 0:1], -BIG))
                        link(nc.vector.tensor_copy(penf[:, :, 1:GE], penb[:, :, 0:GE - 1]))
                        for h in range(H):
                            link(nc.vector.tensor_tensor_scan(flat(fwd[:, h]), flat(penf), flat(asv[:, h]), 0.0, ALU.add, ALU.max))
                            link(nc.vector.tensor_tensor_scan(flat(bwd[:, h])[:, ::-1], flat(penb)[:, ::-1],
                                                              flat(asv[:, h])[:, ::-1], 0.0, ALU.add, ALU.max))
                        link(nc.vector.tensor_copy(sm[:, 0:H], fwd[:, :, :, GE - 1]))
                        link(nc.vector.tensor_copy(sm[:, H:2 * H], bwd[:, :, :, 0]))
                        link(nc.vector.tensor_copy(sm[:, 8], dstR[:, :, 0]))
                        nc.vector.tensor_copy(sm[:, 9], dstR[:, :, GE - 1]).then_inc(small_ready, 1)
                        dve.wait_ge(small_ready, 1)
                        for q in range(NC):
                            link(nc.vector.tensor_scalar(penf[:, q], dstR[:, q], sm[:, 8, q:q + 1], -BIG, ALU.not_equal, ALU.mult))
                            link(nc.vector.tensor_scalar(penb[:, q], dstR[:, q], sm[:, 9, q:q + 1], -BIG, ALU.not_equal, ALU.mult))
                        for h in range(H):
                            link(nc.vector.tensor_tensor(fwd[:, h], fwd[:, h], bwd[:, h], ALU.max))
                        dve.wait_ge(rows_back, 64)
                        link(nc.vector.memset(cont[:], 0.0))
                        link(nc.vector.tensor_tensor(cont[:, 1:U], rd[:, 0, 1:U], rd[:, 1, 0:U - 1], ALU.is_equal))
                        link(nc.vector.tensor_tensor(full[:], rd[:, 0], rd[:, 1], ALU.is_equal))
                        link(nc.vector.tensor_tensor(pen2[:, 0], full[:], cont[:, 0:U], ALU.mult))
                        link(nc.vector.tensor_tensor(pen2[:, 1], full[:], cont[:, 1:U + 1], ALU.mult))
                        link(nc.vector.tensor_scalar(pen2[:], pen2[:], -1.0, BIG, ALU.add, ALU.mult))
                        link(nc.vector.tensor_scalar(penc[:], cont[:], -1.0, BIG, ALU.add, ALU.mult))
                        link(nc.vector.memset(run2[:], 0.0))
                        link(nc.vector.tensor_tensor_scan(run2[:, 0, 1:U + 1], pen2[:, 0], rl[:, 0], -BIG, ALU.add, ALU.max))
                        link(nc.vector.tensor_tensor_scan(run2[:, 1, 0:U][:, ::-1], pen2[:, 1][:, ::-1], rl[:, 1][:, ::-1],
                                                          -BIG, ALU.add, ALU.max))
                        link(nc.vector.tensor_tensor(carry[:, 0], run2[:, 0, 0:U], penc[:, 0:U], ALU.add))
                        nc.vector.tensor_tensor(carry[:, 1], run2[:, 1, 1:U + 1], penc[:, 1:U + 1], ALU.add).then_inc(carry_ready, 1)
                        dve.wait_ge(car_back, 16 * (2 * NC + 1))
                        for h in range(H):
                            for q in range(NC):
                                link(nc.vector.scalar_tensor_tensor(fwd[:, h, q], penf[:, q], car[:, h, q:q + 1], fwd[:, h, q], ALU.add, ALU.max))
                                link(nc.vector.scalar_tensor_tensor(fwd[:, h, q], penb[:, q], car[:, H + h, q:q + 1], fwd[:, h, q], ALU.add, ALU.max))
                        link(nc.vector.tensor_scalar(last1[:, :, GE - 1], car[:, 8], -1.0, 1.0, ALU.mult, ALU.add))
                        for h in range(H):
                            link(nc.vector.tensor_tensor(fwd[:, h], fwd[:, h], aself[:, h], ALU.max))
                            link(nc.vector.tensor_tensor(fwd[:, h], fwd[:, h], adst[:, h], ALU.add))
                            link(nc.vector.scalar_tensor_tensor(fwd[:, h], fwd[:, h], SLOPE, fwd[:, h], ALU.mult, ALU.max))
                            for part in (asv, aself):
                                link(nc.vector.tensor_tensor(part[:, h], part[:, h], adst[:, h], ALU.add))
                                link(nc.vector.scalar_tensor_tensor(part[:, h], part[:, h], SLOPE, part[:, h], ALU.mult, ALU.max))
                                nc.vector.tensor_tensor(part[:, h], part[:, h], fwd[:, h], ALU.subtract).then_inc(logits_ready, 1)
                        for h in range(H):
                            dve.wait_ge(exp_ready, 2 * h + 2)
                            link(nc.vector.tensor_tensor(aself[:, h], aself[:, h], last1, ALU.mult))

                    @block.scalar
                    def _(act):
                        for h in range(H):
                            act.wait_ge(logits_ready, 2 * h + 2)
                            for part in (asv, aself):
                                nc.scalar.activation(part[:, h], part[:, h], ACT.Exp).then_inc(exp_ready, 1)
                        act.wait_ge(exp_ready, 2 * H)

                    @block.sync
                    def _(sp):
                        sp.wait_ge(small_ready, 1)
                        for q in range(NC):
                            sp.dma_start(row_d[:, q * CP:(q + 1) * CP].rearrange("j p -> p j"), sm[:, :, q]).then_inc(rows_out, 16)
                        sp.wait_ge(rows_out, 16 * NC)
                        sp.dma_start(rl[:, 0], row_d[0:H]).then_inc(rows_back, 16)
                        sp.dma_start(rl[:, 1], row_d[H:2 * H]).then_inc(rows_back, 16)
                        sp.dma_start(rd[:, 0], row_d[8].partition_broadcast(H)).then_inc(rows_back, 16)
                        sp.dma_start(rd[:, 1], row_d[9].partition_broadcast(H)).then_inc(rows_back, 16)
                        sp.wait_ge(carry_ready, 1)
                        for k in range(2):
                            sp.dma_start(car_d[k * H:(k + 1) * H], carry[:, k]).then_inc(car_out, 16)
                        sp.dma_start(car_d[8:9], cont[0:1, 1:U + 1]).then_inc(car_out, 16)
                        sp.wait_ge(car_out, 48)
                        for q in range(NC):
                            cols = slice(q * CP, (q + 1) * CP)
                            for k in range(2):
                                sp.dma_start(car[:, k * H:(k + 1) * H, q], car_d[k * H:(k + 1) * H, cols].rearrange("j p -> p j")).then_inc(car_back, 16)
                        sp.dma_start(car[:, 8], car_d[8].rearrange("(q p) -> p q", p=CP)).then_inc(car_back, 16)
                        sp.wait_ge(car_back, 16 * (2 * NC + 1))

        def aggregate():
            S, LAG = 8, 3
            UT = 2
            with ExitStack() as c:
                ix = sb(c, "ix", [P, S, UT], I32)
                g = sb(c, "g", [P, S, UT, H, HD])
                x9 = sb(c, "x9", [P, S, UT, 9])
                dl = sb(c, "dl", [P, S, UT])
                onehot = sb(c, "onehot", [P, S, UT, P])
                nodei = sb(c, "nodei", [P, P], I32)
                nodef = sb(c, "nodef", [P, P])
                psO = ps(c, "psO", [P, 4, D])
                psS = ps(c, "psS", [P, 4, D])
                acc_zero, node_iota, node_row, passed = sem("acc_zero"), sem("node_iota"), sem("node_row"), sem("passedE")
                ix_in, g_in = sems("ix_in", S), sems("g_in", S * UT)
                weights_in, onehot_ready = sems("weights_in", S), sems("onehot_ready", S)
                scaled_act, scaled_dve, summed, added = sems("scaled_act", S), sems("scaled_dve", S), sems("summed", S), sems("added", S)

                def tiles(n, s):
                    return bass.ds(n * (S * UT) + s * UT, UT)

                with nc.Block() as block:
                    @block.sync
                    def _(sp):
                        def indices(n, s):
                            for k in range(UT):
                                reused(sp, g_in[s * UT + k], n * 16, n)
                            sp.dma_start(ix[:, s], srcE[:, tiles(n, s)]).then_inc(ix_in[s], 16)
                        pipeline(sp, S, U, [(0, indices)])

                    @block.gpsimd
                    def _(pool):
                        nc.gpsimd.iota(nodei[:], [[1, P]], base=0, channel_multiplier=0).then_inc(node_iota, 1)

                        def gather(n, s):
                            pool.wait_ge(ix_in[s], n * 16 + 16)
                            reused(pool, summed[s], n, n)
                            pool.sem_inc(passed, 1)
                            for k in range(UT):
                                pool.indirect_dma_start(g[:, s, k].rearrange("p h o -> p (h o)"), None, xp_d,
                                                        bass.IndirectOffsetOnAxis(ap=ix[:, s, k:k + 1], axis=0)
                                                        ).then_inc(g_in[s * UT + k], 16)
                        pipeline(pool, S, U, [(0, gather)])

                    @block.vector
                    def _(dve):
                        nc.vector.memset(acc, 0.0).then_inc(acc_zero, 1)
                        nc.vector.memset(accs[:], 0.0).then_inc(acc_zero, 1)
                        dve.wait_ge(node_iota, 1)
                        nc.vector.tensor_copy(nodef[:], nodei[:]).then_inc(node_row, 1)
                        dve.wait_ge(node_row, 1)
                        dve.wait_ge(acc_zero, 2)

                        def weights(n, s):
                            reused(dve, summed[s], n, n)
                            nc.vector.tensor_copy(x9[:, s], x9E[:, tiles(n, s)]).then_inc(weights_in[s], 1)
                            nc.vector.tensor_copy(dl[:, s], dlE[:, tiles(n, s)]).then_inc(weights_in[s], 1)
                            dve.wait_ge(weights_in[s], n * 2 + 2)
                            for k in range(UT):
                                nc.vector.tensor_scalar(onehot[:, s, k], nodef[:], dl[:, s, k:k + 1], None,
                                                        ALU.is_equal).then_inc(onehot_ready[s], 1)

                        def scale(n, s):
                            for k in range(UT):
                                dve.wait_ge(g_in[s * UT + k], n * 16 + 16)
                                for h in range(2, H):
                                    nc.vector.tensor_scalar(g[:, s, k, h], g[:, s, k, h], x9[:, s, k, h:h + 1], None,
                                                            ALU.mult).then_inc(scaled_dve[s], 1)

                        def tile_of(n, s):
                            if isinstance(n, int):
                                return nc.values_load_multi_w_load_instructions(
                                    trow[0:1, bass.ds(LAG + n * S + s, 1)], [dve.engine], min_val=0, max_val=NT - 1,
                                    skip_runtime_bounds_check_because=IN_RANGE)[1][0]
                            if s == S - LAG:
                                slots[:] = nc.values_load_multi_w_load_instructions(
                                    trow[0:1, bass.ds(n * S + S, S)], [dve.engine], min_val=0, max_val=NT - 1,
                                    skip_runtime_bounds_check_because=IN_RANGE)[1]
                            return slots[(s + LAG) % S]

                        IN_RANGE = "a unit's tile is its index less its group, within 0..NT-1"
                        slots = []

                        def add(n, s):
                            t = tile_of(n, s)
                            dve.wait_ge(summed[s], n + 1)
                            earlier(dve, added, n, s, 1, each=2)
                            nc.vector.tensor_tensor(acc[:, t], acc[:, t], psO[:, s % 4], ALU.add).then_inc(added[s], 1)
                            nc.vector.tensor_tensor(accs[:, t], accs[:, t], psS[:, s % 4, 0:9], ALU.add).then_inc(added[s], 1)
                        pipeline(dve, S, U, [(0, weights), (0, scale), (LAG, add)])

                    @block.scalar
                    def _(act):
                        def scale(n, s):
                            act.wait_ge(weights_in[s], n * 2 + 2)
                            for k in range(UT):
                                act.wait_ge(g_in[s * UT + k], n * 16 + 16)
                                for h in range(2):
                                    nc.scalar.activation(g[:, s, k, h], g[:, s, k, h], ACT.Copy,
                                                         scale=x9[:, s, k, h:h + 1]).then_inc(scaled_act[s], 1)
                        pipeline(act, S, U, [(0, scale)])

                    @block.tensor
                    def _(pe):
                        def sum_unit(n, s):
                            earlier(pe, added, n, s, 4, each=2)
                            pe.wait_ge(onehot_ready[s], n * UT + UT)
                            for k in range(UT):
                                pe.wait_ge(scaled_act[s], n * (2 * UT) + (k + 1) * 2)
                                pe.wait_ge(scaled_dve[s], n * (2 * UT) + (k + 1) * 2)
                                nc.tensor.matmul(psO[:, s % 4], onehot[:, s, k], g[:, s, k].rearrange("p h o -> p (h o)"),
                                                 start=(k == 0), stop=(k == UT - 1))
                                last = nc.tensor.matmul(psS[:, s % 4, 0:9], onehot[:, s, k], x9[:, s, k],
                                                        start=(k == 0), stop=(k == UT - 1))
                            last.then_inc(summed[s], 1)
                        pipeline(pe, S, U, [(0, sum_unit)])

        def finish_nodes():
            S = 6
            with ExitStack() as c:
                woT = sb(c, "woT", [P, KD, D])
                ws1 = sb(c, "ws1", [P, KD, FF])
                ws2 = sb(c, "ws2", [P, FF // P, D])
                wr = sb(c, "wr", [P, KD, 2 * NE])
                bs1 = sb(c, "bs1", [P, FF // P])
                row = {name: sb(c, "row_" + name, [P, D]) for name in ("bias_h", "b_out", "gamma", "beta", "bs2")}
                eself = sb(c, "eself", [P, NT, H])
                rsum = sb(c, "rsum", [P, NT, H])
                xp = sb(c, "xpF", [P, S, D])
                xin = sb(c, "xinF", [P, S, D])
                rT = sb(c, "rT", [P, 2, D])
                y = sb(c, "y", [P, 2, D])
                x1b = sb(c, "x1b", [P, 3, D])
                xl = sb(c, "xlF", [P, 3, D])
                x2T = sb(c, "x2T", [P, 2, D])
                hsT = sb(c, "hsT", [P, 2, FF])
                st = sb(c, "stF", [P, S, 2, 6])
                mv = sb(c, "mvF", [P, S, 2, 2])
                ve = sb(c, "veF", [P, S, 2])
                rstd = sb(c, "rstdF", [P, S, 2])
                wo = xin[:, 0:KD]
                psT = ps(c, "psTF", [P, 2, D])
                psY = ps(c, "psYF", [P, 2, D])
                psU = ps(c, "psUF", [P, 2, D])
                psD = ps(c, "psDF", [P, 2, D])
                w_in, wT_turned, wT_ready, sums_ready = sem("w_inF"), sem("wT_turned"), sem("wT_ready"), sem("sums_ready")
                x_in, x_zero, passed = sems("x_inF", S), sem("x_zeroF"), sem("passedF")
                self_added, hh_ready, hT_turned, hT_ready = sems("self_added", S), sems("hh_ready", S), sems("hT_turned", S), sems("hT_ready", S)
                y_summed, y_ready, st_ready, mv_ready = sems("y_summed", S), sems("y_readyF", S), sems("st_readyF", S), sems("mv_readyF", S)
                ve_ready, rstd_ready, norm_steps = sems("ve_readyF", S), sems("rstd_readyF", S), sems("norm_steps", S)
                xb_ready, x1_ready, x1b_ready = sems("xb_ready", S), sems("x1_ready", S), sems("x1b_ready", S)
                xl_ready, xl_turned, x2T_ready = sems("xl_readyF", S), sems("xl_turned", S), sems("x2T_ready", S)
                up_summed, hs_ready, down_summed = sems("up_summed", S), sems("hs_ready", S), sems("down_summed", S)
                z_ready, xl_stored, z_stored = sems("z_ready", S), sems("xl_stored", S), sems("z_stored", S)
                LOADS = 13 - 2
                R0 = FF

                def is_last(n, j):
                    return isinstance(n, int) and n * S + j == NT - 1

                with nc.Block() as block:
                    @block.sync
                    def _(sp):
                        sp.dma_start(wo, a["W_out"].rearrange("(k p) i -> p k i", p=P)).then_inc(w_in, 16)
                        sp.dma_start(ws1[:], a["Ws1"].rearrange("(k p) f -> p k f", p=P)).then_inc(w_in, 16)
                        sp.dma_start(ws2[:], a["Ws2"].rearrange("(k p) o -> p k o", p=P)).then_inc(w_in, 16)
                        sp.dma_start(bs1[:], a["bs1"].rearrange("(f p) -> p f", p=P)).then_inc(w_in, 16)
                        for b, bank in enumerate(("sp", "fq")):
                            sp.dma_start(wr[:, :, b * NE:(b + 1) * NE], a["Wr_" + bank].rearrange("(k p) e -> p k e", p=P)).then_inc(w_in, 16)
                        for name, to in row.items():
                            v = a[name].rearrange("h o -> (h o)") if name == "bias_h" else a[name]
                            sp.dma_start(to[:], v.partition_broadcast(P)).then_inc(w_in, 16)

                        sp.wait_ge(wT_turned, KD)

                        def load(n, j):
                            reused(sp, hT_turned[j], n, n)
                            tile = bass.ts(n * S + j, P)
                            sp.dma_start(xp[:, j], xp_d[tile, :]).then_inc(x_in[j], 16)
                            if is_last(n, j):
                                sp.wait_ge(x_zero, 1)
                                sp.dma_start(xin[0:LAST, j], a["x"][(NT - 1) * P:N, :]).then_inc(x_in[j], 16)
                            else:
                                reused(sp, x1b_ready[j], n, n)
                                reused(sp, xl_ready[j], n, n)
                                sp.dma_start(xin[:, j], a["x"][tile, :]).then_inc(x_in[j], 16)
                        pipeline(sp, S, NT, [(0, load)])

                    @block.gpsimd
                    def _(pool):
                        pool.wait_ge(w_in, 16 * LOADS)

                        def add_beta(n, j):
                            if is_last(n, j):
                                pool.wait_ge(x1b_ready[j], n)
                                pool.wait_ge(xl_ready[j], n)
                                nc.gpsimd.memset(xin[:, j], 0.0).then_inc(x_zero, 1)
                            pool.wait_ge(x_in[j], n * 32 + 32)
                            nc.gpsimd.tensor_tensor(xin[:, j], xin[:, j], row["beta"][:], ALU.add).then_inc(xb_ready[j], 1)

                        def deviation(which):
                            def fn(n, j):
                                pool.wait_ge(ve_ready[j], n * 2 + which + 1)
                                nc.gpsimd.tensor_tensor(rstd[:, j, which:which + 1], ve[:, j, which:which + 1], halfneg[:],
                                                        ALU.pow).then_inc(rstd_ready[j], 1)
                            return fn

                        def add_bs2(n, j):
                            pool.wait_ge(x1_ready[j], n + 1)
                            earlier(pool, z_stored, n, j, 3, each=16)
                            nc.gpsimd.tensor_tensor(x1b[:, j % 3], xin[:, j], row["bs2"][:], ALU.add).then_inc(x1b_ready[j], 1)
                        pipeline(pool, S, NT, [(0, add_beta), (3, deviation(1)), (2, deviation(0)), (3, add_bs2)])

                    @block.vector
                    def _(dve):
                        dve.wait_ge(w_in, 16 * LOADS)
                        for k in range(KD):
                            dve.wait_ge(wT_turned, k + 1)
                            nc.vector.tensor_copy(woT[:, k], psT[:, k % 2]).then_inc(wT_ready, 1)
                        nc.vector.tensor_scalar(rsum[:], accs[:, :, 8:9].to_broadcast([P, NT, H]), -1.0, 1.0, ALU.mult, ALU.add).then_inc(sums_ready, 1)
                        dve.wait_ge(sums_ready, 1)
                        nc.vector.tensor_tensor(eself[:], accs[:, :, H:2 * H], rsum[:], ALU.add).then_inc(sums_ready, 1)
                        dve.wait_ge(sums_ready, 2)
                        nc.vector.scalar_tensor_tensor(rsum[:], accs[:, :, 0:H], 1e-16, eself[:], ALU.add, ALU.add).then_inc(sums_ready, 1)
                        dve.wait_ge(sums_ready, 3)
                        nc.vector.reciprocal(rsum[:], rsum[:]).then_inc(sums_ready, 1)
                        dve.wait_ge(sums_ready, 4)

                        def heads(n, j):
                            t = n * S + j
                            dve.wait_ge(x_in[j], n * 32 + 32)
                            for h in range(H):
                                cols = slice(h * HD, (h + 1) * HD)
                                nc.vector.scalar_tensor_tensor(xp[:, j, cols], xp[:, j, cols], eself[:, bass.ds(t, 1), h],
                                                               acc[:, bass.ds(t, 1), cols].rearrange("p a d -> p (a d)"), ALU.mult, ALU.add
                                                               ).then_inc(self_added[j], 1)
                            dve.wait_ge(self_added[j], n * 4 + 4)
                            for h in range(H):
                                cols = slice(h * HD, (h + 1) * HD)
                                nc.vector.scalar_tensor_tensor(xp[:, j, cols], xp[:, j, cols], rsum[:, bass.ds(t, 1), h],
                                                               row["bias_h"][:, cols], ALU.mult, ALU.add).then_inc(hh_ready[j], 1)

                        def stats(v, which, n, j):
                            nc.vector.bn_stats(st[:, j, which], v).then_inc(st_ready[j], 1)
                            dve.wait_ge(st_ready[j], n * 2 + which + 1)
                            dve.sem_inc(passed, 1)
                            nc.vector.bn_aggr(mv[:, j, which], st[:, j, which]).then_inc(mv_ready[j], 1)
                            dve.wait_ge(mv_ready[j], n * 2 + which + 1)
                            nc.vector.tensor_scalar_add(ve[:, j, which:which + 1], mv[:, j, which, 1:2], EPS).then_inc(ve_ready[j], 1)

                        def project(n, j):
                            dve.wait_ge(y_summed[j], n + 1)
                            earlier(dve, x1_ready, n, j, 2)
                            nc.vector.tensor_tensor(y[:, j % 2], psY[:, j % 2], row["b_out"][:], ALU.add).then_inc(y_ready[j], 1)
                            dve.wait_ge(y_ready[j], n + 1)
                            dve.sem_inc(passed, 1)
                            stats(y[:, j % 2], 0, n, j)

                        def residual(n, j):
                            dve.wait_ge(rstd_ready[j], n * 2 + 1)
                            nc.vector.tensor_scalar(y[:, j % 2], y[:, j % 2], mv[:, j, 0, 0:1], rstd[:, j, 0:1],
                                                    ALU.subtract, ALU.mult).then_inc(norm_steps[j], 1)
                            dve.wait_ge(norm_steps[j], n * 2 + 1)
                            nc.vector.tensor_tensor(y[:, j % 2], y[:, j % 2], row["gamma"][:], ALU.mult).then_inc(norm_steps[j], 1)
                            dve.wait_ge(norm_steps[j], n * 2 + 2)
                            dve.wait_ge(xb_ready[j], n + 1)
                            nc.vector.tensor_tensor(xin[:, j], y[:, j % 2], xin[:, j], ALU.add).then_inc(x1_ready[j], 1)
                            dve.wait_ge(x1_ready[j], n + 1)
                            dve.sem_inc(passed, 1)
                            stats(xin[:, j], 1, n, j)

                        def normalise(n, j):
                            dve.wait_ge(rstd_ready[j], n * 2 + 2)
                            earlier(dve, xl_stored, n, j, 3, each=16)
                            earlier(dve, xl_turned, n, j, 3)
                            nc.vector.tensor_scalar(xl[:, j % 3], xin[:, j], mv[:, j, 1, 0:1], rstd[:, j, 1:2],
                                                    ALU.subtract, ALU.mult).then_inc(xl_ready[j], 1)

                        def total(n, j):
                            dve.wait_ge(down_summed[j], n + 1)
                            dve.wait_ge(x1b_ready[j], n + 1)
                            nc.vector.tensor_tensor(x1b[:, j % 3], psD[:, j % 2], x1b[:, j % 3], ALU.add).then_inc(z_ready[j], 1)
                        pipeline(dve, S, NT, [(4, normalise), (3, residual), (2, project), (0, heads), (5, total)])

                    @block.tensor
                    def _(pe):
                        pe.wait_ge(w_in, 16 * LOADS)
                        for k in range(KD):
                            if k >= 2:
                                pe.wait_ge(wT_ready, k - 1)
                            for o in range(KD):
                                last = nc.tensor.transpose(psT[:, k % 2, o * P:(o + 1) * P], wo[:, o, k * P:(k + 1) * P], ident[:])
                            last.then_inc(wT_turned, 1)
                        pe.wait_ge(wT_ready, KD)

                        def turn(to, rows):
                            for k in range(KD):
                                last = nc.tensor.transpose(to[:, k * P:(k + 1) * P], rows[:, k * P:(k + 1) * P], ident[:])
                            return last

                        def turn_heads(n, j):
                            pe.wait_ge(hh_ready[j], n * 4 + 4)
                            earlier(pe, hT_ready, n, j, 1)
                            turn(psT[:, 0], xp[:, j]).then_inc(hT_turned[j], 1)

                        def project(n, j):
                            pe.wait_ge(hT_ready[j], n + 1)
                            earlier(pe, y_ready, n, j, 2)
                            for k in range(KD):
                                last = nc.tensor.matmul(psY[:, j % 2], rT[:, j % 2, k * P:(k + 1) * P], woT[:, k], start=(k == 0), stop=(k == KD - 1))
                            last.then_inc(y_summed[j], 1)

                        def turn_rows(n, j):
                            pe.wait_ge(xl_ready[j], n + 1)
                            earlier(pe, x2T_ready, n, j, 1)
                            turn(psT[:, 1], xl[:, j % 3]).then_inc(xl_turned[j], 1)

                        def up(n, j):
                            pe.wait_ge(x2T_ready[j], n + 1)
                            earlier(pe, hs_ready, n, j, 2, each=3)
                            for k in range(KD):
                                nc.tensor.matmul(psU[:, j % 2, R0:R0 + 2 * NE], x2T[:, j % 2, k * P:(k + 1) * P], wr[:, k], start=(k == 0), stop=(k == KD - 1))
                            for f in range(FF // P):
                                for k in range(KD):
                                    last = nc.tensor.matmul(psU[:, j % 2, f * P:(f + 1) * P], ws1[:, k, f * P:(f + 1) * P],
                                                            x2T[:, j % 2, k * P:(k + 1) * P], start=(k == 0), stop=(k == KD - 1))
                            last.then_inc(up_summed[j], 1)

                        def down(n, j):
                            pe.wait_ge(hs_ready[j], n * 3 + 3)
                            earlier(pe, z_ready, n, j, 2)
                            for f in range(FF // P):
                                last = nc.tensor.matmul(psD[:, j % 2], hsT[:, j % 2, f * P:(f + 1) * P], ws2[:, f], start=(f == 0), stop=(f == FF // P - 1))
                            last.then_inc(down_summed[j], 1)
                        pipeline(pe, S, NT, [(4, turn_rows), (5, down), (4, up), (0, turn_heads), (1, project)])

                    @block.scalar
                    def _(act):
                        act.wait_ge(w_in, 16 * LOADS)

                        def copy_heads(n, j):
                            act.wait_ge(hT_turned[j], n + 1)
                            earlier(act, y_summed, n, j, 2)
                            nc.scalar.copy(rT[:, j % 2], psT[:, 0]).then_inc(hT_ready[j], 1)

                        def copy_rows(n, j):
                            act.wait_ge(xl_turned[j], n + 1)
                            earlier(act, up_summed, n, j, 2)
                            nc.scalar.copy(x2T[:, j % 2], psT[:, 1]).then_inc(x2T_ready[j], 1)
                            act.wait_ge(xl_ready[j], n + 1)
                            act.dma_start(xl_d[bass.ts(n * S + j, P), :], xl[:, j % 3]).then_inc(xl_stored[j], 16)

                        def gelu(n, j):
                            act.wait_ge(up_summed[j], n + 1)
                            earlier(act, down_summed, n, j, 2)
                            for f in range(FF // P):
                                cols = slice(f * P, (f + 1) * P)
                                nc.scalar.activation(hsT[:, j % 2, cols], psU[:, j % 2, cols], ACT.Gelu, bias=bs1[:, f:f + 1]).then_inc(hs_ready[j], 1)
                            nc.scalar.copy(lg[:, bass.ds(n * S + j, 1)].rearrange("p a e -> p (a e)"), psU[:, j % 2, R0:R0 + 2 * NE]).then_inc(hs_ready[j], 1)

                        def store(n, j):
                            act.wait_ge(z_ready[j], n + 1)
                            act.dma_start(z_d[bass.ts(n * S + j, P), :], x1b[:, j % 3]).then_inc(z_stored[j], 16)
                        pipeline(act, S, NT, [(4, copy_rows), (4, gelu), (0, copy_heads), (5, store)])
                        for j in range(S):
                            act.wait_ge(xl_stored[j], 16 * ((NT - 1 - j) // S + 1))
                            act.wait_ge(z_stored[j], 16 * ((NT - 1 - j) // S + 1))

        def route():
            B2 = 2 * NE
            with ExitStack() as c:
                iota8 = sb(c, "iota8", [P, B2], I32)
                iota8f = sb(c, "iota8f", [P, B2])
                prow = sb(c, "prow", [P, 1], I32)
                real = sb(c, "real", [P, 1])
                far = sb(c, "far", [P, 1])
                toki = sb(c, "toki", [P, NT], I32)
                jrow = sb(c, "jrow", [1, ET], I32)
                jrowf = sb(c, "jrowf", [1, ET])
                triu = sb(c, "triu", [P, P])
                ones = sb(c, "ones", [P, P])
                mx = sb(c, "mx", [P, 2 * NT])
                br = sb(c, "br", [P, B2])
                br_in = sem("br_in")
                ex = sb(c, "ex", [P, NT, B2])
                oh = sb(c, "oh", [P, NT, B2])
                cum = sb(c, "cum", [P, NT, B2])
                tot = sb(c, "tot", [P, NT, B2])
                pre = sb(c, "pre", [P, NT, B2])
                cnt = sb(c, "cnt", [P, B2], I32)
                nt = sb(c, "nt", [P, B2])
                nti = sb(c, "nti", [P, B2], I32)
                ends = sb(c, "ends", [P, 2, NE])
                base = sb(c, "base", [P, B2])
                slotf = sb(c, "slotf", [P, 2 * NT])
                posf = sb(c, "posf", [P, 2 * NT])
                sci = sb(c, "sci", [P, 2 * NT], I32)
                ecmp = sb(c, "ecmp", [1, 2, ET, NE])
                ef = sb(c, "ef", [1, 2, ET])
                fill = sb(c, "fill", [P, 2 * ET], I32)
                psC = ps(c, "psC", [P, 2, D])
                psN = ps(c, "psN", [P, 2, D])
                SB = 7
                idx = sb(c, "idx", [P, SB, 2], I32)
                tok = sb(c, "tok", [P, SB], I32)
                g1, gz, g2, g3, g4, filled = sem("g1"), sem("gz"), sem("g2"), sem("g3"), sem("g4"), sem("filled")
                e_ready, e_done, staged, scattered, perm_in, passed = (sem("e_ready"), sem("e_done"), sem("staged"), sem("scattered"),
                                                                       sem("perm_in"), sem("passedG"))
                banks = "p t (b e) -> p (t b) e"
                halves = (slice(0, NT // 2), slice(NT // 2, NT))

                with nc.Block() as block:
                    @block.gpsimd
                    def _(pool):
                        nc.gpsimd.iota(iota8[:], [[0, 2], [1, NE]], base=0, channel_multiplier=0).then_inc(gz, 1)
                        nc.gpsimd.iota(prow[:], [[0, 1]], base=0, channel_multiplier=1).then_inc(gz, 1)
                        nc.gpsimd.iota(toki[:], [[P, NT]], base=0, channel_multiplier=1).then_inc(gz, 1)
                        nc.gpsimd.iota(jrow[:], [[1, ET]], base=0, channel_multiplier=0).then_inc(gz, 1)
                        nc.gpsimd.memset(ones[:], 1.0).then_inc(gz, 1)
                        nc.gpsimd.memset(fill[:], NP - 1).then_inc(gz, 1)
                        nc.gpsimd.memset(triu[:], 1.0).then_inc(gz, 1)
                        pool.wait_ge(gz, 7)
                        nc.gpsimd.affine_select(out=triu[:], in_=triu[:], compare_op=ALU.is_ge, fill=0.0,
                                                base=0, pattern=[[1, P]], channel_multiplier=-1).then_inc(gz, 1)
                        pool.wait_ge(filled, 16)

                        def steps(n):
                            pool.wait_ge(staged, n * 2 + 2)
                            pool.sem_inc(passed, 1)
                            for k in range(SB):
                                for b in range(2):
                                    pool.indirect_dma_start(perm_d, bass.IndirectOffsetOnAxis(ap=idx[:, k, b:b + 1], axis=0),
                                                            tok[:, k:k + 1], None, bounds_check=2 * ET * P - 1,
                                                            oob_is_err=False).then_inc(scattered, 16)
                        steps(0)
                        with pool.Fori(1, NT // SB) as i:
                            steps(i)
                        pool.wait_ge(scattered, NT * 32)

                    @block.sync
                    def _(sp):
                        for b, bank in enumerate(("sp", "fq")):
                            sp.dma_start(br[:, b * NE:(b + 1) * NE], a["br_" + bank].partition_broadcast(P)).then_inc(br_in, 16)
                        sp.wait_ge(gz, 8)
                        sp.dma_start(perm_d.rearrange("(p j) a -> p (j a)", p=P), fill[:]).then_inc(filled, 16)
                        for b, bank in enumerate(("sp", "fq")):
                            for e in range(NE):
                                sp.dma_start(w1[:, b * NE + e], a["W1_" + bank][e].rearrange("(k p) f -> p k f", p=P)).then_inc(banks_in, 16)
                                sp.dma_start(w2[:, b * NE + e], a["W2_" + bank][e].rearrange("(k p) o -> p k o", p=P)).then_inc(banks_in, 16)
                            sp.dma_start(b1[:, b * NE:(b + 1) * NE], a["b1_" + bank].partition_broadcast(P)).then_inc(banks_in, 16)
                            sp.dma_start(b2[:, b * NE:(b + 1) * NE], a["b2_" + bank].partition_broadcast(P)).then_inc(banks_in, 16)
                        sp.wait_ge(scattered, NT * 32)
                        sp.dma_start(perm[:], perm_d.rearrange("(j p) a -> p (j a)", p=P)).then_inc(perm_in, 16)
                        sp.wait_ge(perm_in, 16)

                    @block.scalar
                    def _(act):
                        act.wait_ge(e_ready, 1)
                        nc.scalar.activation(ex[:], ex[:], ACT.Exp).then_inc(e_done, 1)

                    @block.tensor
                    def _(pe):
                        pe.wait_ge(gz, 8)
                        pe.wait_ge(g2, 1)
                        for m, w in enumerate(halves):
                            cols = (w.stop - w.start) * B2
                            nc.tensor.matmul(psC[:, m, 0:cols], triu[:], oh[:, w].rearrange("p t e -> p (t e)"), start=True, stop=True)
                            nc.tensor.matmul(psN[:, m, 0:cols], ones[:], oh[:, w].rearrange("p t e -> p (t e)"), start=True, stop=True).then_inc(g3, 1)

                    @block.vector
                    def _(dve):
                        count = [0]

                        def link(ins):
                            count[0] += 1
                            ins.then_inc(g1, 1)
                            dve.wait_ge(g1, count[0])

                        dve.wait_ge(gz, 8)
                        link(nc.vector.tensor_copy(iota8f[:], iota8[:]))
                        link(nc.vector.tensor_copy(far[:], prow[:]))
                        link(nc.vector.tensor_scalar(real[:], far[:], float(LAST), None, ALU.is_lt))
                        link(nc.vector.tensor_scalar(far[:], real[:], -30000.0, 30000.0, ALU.mult, ALU.add))
                        lgb, exb, ohb = lg[:].rearrange(banks, b=2), ex[:].rearrange(banks, b=2), oh[:].rearrange(banks, b=2)
                        dve.wait_ge(br_in, 32)
                        link(nc.vector.tensor_tensor(lg[:], lg[:], br[:].unsqueeze(1).to_broadcast([P, NT, B2]), ALU.add))
                        link(nc.vector.tensor_reduce(mx[:], lgb, AX_X, ALU.max))
                        link(nc.vector.tensor_tensor(ohb, lgb, mx[:].unsqueeze(2).to_broadcast([P, 2 * NT, NE]), ALU.subtract))
                        link(nc.vector.tensor_copy(ex[:], oh[:]))
                        nc.vector.memset(slotf[:], 0.0).then_inc(e_ready, 1)
                        link(nc.vector.tensor_scalar(oh[:], oh[:], 0.0, -float(NE), ALU.is_equal, ALU.mult))
                        link(nc.vector.tensor_tensor(oh[:], oh[:], iota8f[:].unsqueeze(1).to_broadcast([P, NT, B2]), ALU.add))
                        link(nc.vector.tensor_reduce(mx[:], ohb, AX_X, ALU.min))
                        link(nc.vector.tensor_tensor(ohb, ohb, mx[:].unsqueeze(2).to_broadcast([P, 2 * NT, NE]), ALU.is_equal))
                        nc.vector.tensor_scalar(oh[:, NT - 1], oh[:, NT - 1], real[:, 0:1], None, ALU.mult).then_inc(g2, 1)
                        dve.wait_ge(e_done, 1)
                        link(nc.vector.tensor_reduce(gate[:], exb, AX_X, ALU.add))
                        link(nc.vector.reciprocal(gate[:], gate[:]))
                        dve.wait_ge(g3, 2)
                        for m, w in enumerate(halves):
                            cols = (w.stop - w.start) * B2
                            link(nc.vector.tensor_copy(cum[:, w].rearrange("p t e -> p (t e)"), psC[:, m, 0:cols]))
                            link(nc.vector.tensor_copy(tot[:, w].rearrange("p t e -> p (t e)"), psN[:, m, 0:cols]))
                        for k in range(B2):
                            link(nc.vector.tensor_tensor_scan(pre[:, :, k], ones[:, 0:NT], tot[:, :, k], 0.0, ALU.mult, ALU.add))
                        link(nc.vector.tensor_scalar(nt[:], pre[:, NT - 1], float(P - 1), None, ALU.add))
                        link(nc.vector.tensor_tensor(cum[:], cum[:], pre[:], ALU.add))
                        link(nc.vector.scalar_tensor_tensor(cum[:], cum[:], -1.0, tot[:], ALU.add, ALU.subtract))
                        link(nc.vector.tensor_copy(cnt[:], nt[:]))
                        link(nc.vector.tensor_scalar(nti[:], cnt[:], 7, None, ALU.arith_shift_right))
                        link(nc.vector.tensor_copy(nt[:], nti[:]))
                        for b in range(2):
                            link(nc.vector.tensor_tensor_scan(ends[:, b], ones[:, 0:NE], nt[:, b * NE:(b + 1) * NE], 0.0, ALU.mult, ALU.add))
                            link(nc.vector.tensor_tensor(base[:, b * NE:(b + 1) * NE], ends[:, b], nt[:, b * NE:(b + 1) * NE], ALU.subtract))
                            link(nc.vector.tensor_scalar(base[:, b * NE:(b + 1) * NE], base[:, b * NE:(b + 1) * NE], float(P), float(b * ET * P),
                                                         ALU.mult, ALU.add))
                        cumb = cum[:].rearrange(banks, b=2)
                        link(nc.vector.tensor_tensor(tot[:], cum[:], oh[:], ALU.mult))
                        link(nc.vector.tensor_reduce(posf[:], tot[:].rearrange(banks, b=2), AX_X, ALU.add))
                        link(nc.vector.tensor_tensor(cum[:], cum[:], base[:].unsqueeze(1).to_broadcast([P, NT, B2]), ALU.add))
                        link(nc.vector.tensor_tensor(cum[:], cum[:], oh[:], ALU.mult))
                        link(nc.vector.tensor_reduce(slotf[:], cumb, AX_X, ALU.add))
                        link(nc.vector.tensor_copy(slot[:].rearrange("p t b -> p (t b)"), slotf[:]))
                        link(nc.vector.tensor_scalar(slotf[:, 2 * NT - 2:2 * NT], slotf[:, 2 * NT - 2:2 * NT], far[:, 0:1], None, ALU.add))
                        link(nc.vector.tensor_copy(sci[:], slotf[:]))
                        link(nc.vector.scalar_tensor_tensor(gate[:], posf[:], float(CAP), gate[:], ALU.is_lt, ALU.mult))
                        link(nc.vector.tensor_copy(jrowf[:], jrow[:]))
                        for b in range(2):
                            link(nc.vector.tensor_tensor(ecmp[:, b], ends[0:1, b].unsqueeze(1).to_broadcast([1, ET, NE]),
                                                         jrowf[:].unsqueeze(2).to_broadcast([1, ET, NE]), ALU.is_le))
                            link(nc.vector.tensor_reduce(ef[:, b], ecmp[:, b], AX_X, ALU.add))
                            link(nc.vector.tensor_scalar(ef[:, b], ef[:, b], float(NE - 1), float(b * NE), ALU.min, ALU.add))
                        link(nc.vector.tensor_copy(erow[0:1, 4:], ef[:].rearrange("a b j -> a (b j)")))

                        def steps(n):
                            reused(dve, scattered, n * (SB * 32), n)
                            nc.vector.tensor_copy(idx[:].rearrange("p k b -> p (k b)"), sci[:, bass.ds(n * (2 * SB), 2 * SB)]).then_inc(staged, 1)
                            nc.vector.tensor_copy(tok[:], toki[:, bass.ds(n * SB, SB)]).then_inc(staged, 1)
                        steps(0)
                        with dve.Fori(1, NT // SB) as i:
                            steps(i)

        def experts():
            S = 4
            UP, DOWN = 1, 3
            with ExitStack() as c:
                ix = sb(c, "ixH", [P, S], I32)
                xr = sb(c, "xr", [P, S, D])
                xT = sb(c, "xTH", [P, 2, D])
                hp = sb(c, "hp", [P, 2, FF])
                hr = sb(c, "hr", [P, 2, FF])
                hT = sb(c, "hT", [P, 2, FF])
                y = sb(c, "yH", [P, 2, D])
                psT = ps(c, "psTH", [P, 2, D])
                psU = ps(c, "psUH", [P, 2, D])
                psH = ps(c, "psHH", [P, 2, D])
                psD = ps(c, "psDH", [P, 2, D])
                ix_in, x_in, x_turned, xT_ready = sems("ix_inH", S), sems("x_inH", S), sems("x_turnedH", S), sems("xT_readyH", S)
                up_summed, h_biased, h_ready, h_turned = sems("up_summedH", S), sems("h_biased", S), sems("h_readyH", S), sems("h_turned", S)
                hT_ready, down_summed, y_ready, y_stored = sems("hT_readyH", S), sems("down_summedH", S), sems("y_readyH", S), sems("y_storedH", S)
                passed = sem("passedH")

                def experts_of(eng):
                    window = []

                    def load(first, count):
                        return nc.values_load_multi_w_load_instructions(
                            erow[0:1, bass.ds(first, count)], [eng.engine], min_val=0, max_val=2 * NE - 1,
                            skip_runtime_bounds_check_because="a count of ends, held to the bank's experts")[1]

                    def load_round(n, j):
                        if j == 0 and not isinstance(n, int):
                            window[:] = load(n * S, 2 * S)

                    def expert(n, j, lag):
                        if isinstance(n, int):
                            return load(S + n * S + j, 1)[0]
                        return window[S + j] if j + lag < S else window[j]
                    return load_round, expert

                with nc.Block() as block:
                    @block.sync
                    def _(sp):
                        def indices(n, j):
                            reused(sp, x_in[j], n * 16, n)
                            sp.dma_start(ix[:, j:j + 1], perm[:, bass.ds(n * S + j, 1)]).then_inc(ix_in[j], 16)
                        pipeline(sp, S, 2 * ET, [(0, indices)])

                    @block.gpsimd
                    def _(pool):
                        def gather(n, j):
                            pool.wait_ge(ix_in[j], n * 16 + 16)
                            reused(pool, x_turned[j], n, n)
                            pool.sem_inc(passed, 1)
                            pool.indirect_dma_start(xr[:, j], None, xl_d, bass.IndirectOffsetOnAxis(ap=ix[:, j:j + 1], axis=0)
                                                    ).then_inc(x_in[j], 16)
                        pipeline(pool, S, 2 * ET, [(0, gather)])

                    @block.tensor
                    def _(pe):
                        pe.wait_ge(banks_in, 16 * BANK_LOADS)
                        load_round, expert = experts_of(pe)

                        def turn_rows(n, j):
                            pe.wait_ge(x_in[j], n * 16 + 16)
                            earlier(pe, xT_ready, n, j, 2)
                            for k in range(KD):
                                last = nc.tensor.transpose(psT[:, j % 2, k * P:(k + 1) * P], xr[:, j, k * P:(k + 1) * P], ident[:])
                            last.then_inc(x_turned[j], 1)

                        def up(n, j):
                            e = expert(n, j, UP)
                            pe.wait_ge(xT_ready[j], n + 1)
                            earlier(pe, h_biased, n, j, 2)
                            for k in range(KD):
                                last = nc.tensor.matmul(psU[:, j % 2, 0:FF], xT[:, j % 2, k * P:(k + 1) * P], w1[:, e, k],
                                                        start=(k == 0), stop=(k == KD - 1))
                            last.then_inc(up_summed[j], 1)

                        def turn_hidden(n, j):
                            pe.wait_ge(h_ready[j], n + 1)
                            earlier(pe, hT_ready, n, j, 2)
                            for f in range(FF // P):
                                last = nc.tensor.transpose(psH[:, j % 2, f * P:(f + 1) * P], hr[:, j % 2, f * P:(f + 1) * P], ident[:])
                            last.then_inc(h_turned[j], 1)

                        def down(n, j):
                            e = expert(n, j, DOWN)
                            pe.wait_ge(hT_ready[j], n + 1)
                            earlier(pe, y_ready, n, j, 2)
                            for f in range(FF // P):
                                last = nc.tensor.matmul(psD[:, j % 2], hT[:, j % 2, f * P:(f + 1) * P], w2[:, e, f],
                                                        start=(f == 0), stop=(f == FF // P - 1))
                            last.then_inc(down_summed[j], 1)
                        pipeline(pe, S, 2 * ET, [(0, load_round), (0, turn_rows), (DOWN, down), (UP, up), (2, turn_hidden)])

                    @block.scalar
                    def _(act):
                        def copy_rows(n, j):
                            act.wait_ge(x_turned[j], n + 1)
                            earlier(act, up_summed, n, j, 2)
                            nc.scalar.copy(xT[:, j % 2], psT[:, j % 2]).then_inc(xT_ready[j], 1)

                        def gelu(n, j):
                            act.wait_ge(h_biased[j], n + 1)
                            earlier(act, h_turned, n, j, 2)
                            nc.scalar.activation(hr[:, j % 2], hp[:, j % 2], ACT.Gelu).then_inc(h_ready[j], 1)

                        def store(n, j):
                            act.wait_ge(y_ready[j], n + 1)
                            act.dma_start(y_d[bass.ts(n * S + j, P), :], y[:, j % 2]).then_inc(y_stored[j], 16)
                        pipeline(act, S, 2 * ET, [(0, copy_rows), (DOWN, store), (UP, gelu)])
                        for j in range(S):
                            act.wait_ge(y_stored[j], 16 * (2 * ET // S))

                    @block.vector
                    def _(dve):
                        dve.wait_ge(banks_in, 16 * BANK_LOADS)
                        load_round, expert = experts_of(dve)

                        def bias_up(n, j):
                            e = expert(n, j, UP)
                            dve.wait_ge(up_summed[j], n + 1)
                            earlier(dve, h_ready, n, j, 2)
                            nc.vector.tensor_tensor(hp[:, j % 2], psU[:, j % 2, 0:FF], b1[:, e], ALU.add).then_inc(h_biased[j], 1)

                        def copy_hidden(n, j):
                            dve.wait_ge(h_turned[j], n + 1)
                            earlier(dve, down_summed, n, j, 2)
                            nc.vector.tensor_copy(hT[:, j % 2], psH[:, j % 2, 0:FF]).then_inc(hT_ready[j], 1)

                        def bias_down(n, j):
                            e = expert(n, j, DOWN)
                            dve.wait_ge(down_summed[j], n + 1)
                            earlier(dve, y_stored, n, j, 2, each=16)
                            nc.vector.tensor_tensor(y[:, j % 2], psD[:, j % 2], b2[:, e], ALU.add).then_inc(y_ready[j], 1)
                        pipeline(dve, S, 2 * ET, [(0, load_round), (DOWN, bias_down), (UP, bias_up), (2, copy_hidden)])

        def combine():
            S = 6
            with ExitStack() as c:
                ix = sb(c, "ixI", [P, S, 2], I32)
                yb = sb(c, "yb", [P, S, 2, D])
                z = sb(c, "zI", [P, S, D])
                ix_in, y_in, z_in = sems("ix_inI", S), sems("y_inI", S), sems("z_inI", S)
                part, o_ready, stored, passed = sems("partI", S), sems("o_ready", S), sems("storedI", S), sem("passedI")

                with nc.Block() as block:
                    @block.sync
                    def _(sp):
                        def load(n, s):
                            reused(sp, y_in[s], n * 32, n)
                            sp.dma_start(ix[:, s], slot[:, bass.ds(n * S + s, 1)].rearrange("p a b -> p (a b)")).then_inc(ix_in[s], 16)
                            reused(sp, stored[s], n * 16, n)
                            sp.dma_start(z[:, s], z_d[bass.ts(n * S + s, P), :]).then_inc(z_in[s], 16)
                        pipeline(sp, S, NT, [(0, load)])

                    @block.gpsimd
                    def _(pool):
                        def gather(n, s):
                            pool.wait_ge(ix_in[s], n * 16 + 16)
                            reused(pool, o_ready[s], n, n)
                            pool.sem_inc(passed, 1)
                            for b in range(2):
                                pool.indirect_dma_start(yb[:, s, b], None, y_d, bass.IndirectOffsetOnAxis(ap=ix[:, s, b:b + 1], axis=0)
                                                        ).then_inc(y_in[s], 16)
                        pipeline(pool, S, NT, [(0, gather)])

                    @block.vector
                    def _(dve):
                        def add(n, s):
                            dve.wait_ge(z_in[s], n * 16 + 16)
                            dve.wait_ge(y_in[s], n * 32 + 32)
                            first, second = (gate[:, bass.ds((n * S + s) * 2 + b, 1)] for b in range(2))
                            nc.vector.scalar_tensor_tensor(z[:, s], yb[:, s, 0], first, z[:, s], ALU.mult, ALU.add).then_inc(part[s], 1)
                            dve.wait_ge(part[s], n + 1)
                            nc.vector.scalar_tensor_tensor(z[:, s], yb[:, s, 1], second, z[:, s], ALU.mult, ALU.add).then_inc(o_ready[s], 1)
                        pipeline(dve, S, NT, [(0, add)])

                    @block.scalar
                    def _(act):
                        def store(n, s):
                            act.wait_ge(o_ready[s], n + 1)
                            if isinstance(n, int) and n * S + s == NT - 1:
                                act.dma_start(out[(NT - 1) * P:N, :], z[0:LAST, s]).then_inc(stored[s], 16)
                            else:
                                act.dma_start(out[bass.ts(n * S + s, P), :], z[:, s]).then_inc(stored[s], 16)
                        pipeline(act, S, NT, [(0, store)])
                        for s in range(S):
                            act.wait_ge(stored[s], 16 * ((NT - 1 - s) // S + 1))

        phase(constants)
        aN = sb(edges, "aN", [P, NT, 2 * H])
        phase(project_nodes)
        if phases >= 2:
            with ExitStack() as soft:
                dstR = sb(soft, "dstR", [CP, NC, GE])
                dlR = sb(soft, "dlR", [CP, NC, GE])
                tbase = sb(soft, "tbase", [CP, NC])
                with ExitStack() as raw:
                    srcR = sb(raw, "srcR", [CP, NC, GE])
                    hiR = sb(raw, "hiR", [CP, NC, GE])
                    srcRi = sb(raw, "srcRi", [CP, NC, GE], I32)
                    dstRi = sb(raw, "dstRi", [CP, NC, GE], I32)
                    phase(plan_units)
                    phase(rows_to_edges, ((srcR, srcE[:]), (hiR, hiE[:]), (dlR, dlE[:])), "B")
                aR, rest = acc[0:CP, 0:3 * H * NC * GE], acc[0:CP, 3 * H * NC * GE:]
                aR = aR.rearrange("p (j q e) -> p j q e", j=3 * H, q=NC)
                aE = acc[:, 3 * H * NC * GE:3 * H * NC * GE + TU * 3 * H].rearrange("p (t j) -> p t j", t=TU)
                phase(gather_logits)
                phase(edges_to_rows)
                parts = rest[:, 0:12 * NC * GE].rearrange("p (j q e) -> p j q e", j=12, q=NC)
                fwd, bwd, penv, last1, penf, penb = parts[:, 0:H], parts[:, H:2 * H], parts[:, 8], parts[:, 9], parts[:, 10], parts[:, 11]
                phase(edge_softmax)
                phase(rows_to_edges, [(aR[:, h], x9E[:, :, h]) for h in range(2 * H)] + [(last1, x9E[:, :, 8])], "D")
                if scratch != "Internal" and phases == 2:
                    x9_d = dram("x9_d", [P, TU, 9])
                    with nc.Block() as block:
                        @block.sync
                        def _(sp):
                            x9o = sem("x9o")
                            sp.dma_start(x9_d, x9E[:]).then_inc(x9o, 16)
                            sp.wait_ge(x9o, 16)
        if phases >= 3:
            xl_d = dram("xl_d", [NP, D])
            z_d = dram("z_d", [NP, D])
            y_d = dram("y_d", [2 * ET * P, D])
            perm_d = dram("perm_d", [2 * ET * P, 1], I32)
            with sums:
                with edges:
                    acc = acc[:].rearrange("p (t d) -> p t d", d=D)
                    phase(aggregate)
                if scratch != "Internal" and phases == 3:
                    acc_d, accs_d = dram("acc_d", [P, NT, D]), dram("accs_d", [P, NT, 9])
                    with nc.Block() as block:
                        @block.sync
                        def _(sp):
                            x9o = sem("x9o")
                            sp.dma_start(acc_d, acc).then_inc(x9o, 16)
                            sp.dma_start(accs_d, accs[:]).then_inc(x9o, 16)
                            sp.wait_ge(x9o, 32)
                if phases > 3:
                    phase(finish_nodes)
            if phases > 4:
                gate = sb(ctx, "gate", [P, 2 * NT])
                slot = sb(ctx, "slot", [P, NT, 2], I32)
                perm = sb(ctx, "perm", [P, 2 * ET], I32)
                erow = sb(ctx, "erow", [1, 4 + 2 * ET], I32)
                with ExitStack() as weights:
                    w1 = sb(weights, "w1", [P, 2 * NE, KD, FF])
                    w2 = sb(weights, "w2", [P, 2 * NE, FF // P, D])
                    b1 = sb(weights, "b1", [P, 2 * NE, FF])
                    b2 = sb(weights, "b2", [P, 2 * NE, D])
                    banks_in = ctx.enter_context(nc.semaphore("banks_in"))
                    BANK_LOADS = 4 * NE + 4
                    phase(route)
                    phase(experts)
                phase(combine)


_INS = {"x": "x", "src": "src", "dst": "dst", "Wh": "L0_gnn_Wh", "att_src": "L0_gnn_att_src", "att_dst": "L0_gnn_att_dst",
        "bias_h": "L0_gnn_bias_h", "W_out": "L0_gnn_W_out", "b_out": "L0_gnn_b_out", "gamma": "L0_gnn_gamma",
        "beta": "L0_gnn_beta", "Wr_sp": "L0_ffn_Wr_sp", "br_sp": "L0_ffn_br_sp", "Wr_fq": "L0_ffn_Wr_fq",
        "br_fq": "L0_ffn_br_fq", "Ws1": "L0_ffn_Ws1", "bs1": "L0_ffn_bs1", "Ws2": "L0_ffn_Ws2", "bs2": "L0_ffn_bs2",
        "W1_sp": "L0_ffn_W1_sp", "b1_sp": "L0_ffn_b1_sp", "W2_sp": "L0_ffn_W2_sp", "b2_sp": "L0_ffn_b2_sp",
        "W1_fq": "L0_ffn_W1_fq", "b1_fq": "L0_ffn_b1_fq", "W2_fq": "L0_ffn_W2_fq", "b2_fq": "L0_ffn_b2_fq"}
SCRATCH, PHASES = "Internal", 9


def kernel(**inputs):
    import numpy as np
    import concourse.bacc as bacc
    from concourse.bass_utils import run_bass_kernel_spmd as run

    nc = bacc.Bacc("TRN2", target_bir_lowering=False, num_devices=1)
    arrays, aps = {}, {}
    for short, name in _INS.items():
        arrays["in_" + short] = v = np.ascontiguousarray(inputs[name])
        aps[short] = nc.dram_tensor("in_" + short, v.shape, mybir.dt.from_np(v.dtype), kind="ExternalInput").ap()
    out = nc.dram_tensor("out_x", (N, D), F32, kind="ExternalOutput").ap()
    build(nc, aps, out, SCRATCH, PHASES)
    r = run(nc, [arrays], core_ids=[0])
    return r.results[0]["out_x"]
```

```python
from contextlib import ExitStack

import concourse.bass as bass
from concourse import mybir

F32 = mybir.dt.float32
BF16 = mybir.dt.bfloat16
I32 = mybir.dt.int32
ALU = mybir.AluOpType
ACT = mybir.ActivationFunctionType
AX_X = mybir.AxisListType.X

P = 128
N = 6250
D = 512
KD = D // P
H = 4
HD = D // H
E = 106250
NT = (N + P - 1) // P
NP = NT * P
LAST = N - (NT - 1) * P
GE = 256
NG = (E + GE - 1) // GE
PAD = NG * GE - E
U = NG + NT - 1
CP = 116
NC = U // CP
TU = 2 * U
SLOPE = 0.2
EPS = 1e-5
BIG = 1.0e30
FF = 256
NE = 8
CAP = 5120
ET = NT + NE - 1
SUMMED = 40
assert NC * CP == U


def build(nc, a, out, scratch="Internal", phases=9):
    with ExitStack() as ctx:
        ctx.enter_context(nc.allow_non_contiguous_dma(reason="small columns and index rows"))

        def dram(name, shape, dt=F32):
            if scratch == "Internal":
                return nc.dram_tensor(name, shape, dt).ap()
            return nc.dram_tensor("dbg_" + name, shape, dt, kind=scratch).ap()

        held = []

        def sem(name):
            held.append(nc.alloc_semaphore(name))
            return held[-1]

        def phase(run, *args):
            run(*args)
            nc.clear_and_free_semaphores(list(held))
            held.clear()
            nc.all_engine_barrier()

        def sems(name, n):
            return [sem(f"{name}{i}") for i in range(n)]

        def reused(eng, semaphore, value, n):
            if not isinstance(n, int) or n:
                eng.wait_ge(semaphore, value)

        def pipeline(eng, slots, total, stages, loops=()):
            rounds = total // slots

            def step(n, s, more=()):
                for lag, fn in (*stages, *more):
                    if s >= lag:
                        fn(n, s - lag)
                    elif not isinstance(n, int) or n:
                        fn(n - 1, s - lag + slots)

            for n in range(2):
                for s in range(slots):
                    step(n, s)
            first = 2
            for cut, more, at_cut in loops:
                with eng.Fori(first, cut) as i:
                    for s in range(slots):
                        step(i, s, more)
                at_cut()
                first = cut
            if first < rounds:
                with eng.Fori(first, rounds) as i:
                    for s in range(slots):
                        step(i, s)
            for t in range(rounds * slots, total + max(lag for lag, _ in stages)):
                for lag, fn in stages:
                    if t - lag < total:
                        fn((t - lag) // slots, (t - lag) % slots)

        def earlier(eng, semaphores, n, s, back, each=1):
            if s >= back:
                eng.wait_ge(semaphores[s - back], (n + 1) * each)
            elif not isinstance(n, int) or n:
                eng.wait_ge(semaphores[s - back + len(semaphores)], n * each)

        def sb(stack, name, shape, dt=F32):
            return stack.enter_context(nc.sbuf_tensor(name, shape, dt))

        def ps(stack, name, shape, dt=F32):
            return stack.enter_context(nc.psum_tensor(name, shape, dt))

        xp_d = dram("xp_d", [NP, D])
        as_d = dram("as_d", [NP, H])
        src_d = dram("src_d", [NG, GE], I32)
        dst_d = dram("dst_d", [NG, GE], I32)
        tile_d = dram("tile_d", [U], I32)
        dlb_d = dram("dlb_d", [U, GE], BF16)
        lob_d = dram("lob_d", [U, GE], BF16)
        row_d = dram("row_d", [10, U])
        car_d = dram("car_d", [9, U])

        ident = sb(ctx, "ident", [P, P])
        halfneg = sb(ctx, "halfneg", [P, 1])
        lg = sb(ctx, "lg", [P, NT, 2 * NE])
        sums, edges = ExitStack(), ExitStack()
        acc = sb(sums, "acc", [P, NT * D])
        accs = sb(sums, "accs", [P, NT, 9])
        srcE = sb(edges, "srcE", [P, TU], I32)
        dlE = sb(edges, "dlE", [P, TU])
        trow = sb(edges, "trow", [1, U + 8], I32)
        hiE = sb(edges, "hiE", [P, TU])
        trow0 = sb(edges, "trow0", [1, U], I32)
        x9E = sb(edges, "x9E", [P, TU, 9])

        def constants():
            cz, ci = sem("cz"), sem("ci")
            with nc.Block() as block:
                @block.gpsimd
                def _(pool):
                    nc.gpsimd.memset(ident[:], 0.0).then_inc(cz, 1)
                    nc.gpsimd.memset(halfneg[:], -0.5).then_inc(ci, 1)
                    pool.wait_ge(cz, 1)
                    nc.gpsimd.affine_select(out=ident[:], in_=ident[:], compare_op=ALU.not_equal, fill=1.0,
                                            base=0, pattern=[[-1, P]], channel_multiplier=1).then_inc(ci, 1)
                    pool.wait_ge(ci, 2)

        def project_nodes():
            S = 4
            with ExitStack() as c:
                wc = sb(c, "wc", [P, KD, H, HD])
                att = sb(c, "att", [P, 2, H, HD])
                prod = sb(c, "prod", [P, 2, 2, H, HD])
                xin = sb(c, "xin", [P, S, D])
                xl = sb(c, "xl", [P, S, D])
                xT = sb(c, "xT", [P, S, D])
                xp = sb(c, "xp", [P, S, D])
                st = sb(c, "st", [P, S, 6])
                mv = sb(c, "mv", [P, S, 2])
                ve = sb(c, "ve", [P, S, 1])
                rstd = sb(c, "rstd", [P, S, 1])
                psT = ps(c, "psT", [P, 2, D])
                psX = ps(c, "psX", [P, 2, D])
                w_in, att_in, x_zero, passed = sem("w_in"), sem("att_in"), sem("x_zero"), sem("passedA")
                prod_ready, logits_ready = sems("prod_ready", S), sems("node_logits_ready", S)
                x_in, st_ready, mv_ready, ve_ready = sems("x_in", S), sems("st_ready", S), sems("mv_ready", S), sems("ve_ready", S)
                rstd_ready, xl_ready, xlT_ready, xT_ready = sems("rstd_ready", S), sems("xl_ready", S), sems("xlT_ready", S), sems("xT_ready", S)
                proj_ready, xp_ready, stored = sems("proj_ready", S), sems("xp_ready", S), sems("stored", S)

                def is_last(n, j):
                    return isinstance(n, int) and n * S + j == NT - 1

                with nc.Block() as block:
                    @block.sync
                    def _(sp):
                        def weights(n, j):
                            if isinstance(n, int) and n * S + j == 0:
                                for h in range(H):
                                    sp.dma_start(wc[:, :, h], a["Wh"][h].rearrange("(k p) o -> p k o", p=P)).then_inc(w_in, 16)
                                for s, name in ((0, "att_src"), (1, "att_dst")):
                                    sp.dma_start(att[:, s], a[name].partition_broadcast(P)).then_inc(att_in, 16)

                        def load(n, j):
                            if is_last(n, j):
                                sp.wait_ge(x_zero, 1)
                                sp.dma_start(xin[0:LAST, j], a["x"][(NT - 1) * P:N, :]).then_inc(x_in[j], 16)
                            else:
                                reused(sp, xl_ready[j], n, n)
                                sp.dma_start(xin[:, j], a["x"][bass.ts(n * S + j, P), :]).then_inc(x_in[j], 16)
                        pipeline(sp, S, NT, [(0, load), (0, weights)])

                    @block.vector
                    def _(dve):
                        def stats(n, j):
                            if is_last(n, j):
                                dve.wait_ge(xl_ready[j], n)
                                nc.vector.memset(xin[:, j], 0.0).then_inc(x_zero, 1)
                            dve.wait_ge(x_in[j], n * 16 + 16)
                            nc.vector.bn_stats(st[:, j], xin[:, j]).then_inc(st_ready[j], 1)
                            dve.wait_ge(st_ready[j], n + 1)
                            dve.sem_inc(passed, 1)
                            nc.vector.bn_aggr(mv[:, j], st[:, j]).then_inc(mv_ready[j], 1)
                            dve.wait_ge(mv_ready[j], n + 1)
                            nc.vector.tensor_scalar_add(ve[:, j], mv[:, j, 1:2], EPS).then_inc(ve_ready[j], 1)

                        def normalise(n, j):
                            dve.wait_ge(rstd_ready[j], n + 1)
                            reused(dve, xlT_ready[j], n, n)
                            nc.vector.tensor_scalar(xl[:, j], xin[:, j], mv[:, j, 0:1], rstd[:, j, 0:1],
                                                    ALU.subtract, ALU.mult).then_inc(xl_ready[j], 1)

                        def copy_out(n, j):
                            dve.wait_ge(proj_ready[j], n + 1)
                            reused(dve, stored[j], n * 32, n)
                            reused(dve, prod_ready[j], n * 2, n)
                            nc.vector.tensor_copy(xp[:, j], psX[:, j % 2]).then_inc(xp_ready[j], 1)

                        def node_logits(n, j):
                            dve.wait_ge(prod_ready[j], n * 2 + 2)
                            nc.vector.tensor_reduce(aN[:, bass.ds(n * S + j, 1)].rearrange("p a e -> p (a e)"),
                                                    prod[:, j % 2].rearrange("p s h o -> p (s h) o"), AX_X, ALU.add).then_inc(logits_ready[j], 1)
                        pipeline(dve, S, NT, [(0, stats), (1, normalise), (3, copy_out), (4, node_logits)])

                    @block.gpsimd
                    def _(pool):
                        def deviation(n, j):
                            pool.wait_ge(ve_ready[j], n + 1)
                            nc.gpsimd.tensor_tensor(rstd[:, j], ve[:, j], halfneg[:], ALU.pow).then_inc(rstd_ready[j], 1)

                        def multiply(n, j):
                            if isinstance(n, int) and n * S + j == 0:
                                pool.wait_ge(att_in, 32)
                            pool.wait_ge(xp_ready[j], n + 1)
                            earlier(pool, logits_ready, n, j, 2)
                            for s in range(2):
                                nc.gpsimd.tensor_tensor(prod[:, j % 2, s].rearrange("p h o -> p (h o)"), xp[:, j],
                                                        att[:, s].rearrange("p h o -> p (h o)"), ALU.mult).then_inc(prod_ready[j], 1)
                        pipeline(pool, S, NT, [(0, deviation), (3, multiply)])

                    @block.tensor
                    def _(pe):
                        def turn(n, j):
                            pe.wait_ge(xl_ready[j], n + 1)
                            earlier(pe, xT_ready, n, j, 2)
                            for k in range(KD):
                                last = nc.tensor.transpose(psT[:, j % 2, k * P:(k + 1) * P], xl[:, j, k * P:(k + 1) * P], ident[:])
                            last.then_inc(xlT_ready[j], 1)

                        def project(n, j):
                            if isinstance(n, int) and n * S + j == 0:
                                pe.wait_ge(w_in, 16 * H)
                            pe.wait_ge(xT_ready[j], n + 1)
                            earlier(pe, xp_ready, n, j, 2)
                            for k in range(KD):
                                last = nc.tensor.matmul(psX[:, j % 2], xT[:, j, k * P:(k + 1) * P], wc[:, k].rearrange("p h o -> p (h o)"),
                                                        start=(k == 0), stop=(k == KD - 1))
                            last.then_inc(proj_ready[j], 1)
                        pipeline(pe, S, NT, [(0, turn), (1, project)])

                    @block.scalar
                    def _(act):
                        def copy_turned(n, j):
                            act.wait_ge(xlT_ready[j], n + 1)
                            reused(act, proj_ready[j], n, n)
                            nc.scalar.copy(xT[:, j], psT[:, j % 2]).then_inc(xT_ready[j], 1)

                        def store(n, j):
                            row = bass.ts(n * S + j, P)
                            act.wait_ge(xp_ready[j], n + 1)
                            act.dma_start(xp_d[row, :], xp[:, j]).then_inc(stored[j], 16)
                            act.wait_ge(logits_ready[j], n + 1)
                            act.dma_start(as_d[row, :], aN[:, bass.ds(n * S + j, 1), 0:H].rearrange("p a e -> p (a e)")).then_inc(stored[j], 16)
                        pipeline(act, S, NT, [(0, copy_turned), (4, store)])
                        for j in range(S):
                            act.wait_ge(stored[j], ((NT - 1 - j) // S + 1) * 32)

        def plan_units():
            with ExitStack() as c:
                padv = sb(c, "padv", [1, 2, PAD], I32)
                hi = sb(c, "hi", [1, NG], I32)
                hs = sb(c, "hs", [1, NG], I32)
                gi = sb(c, "gi", [1, NG], I32)
                gf = sb(c, "gf", [1, 2, NG])
                key1 = sb(c, "key1", [1, NG])
                key = sb(c, "key", [P, NG])
                lt = sb(c, "lt", [CP, NC, NG])
                ui = sb(c, "ui", [CP, NC], I32)
                uf = sb(c, "uf", [CP, NC])
                gu = sb(c, "gu", [CP, NC])
                tu = sb(c, "tu", [CP, NC])
                ti = sb(c, "ti", [CP, NC], I32)
                gc = sb(c, "gc", [CP, NC], I32)
                pad_set, edges_in, hi_in, iotas = sem("pad_set"), sem("edges_in"), sem("hi_in"), sem("iotas")
                rows_b, rows_out, lo_steps = sem("rows_b"), sem("rows_outB"), sem("lo_steps")
                loR = sb(c, "loR", [CP, NC, GE], I32)
                loRb = sb(c, "loRb", [CP, NC, GE], BF16)
                dlRb = sb(c, "dlRb", [CP, NC, GE], BF16)
                b1, key_b, gidx, rows_in, rows_f, tile_out, tile_in = (
                    sem("b1"), sem("key_b"), sem("gidx"), sem("rows_in"), sem("rows_f"), sem("tile_out"), sem("tile_in"))

                with nc.Block() as block:
                    @block.sync
                    def _(sp):
                        for k, (to, name) in enumerate(((src_d, "src"), (dst_d, "dst"))):
                            flat = to.rearrange("g e -> (g e)")
                            sp.dma_start(flat[0:E], a[name]).then_inc(edges_in, 16)
                        sp.wait_ge(pad_set, 2)
                        for k, to in enumerate((src_d, dst_d)):
                            flat = to.rearrange("g e -> (g e)")
                            sp.dma_start(flat[E:NG * GE].rearrange("(a e) -> a e", a=1), padv[:, k]).then_inc(edges_in, 16)
                        sp.wait_ge(edges_in, 64)
                        sp.dma_start(hi[:], dst_d[:, GE - 1:GE].rearrange("g e -> e g")).then_inc(hi_in, 16)
                        sp.wait_ge(gidx, 1)
                        sp.dma_start(tile_d.rearrange("(c p) -> p c", p=CP), ti[:]).then_inc(tile_out, 16)
                        sp.wait_ge(tile_out, 16)
                        sp.dma_start(trow[0:1, 3:3 + U], tile_d.rearrange("(a u) -> a u", a=1)).then_inc(tile_in, 16)
                        sp.dma_start(trow0[:], tile_d.rearrange("(a u) -> a u", a=1)).then_inc(tile_in, 16)
                        sp.wait_ge(tile_in, 32)
                        sp.wait_ge(rows_b, 2)
                        for q in range(NC):
                            units = slice(q * CP, (q + 1) * CP)
                            sp.dma_start(dlb_d[units, :], dlRb[:, q]).then_inc(rows_out, 16)
                            sp.dma_start(lob_d[units, :], loRb[:, q]).then_inc(rows_out, 16)
                        sp.wait_ge(rows_out, 32 * NC)

                    @block.gpsimd
                    def _(pool):
                        nc.gpsimd.memset(padv[:, 0], 0).then_inc(pad_set, 1)
                        nc.gpsimd.memset(padv[:, 1], NP - 1).then_inc(pad_set, 1)
                        nc.gpsimd.iota(gi[:], [[1, NG]], base=0, channel_multiplier=0).then_inc(iotas, 1)
                        nc.gpsimd.iota(ui[:], [[CP, NC]], base=0, channel_multiplier=1).then_inc(iotas, 1)
                        pool.wait_ge(b1, 4)
                        nc.gpsimd.partition_broadcast(key[:], key1[:], P).then_inc(key_b, 1)
                        pool.wait_ge(gidx, 2)
                        for k, (rows, table) in enumerate(((srcRi, src_d), (dstRi, dst_d))):
                            for q in range(NC):
                                pool.indirect_dma_start(rows[:, q, :], None, table, bass.IndirectOffsetOnAxis(ap=gc[:, q:q + 1], axis=0)
                                                        ).then_inc(rows_in, 16)
                        pool.wait_ge(rows_in, 32 * NC)

                    @block.vector
                    def _(dve):
                        dve.wait_ge(hi_in, 16)
                        dve.wait_ge(iotas, 2)
                        nc.vector.tensor_scalar(hs[:], hi[:], 7, None, ALU.arith_shift_right).then_inc(b1, 1)
                        nc.vector.tensor_copy(gf[:, 1], gi[:]).then_inc(b1, 1)
                        dve.wait_ge(b1, 2)
                        nc.vector.tensor_copy(gf[:, 0], hs[:]).then_inc(b1, 1)
                        nc.vector.tensor_copy(uf[:], ui[:])
                        dve.wait_ge(b1, 3)
                        nc.vector.tensor_tensor(key1[:], gf[:, 0], gf[:, 1], ALU.add).then_inc(b1, 1)
                        dve.wait_ge(key_b, 1)
                        for q in range(NC):
                            nc.vector.tensor_scalar(lt[:, q], key[0:CP], uf[:, q:q + 1], None, ALU.is_lt).then_inc(b1, 1)
                        dve.wait_ge(b1, 4 + NC)
                        nc.vector.tensor_reduce(gu[:], lt[:], AX_X, ALU.add).then_inc(b1, 1)
                        dve.wait_ge(b1, 5 + NC)
                        nc.vector.tensor_tensor(tu[:], uf[:], gu[:], ALU.subtract).then_inc(b1, 1)
                        dve.wait_ge(b1, 6 + NC)
                        nc.vector.tensor_copy(ti[:], tu[:]).then_inc(gidx, 1)
                        nc.vector.tensor_scalar(gc[:], gu[:], float(NG - 1), None, ALU.min).then_inc(gidx, 1)
                        nc.vector.tensor_scalar(tbase[:], tu[:], float(P), None, ALU.mult).then_inc(b1, 1)
                        dve.wait_ge(b1, 7 + NC)
                        dve.wait_ge(rows_in, 32 * NC)
                        nc.vector.tensor_copy(srcR[:], srcRi[:]).then_inc(rows_f, 1)
                        nc.vector.tensor_copy(dstR[:], dstRi[:]).then_inc(rows_f, 1)
                        dve.wait_ge(rows_f, 2)
                        for q in range(NC):
                            nc.vector.tensor_scalar(dlR[:, q], dstR[:, q], tbase[:, q:q + 1], None, ALU.subtract).then_inc(rows_f, 1)
                        dve.wait_ge(rows_f, 2 + NC)
                        nc.vector.tensor_copy(dlRb[:], dlR[:]).then_inc(rows_b, 1)
                        nc.vector.tensor_scalar(loR[:], srcRi[:], P - 1, None, ALU.bitwise_and).then_inc(lo_steps, 1)
                        dve.wait_ge(lo_steps, 1)
                        nc.vector.tensor_copy(loRb[:], loR[:]).then_inc(rows_b, 1)
                        dve.wait_ge(rows_b, 2)
                        nc.vector.tensor_scalar(loR[:], srcRi[:], 7, None, ALU.arith_shift_right).then_inc(lo_steps, 1)
                        dve.wait_ge(lo_steps, 2)
                        nc.vector.tensor_copy(hiR[:], loR[:]).then_inc(lo_steps, 1)
                        dve.wait_ge(lo_steps, 3)

        def rows_to_edges(pairs, tag, zero=()):
            with ExitStack() as c:
                pt = ps(c, "pt" + tag, [P, 2, D])
                turned, copied = sem("turned" + tag), sem("copied" + tag)
                zeroed, zcol = sem("zeroed" + tag), sb(c, "zcol" + tag, [P, 1])
                jobs = [(rows, to, k) for rows, to in pairs for k in range(2)]
                with nc.Block() as block:
                    if zero:
                        @block.gpsimd
                        def _(pool):
                            nc.gpsimd.memset(zcol[:], 0.0).then_inc(zeroed, 1)
                            nc.gpsimd.memset(zero[0], 0.0).then_inc(zeroed, 1)

                        @block.scalar
                        def _(act):
                            act.wait_ge(zeroed, 1)
                            for to in zero[1:]:
                                nc.scalar.copy(to, zcol[:].to_broadcast([P, to.shape[1]])).then_inc(zeroed, 1)

                    @block.tensor
                    def _(pe):
                        for n, (rows, to, k) in enumerate(jobs):
                            if n >= 2:
                                pe.wait_ge(copied, n - 1)
                            for q in range(NC):
                                last = nc.tensor.transpose(pt[:, n % 2, q * CP:(q + 1) * CP], rows[:, q, k * P:(k + 1) * P],
                                                           ident[0:CP, 0:CP])
                            last.then_inc(turned, 1)

                    @block.vector
                    def _(dve):
                        for n, (rows, to, k) in enumerate(jobs):
                            dve.wait_ge(turned, n + 1)
                            nc.vector.tensor_copy(to.rearrange("p (u k) -> p k u", k=2)[:, k], pt[:, n % 2, 0:U]).then_inc(copied, 1)
                        dve.wait_ge(copied, len(jobs))

        def gather_logits():
            S, CU = 2, 8
            CT, VT = 2 * CU, 10
            CHUNKS = U // CU
            W = NT * H
            with ExitStack() as c:
                t3 = sb(c, "t3", [P, NT, 3, 2 * H], BF16)
                left = sb(c, "left", [P, 2, NT, 2 * H])
                pidx = sb(c, "pidx", [P, 1], I32)
                pcol = sb(c, "pcol", [P, 1])
                nepcol = sb(c, "nepcol", [P, 1])
                hidx = sb(c, "hidx", [P, NT, H], I32)
                hrow = sb(c, "hrow", [P, W])
                dlb = sb(c, "dlb", [P, S, CT * P], BF16)
                lob = sb(c, "lob", [P, S, VT * P], BF16)
                dstT = sb(c, "dstT", [P, S, CT * P], BF16)
                loT = sb(c, "loT", [P, S, VT * P], BF16)
                sel = sb(c, "sel", [P, VT, NT, H])
                ix = sb(c, "ixC", [P, S, CT - VT], I32)
                gs = sb(c, "gs", [P, S, CT - VT, H])
                psV = ps(c, "psV", [P, VT // 2, D])
                psW = ps(c, "psW", [P, S, D])
                iotas, prep, table_ready = sem("iotasC"), sem("prepC"), sem("table_ready")
                rows_in, ix_in, onehots = sems("rows_inC", S), sems("ix_inC", S), sems("onehots", S)
                dst_rows_in, dst_onehots, column_ready = sems("dst_rows_in", S), sems("dst_onehots", S), sem("column_ready")
                picked, selected, dst_picked, dst_kept = sems("picked", VT // 2), sems("selected", VT // 2), sems("dst_picked", S), sems("dst_kept", S)
                sel_read, gathered, kept, passed = sem("sel_read"), sems("gathered", S), sems("kept", S), sem("passedC")

                with nc.Block() as block:
                    @block.sync
                    def _(sp):
                        def load(n, s):
                            reused(sp, dst_onehots[s], n * 2, n)
                            units = bass.ds((n * S + s) * CU, CU)
                            sp.dma_start(dlb[:, s], dlb_d[units, :].rearrange("u e -> (u e)").partition_broadcast(P)).then_inc(dst_rows_in[s], 16)
                            units = bass.ds((n * S + s) * CU, VT // 2)
                            sp.dma_start(lob[:, s], lob_d[units, :].rearrange("u e -> (u e)").partition_broadcast(P)).then_inc(rows_in[s], 16)
                            reused(sp, gathered[s], n * (16 * (CT - VT)), n)
                            sp.dma_start(ix[:, s], srcE[:, bass.ds((n * S + s) * CT + VT, CT - VT)]).then_inc(ix_in[s], 16)
                        pipeline(sp, S, CHUNKS, [(0, load)])

                    @block.gpsimd
                    def _(pool):
                        nc.gpsimd.iota(pidx[:], [[0, 1]], base=0, channel_multiplier=1).then_inc(iotas, 1)
                        nc.gpsimd.iota(hidx[:], [[1, NT], [0, H]], base=0, channel_multiplier=0).then_inc(iotas, 1)

                        def gather(n, s):
                            pool.wait_ge(ix_in[s], n * 16 + 16)
                            reused(pool, kept[s], n, n)
                            pool.sem_inc(passed, 1)
                            for k in range(CT - VT):
                                pool.indirect_dma_start(gs[:, s, k], None, as_d, bass.IndirectOffsetOnAxis(ap=ix[:, s, k:k + 1], axis=0)
                                                        ).then_inc(gathered[s], 16)
                        pipeline(pool, S, CHUNKS, [(0, gather)])

                    @block.vector
                    def _(dve):
                        count = [0]

                        def link(ins):
                            count[0] += 1
                            ins.then_inc(prep, 1)
                            dve.wait_ge(prep, count[0])

                        dve.wait_ge(iotas, 2)
                        link(nc.vector.tensor_copy(pcol[:], pidx[:]))
                        nc.vector.tensor_scalar_mul(nepcol[:], pcol[:], -1.0).then_inc(column_ready, 1)
                        link(nc.vector.tensor_copy(hrow[:], hidx[:].rearrange("p t h -> p (t h)")))
                        link(nc.vector.tensor_copy(t3[:, :, 0], aN[:]))
                        link(nc.vector.tensor_tensor(left[:, 0], aN[:], t3[:, :, 0], ALU.subtract))
                        link(nc.vector.tensor_copy(t3[:, :, 1], left[:, 0]))
                        link(nc.vector.tensor_tensor(left[:, 1], left[:, 0], t3[:, :, 1], ALU.subtract))
                        nc.vector.tensor_copy(t3[:, :, 2], left[:, 1]).then_inc(table_ready, 1)

                        def select(n, s):
                            chunk = n * S + s
                            if not (isinstance(chunk, int) and chunk == 0):
                                dve.wait_ge(sel_read, chunk)
                            for v in range(VT):
                                if v % 2 == 0:
                                    dve.wait_ge(picked[v // 2], chunk + 1)
                                nc.vector.scalar_tensor_tensor(sel[:, v].rearrange("p t h -> p (t h)"), hrow[:], hiE[:, bass.ds(chunk * CT + v, 1)],
                                                               psV[:, v // 2, (v % 2) * W:(v % 2 + 1) * W], ALU.is_equal, ALU.mult
                                                               ).then_inc(selected[v // 2], 1)
                            for m in range(VT // 2):
                                dve.wait_ge(selected[m], chunk * 2 + 2)
                            nc.vector.tensor_reduce(aE[:, bass.ds(chunk * CT, VT), 0:H], sel[:].rearrange("p v t h -> p v h t"), AX_X,
                                                    ALU.add).then_inc(sel_read, 1)
                            dve.wait_ge(dst_picked[s], n + 1)
                            nc.vector.tensor_reduce(aE[:, bass.ds(chunk * CT, CT), H:3 * H],
                                                    psW[:, s, 0:CT * 6 * H].rearrange("p (k s a) -> p k a s", k=CT, s=3), AX_X, ALU.add
                                                    ).then_inc(dst_kept[s], 1)
                        pipeline(dve, S, CHUNKS, [(0, select)])
                        dve.wait_ge(sel_read, CHUNKS)
                        for s in range(S):
                            dve.wait_ge(dst_kept[s], CHUNKS // S)

                    @block.tensor
                    def _(pe):
                        pe.wait_ge(table_ready, 1)

                        def pick(n, s):
                            chunk = n * S + s
                            slots = nc.values_load_multi_w_load_instructions(
                                trow0[0:1, bass.ds(chunk * CU, CU)], [pe.engine], min_val=0, max_val=NT - 1,
                                skip_runtime_bounds_check_because="a unit's tile is its index less its group, within 0..NT-1")[1]
                            pe.wait_ge(onehots[s], n * 2 + 2)
                            for v in range(VT):
                                if v % 2 == 0 and not (isinstance(chunk, int) and chunk == 0):
                                    pe.wait_ge(selected[v // 2], chunk * 2)
                                for part in range(3):
                                    last = nc.tensor.matmul(psV[:, v // 2, (v % 2) * W:(v % 2 + 1) * W], loT[:, s, v * P:(v + 1) * P],
                                                            t3[:, :, part, 0:H], start=(part == 0), stop=(part == 2))
                                if v % 2:
                                    last.then_inc(picked[v // 2], 1)
                            reused(pe, dst_kept[s], n, n)
                            pe.wait_ge(dst_onehots[s], n * 2 + 2)
                            for k in range(CT):
                                last = nc.tensor.matmul(psW[:, s, k * 6 * H:(k + 1) * 6 * H], dstT[:, s, k * P:(k + 1) * P],
                                                        t3[:, slots[k // 2]].rearrange("p s a -> p (s a)"), start=True, stop=True)
                            last.then_inc(dst_picked[s], 1)
                        pipeline(pe, S, CHUNKS, [(0, pick)])

                    @block.scalar
                    def _(act):
                        act.wait_ge(column_ready, 1)

                        def onehot(n, s):
                            reused(act, dst_picked[s], n, n)
                            act.wait_ge(rows_in[s], n * 16 + 16)
                            nc.scalar.activation(loT[:, s], lob[:, s], ACT.Abs, bias=nepcol[:, 0:1]).then_inc(onehots[s], 1)
                            act.wait_ge(onehots[s], n * 2 + 1)
                            nc.scalar.activation(loT[:, s], loT[:, s], ACT.Relu, bias=1.0, scale=-1.0).then_inc(onehots[s], 1)
                            act.wait_ge(dst_rows_in[s], n * 16 + 16)
                            nc.scalar.activation(dstT[:, s], dlb[:, s], ACT.Abs, bias=nepcol[:, 0:1]).then_inc(dst_onehots[s], 1)
                            act.wait_ge(dst_onehots[s], n * 2 + 1)
                            nc.scalar.activation(dstT[:, s], dstT[:, s], ACT.Relu, bias=1.0, scale=-1.0).then_inc(dst_onehots[s], 1)

                        def keep(n, s):
                            act.wait_ge(gathered[s], n * (16 * (CT - VT)) + 16 * (CT - VT))
                            nc.scalar.copy(aE[:, bass.ds((n * S + s) * CT + VT, CT - VT), 0:H], gs[:, s]).then_inc(kept[s], 1)
                        pipeline(act, S, CHUNKS, [(0, onehot), (1, keep)])
                        for s in range(S):
                            act.wait_ge(kept[s], CHUNKS // S)

        def edges_to_rows():
            with ExitStack() as c:
                pt = ps(c, "ptC", [CP, 2, NC, P])
                turned, copied = sem("turnedC"), sem("copiedC")
                jobs = [(j, k) for j in range(3 * H) for k in range(2)]
                columns = aE.rearrange("p (q u k) j -> p q k j u", q=NC, k=2)
                with nc.Block() as block:
                    @block.tensor
                    def _(pe):
                        for n, (j, k) in enumerate(jobs):
                            if n >= 2:
                                pe.wait_ge(copied, n - 1)
                            for q in range(NC):
                                last = nc.tensor.transpose(pt[:, n % 2, q], columns[:, q, k, j], ident[:])
                            last.then_inc(turned, 1)

                    @block.vector
                    def _(dve):
                        for n, (j, k) in enumerate(jobs):
                            dve.wait_ge(turned, n + 1)
                            nc.vector.tensor_copy(aR[:, j, :, k * P:(k + 1) * P], pt[:, n % 2]).then_inc(copied, 1)
                        dve.wait_ge(copied, len(jobs))

        def edge_softmax():
            with ExitStack() as c:
                sm = sb(c, "sm", [CP, 10, NC])
                car = sb(c, "car", [CP, 9, NC])
                rl = sb(c, "rl", [H, 2, U])
                rd = sb(c, "rd", [H, 2, U])
                cont = sb(c, "cont", [H, U + 1])
                full = sb(c, "full", [H, U])
                pen2 = sb(c, "pen2", [H, 2, U])
                penc = sb(c, "penc", [H, U + 1])
                run2 = sb(c, "run2", [H, 2, U + 1])
                carry = sb(c, "carry", [H, 2, U])
                d1, rows_out, rows_back, car_out, car_back = (sem("d1"), sem("rows_out"), sem("rows_back"),
                                                              sem("car_out"), sem("car_back"))
                small_ready, carry_ready, logits_ready, exp_ready = sem("small_ready"), sem("carry_ready"), sem("logits_ready"), sem("exp_ready")
                self_summed = sem("self_summed")
                asv, aself, adst = aR[:, 0:H], aR[:, H:2 * H], aR[:, 2 * H:3 * H]

                with nc.Block() as block:
                    @block.gpsimd
                    def _(pool):
                        for h in range(H):
                            nc.gpsimd.tensor_tensor(aself[:, h], aself[:, h], adst[:, h], ALU.add).then_inc(self_summed, 1)

                    @block.vector
                    def _(dve):
                        count = [0]

                        def link(ins):
                            count[0] += 1
                            ins.then_inc(d1, 1)
                            dve.wait_ge(d1, count[0])

                        def flat(ap):
                            return ap.rearrange("p q e -> p (q e)")

                        link(nc.vector.tensor_scalar(penv, dlR[:], 0.0, None, ALU.is_ge))
                        link(nc.vector.scalar_tensor_tensor(penf, dlR[:], float(P), penv, ALU.is_lt, ALU.mult))
                        link(nc.vector.tensor_scalar(penv, penf, -1.0, BIG, ALU.add, ALU.mult))
                        for h in range(H):
                            link(nc.vector.tensor_tensor(asv[:, h], asv[:, h], adst[:, h], ALU.add))
                            link(nc.vector.scalar_tensor_tensor(asv[:, h], asv[:, h], SLOPE, asv[:, h], ALU.mult, ALU.max))
                            link(nc.vector.tensor_tensor(asv[:, h], asv[:, h], penv, ALU.add))
                        link(nc.vector.memset(last1[:, :, GE - 1:GE], 1.0))
                        link(nc.vector.tensor_tensor(last1[:, :, 0:GE - 1], dstR[:, :, 1:GE], dstR[:, :, 0:GE - 1], ALU.not_equal))
                        link(nc.vector.tensor_scalar(penb, last1, -BIG, None, ALU.mult))
                        link(nc.vector.memset(penf[:, :, 0:1], -BIG))
                        link(nc.vector.tensor_copy(penf[:, :, 1:GE], penb[:, :, 0:GE - 1]))
                        for h in range(H):
                            link(nc.vector.tensor_tensor_scan(flat(fwd[:, h]), flat(penf), flat(asv[:, h]), 0.0, ALU.add, ALU.max))
                            link(nc.vector.tensor_tensor_scan(flat(bwd[:, h])[:, ::-1], flat(penb)[:, ::-1],
                                                              flat(asv[:, h])[:, ::-1], 0.0, ALU.add, ALU.max))
                        link(nc.vector.tensor_copy(sm[:, 0:H], fwd[:, :, :, GE - 1]))
                        link(nc.vector.tensor_copy(sm[:, H:2 * H], bwd[:, :, :, 0]))
                        link(nc.vector.tensor_copy(sm[:, 8], dstR[:, :, 0]))
                        nc.vector.tensor_copy(sm[:, 9], dstR[:, :, GE - 1]).then_inc(small_ready, 1)
                        dve.wait_ge(small_ready, 1)
                        for q in range(NC):
                            link(nc.vector.tensor_scalar(penf[:, q], dstR[:, q], sm[:, 8, q:q + 1], -BIG, ALU.not_equal, ALU.mult))
                            link(nc.vector.tensor_scalar(penb[:, q], dstR[:, q], sm[:, 9, q:q + 1], -BIG, ALU.not_equal, ALU.mult))
                        for h in range(H):
                            link(nc.vector.tensor_tensor(fwd[:, h], fwd[:, h], bwd[:, h], ALU.max))
                        dve.wait_ge(rows_back, 64)
                        link(nc.vector.memset(cont[:], 0.0))
                        link(nc.vector.tensor_tensor(cont[:, 1:U], rd[:, 0, 1:U], rd[:, 1, 0:U - 1], ALU.is_equal))
                        link(nc.vector.tensor_tensor(full[:], rd[:, 0], rd[:, 1], ALU.is_equal))
                        link(nc.vector.tensor_tensor(pen2[:, 0], full[:], cont[:, 0:U], ALU.mult))
                        link(nc.vector.tensor_tensor(pen2[:, 1], full[:], cont[:, 1:U + 1], ALU.mult))
                        link(nc.vector.tensor_scalar(pen2[:], pen2[:], -1.0, BIG, ALU.add, ALU.mult))
                        link(nc.vector.tensor_scalar(penc[:], cont[:], -1.0, BIG, ALU.add, ALU.mult))
                        link(nc.vector.memset(run2[:], 0.0))
                        link(nc.vector.tensor_tensor_scan(run2[:, 0, 1:U + 1], pen2[:, 0], rl[:, 0], -BIG, ALU.add, ALU.max))
                        link(nc.vector.tensor_tensor_scan(run2[:, 1, 0:U][:, ::-1], pen2[:, 1][:, ::-1], rl[:, 1][:, ::-1],
                                                          -BIG, ALU.add, ALU.max))
                        link(nc.vector.tensor_tensor(carry[:, 0], run2[:, 0, 0:U], penc[:, 0:U], ALU.add))
                        nc.vector.tensor_tensor(carry[:, 1], run2[:, 1, 1:U + 1], penc[:, 1:U + 1], ALU.add).then_inc(carry_ready, 1)
                        dve.wait_ge(self_summed, H)
                        for h in range(H):
                            link(nc.vector.scalar_tensor_tensor(aself[:, h], aself[:, h], SLOPE, aself[:, h], ALU.mult, ALU.max))
                        dve.wait_ge(car_back, 16 * (2 * NC + 1))
                        for h in range(H):
                            for q in range(NC):
                                link(nc.vector.scalar_tensor_tensor(fwd[:, h, q], penf[:, q], car[:, h, q:q + 1], fwd[:, h, q], ALU.add, ALU.max))
                                link(nc.vector.scalar_tensor_tensor(fwd[:, h, q], penb[:, q], car[:, H + h, q:q + 1], fwd[:, h, q], ALU.add, ALU.max))
                        link(nc.vector.tensor_scalar(last1[:, :, GE - 1], car[:, 8], -1.0, 1.0, ALU.mult, ALU.add))
                        for h in range(H):
                            link(nc.vector.tensor_tensor(fwd[:, h], fwd[:, h], aself[:, h], ALU.max))
                            for part in (asv, aself):
                                nc.vector.tensor_tensor(part[:, h], part[:, h], fwd[:, h], ALU.subtract).then_inc(logits_ready, 1)
                        for h in range(H):
                            dve.wait_ge(exp_ready, 2 * h + 2)
                            link(nc.vector.tensor_tensor(aself[:, h], aself[:, h], last1, ALU.mult))

                    @block.scalar
                    def _(act):
                        for h in range(H):
                            act.wait_ge(logits_ready, 2 * h + 2)
                            for part in (asv, aself):
                                nc.scalar.activation(part[:, h], part[:, h], ACT.Exp).then_inc(exp_ready, 1)
                        act.wait_ge(exp_ready, 2 * H)

                    @block.sync
                    def _(sp):
                        sp.wait_ge(small_ready, 1)
                        for q in range(NC):
                            sp.dma_start(row_d[:, q * CP:(q + 1) * CP].rearrange("j p -> p j"), sm[:, :, q]).then_inc(rows_out, 16)
                        sp.wait_ge(rows_out, 16 * NC)
                        sp.dma_start(rl[:, 0], row_d[0:H]).then_inc(rows_back, 16)
                        sp.dma_start(rl[:, 1], row_d[H:2 * H]).then_inc(rows_back, 16)
                        sp.dma_start(rd[:, 0], row_d[8].partition_broadcast(H)).then_inc(rows_back, 16)
                        sp.dma_start(rd[:, 1], row_d[9].partition_broadcast(H)).then_inc(rows_back, 16)
                        sp.wait_ge(carry_ready, 1)
                        for k in range(2):
                            sp.dma_start(car_d[k * H:(k + 1) * H], carry[:, k]).then_inc(car_out, 16)
                        sp.dma_start(car_d[8:9], cont[0:1, 1:U + 1]).then_inc(car_out, 16)
                        sp.wait_ge(car_out, 48)
                        for q in range(NC):
                            cols = slice(q * CP, (q + 1) * CP)
                            for k in range(2):
                                sp.dma_start(car[:, k * H:(k + 1) * H, q], car_d[k * H:(k + 1) * H, cols].rearrange("j p -> p j")).then_inc(car_back, 16)
                        sp.dma_start(car[:, 8], car_d[8].rearrange("(q p) -> p q", p=CP)).then_inc(car_back, 16)
                        sp.wait_ge(car_back, 16 * (2 * NC + 1))

        def aggregate():
            S, LAG = 8, 3
            UT = 2
            with ExitStack() as c:
                ix = sb(c, "ix", [P, S, UT], I32)
                g = sb(c, "g", [P, S, UT, H, HD])
                x9 = sb(c, "x9", [P, S, UT, 9])
                dl = sb(c, "dl", [P, S, UT])
                onehot = sb(c, "onehot", [P, S, UT, P])
                nodei = sb(c, "nodei", [P, P], I32)
                nodef = sb(c, "nodef", [P, P])
                psO = ps(c, "psO", [P, 4, D])
                psS = ps(c, "psS", [P, 4, D])
                acc_zero, node_iota, node_row, passed = sem("acc_zero"), sem("node_iota"), sem("node_row"), sem("passedE")
                ix_in, g_in = sems("ix_in", S), sems("g_in", S * UT)
                weights_in, onehot_ready = sems("weights_in", S), sems("onehot_ready", S)
                scaled_act, scaled_dve, summed, added = sems("scaled_act", S), sems("scaled_dve", S), sems("summed", S), sems("added", S)

                def tiles(n, s):
                    return bass.ds(n * (S * UT) + s * UT, UT)

                with nc.Block() as block:
                    @block.sync
                    def _(sp):
                        def indices(n, s):
                            for k in range(UT):
                                reused(sp, g_in[s * UT + k], n * 16, n)
                            sp.dma_start(ix[:, s], srcE[:, tiles(n, s)]).then_inc(ix_in[s], 16)
                        pipeline(sp, S, U, [(0, indices)])

                    @block.gpsimd
                    def _(pool):
                        nc.gpsimd.iota(nodei[:], [[1, P]], base=0, channel_multiplier=0).then_inc(node_iota, 1)

                        def gather(n, s):
                            pool.wait_ge(ix_in[s], n * 16 + 16)
                            reused(pool, summed[s], n, n)
                            pool.sem_inc(passed, 1)
                            for k in range(UT):
                                pool.indirect_dma_start(g[:, s, k].rearrange("p h o -> p (h o)"), None, xp_d,
                                                        bass.IndirectOffsetOnAxis(ap=ix[:, s, k:k + 1], axis=0)
                                                        ).then_inc(g_in[s * UT + k], 16)
                        pipeline(pool, S, U, [(0, gather)])

                    @block.vector
                    def _(dve):
                        nc.vector.memset(accs[:], 0.0).then_inc(acc_zero, 1)
                        nc.vector.memset(acc[:, 0:1], 0.0).then_inc(acc_zero, 1)
                        dve.wait_ge(node_iota, 1)
                        nc.vector.tensor_copy(nodef[:], nodei[:]).then_inc(node_row, 1)
                        dve.wait_ge(node_row, 1)
                        dve.wait_ge(acc_zero, 2)
                        assert KEPT[0] <= 2 * S
                        def zero(n, s):
                            if isinstance(n, int) and n < 2:
                                u = n * S + s
                                tiles_of = slice(u + 1, u + 2) if u + 1 < KEPT[0] else slice(*KEPT[1:])
                                nc.vector.memset(acc[:, tiles_of], 0.0).then_inc(acc_zero, 1)
                            if isinstance(n, int) and n == 1 and s == S - 1:
                                dve.wait_ge(acc_zero, 2 + 2 * S)

                        def weights(n, s):
                            reused(dve, summed[s], n, n)
                            nc.vector.tensor_copy(x9[:, s], x9E[:, tiles(n, s)]).then_inc(weights_in[s], 1)
                            nc.vector.tensor_copy(dl[:, s], dlE[:, tiles(n, s)]).then_inc(weights_in[s], 1)
                            dve.wait_ge(weights_in[s], n * 2 + 2)
                            for k in range(UT):
                                nc.vector.tensor_scalar(onehot[:, s, k], nodef[:], dl[:, s, k:k + 1], None,
                                                        ALU.is_equal).then_inc(onehot_ready[s], 1)

                        def scale(n, s):
                            for k in range(UT):
                                dve.wait_ge(g_in[s * UT + k], n * 16 + 16)
                                for h in range(2, H):
                                    nc.vector.tensor_scalar(g[:, s, k, h], g[:, s, k, h], x9[:, s, k, h:h + 1], None,
                                                            ALU.mult).then_inc(scaled_dve[s], 1)

                        def tile_of(n, s):
                            if isinstance(n, int):
                                return nc.values_load_multi_w_load_instructions(
                                    trow[0:1, bass.ds(LAG + n * S + s, 1)], [dve.engine], min_val=0, max_val=NT - 1,
                                    skip_runtime_bounds_check_because=IN_RANGE)[1][0]
                            if s == S - LAG:
                                slots[:] = nc.values_load_multi_w_load_instructions(
                                    trow[0:1, bass.ds(n * S + S, S)], [dve.engine], min_val=0, max_val=NT - 1,
                                    skip_runtime_bounds_check_because=IN_RANGE)[1]
                            return slots[(s + LAG) % S]

                        IN_RANGE = "a unit's tile is its index less its group, within 0..NT-1"
                        slots = []

                        def add(n, s):
                            t = tile_of(n, s)
                            if isinstance(n, int) and n < 2:
                                dve.wait_ge(acc_zero, 2 + n * S + s)
                            dve.wait_ge(summed[s], n + 1)
                            earlier(dve, added, n, s, 1, each=2)
                            nc.vector.tensor_tensor(acc[:, t], acc[:, t], psO[:, s % 4], ALU.add).then_inc(added[s], 1)
                            nc.vector.tensor_tensor(accs[:, t], accs[:, t], psS[:, s % 4, 0:9], ALU.add).then_inc(added[s], 1)
                        pipeline(dve, S, U, [(0, weights), (0, scale), (0, zero), (LAG, add)])

                    @block.scalar
                    def _(act):
                        def scale(n, s):
                            act.wait_ge(weights_in[s], n * 2 + 2)
                            for k in range(UT):
                                act.wait_ge(g_in[s * UT + k], n * 16 + 16)
                                for h in range(2):
                                    nc.scalar.activation(g[:, s, k, h], g[:, s, k, h], ACT.Copy,
                                                         scale=x9[:, s, k, h:h + 1]).then_inc(scaled_act[s], 1)
                        pipeline(act, S, U, [(0, scale)])

                    @block.tensor
                    def _(pe):
                        def sum_unit(n, s):
                            earlier(pe, added, n, s, 4, each=2)
                            pe.wait_ge(onehot_ready[s], n * UT + UT)
                            for k in range(UT):
                                pe.wait_ge(scaled_act[s], n * (2 * UT) + (k + 1) * 2)
                                pe.wait_ge(scaled_dve[s], n * (2 * UT) + (k + 1) * 2)
                                nc.tensor.matmul(psO[:, s % 4], onehot[:, s, k], g[:, s, k].rearrange("p h o -> p (h o)"),
                                                 start=(k == 0), stop=(k == UT - 1))
                                last = nc.tensor.matmul(psS[:, s % 4, 0:9], onehot[:, s, k], x9[:, s, k],
                                                        start=(k == 0), stop=(k == UT - 1))
                            last.then_inc(summed[s], 1)
                        pipeline(pe, S, U, [(0, sum_unit)])

        def finish_nodes():
            S = 6
            with ExitStack() as c:
                woT = sb(c, "woT", [P, KD, D])
                wr = sb(c, "wr", [P, KD, 2 * NE])
                row = {name: sb(c, "row_" + name, [P, D]) for name in ("gamma", "beta", "bs2")}
                bhT = sb(c, "bhT", [P, KD])
                brow = sb(c, "brow", [1, D])
                bpart = sb(c, "bpart", [1, 3, D], BF16)
                bparts = sb(c, "bparts", [3, D], BF16)
                ones = sb(c, "onesF", [3, P], BF16)
                eself = sb(c, "eself", [P, NT, H])
                rsum = sb(c, "rsum", [P, NT, H])
                xp = sb(c, "xpF", [P, S, D])
                xin = sb(c, "xinF", [P, S, D])
                rT = sb(c, "rT", [P, 2, D])
                y = sb(c, "y", [P, 2, D])
                x1b = sb(c, "x1b", [P, 3, D])
                xl = sb(c, "xlF", [P, 3, D])
                x2T = sb(c, "x2T", [P, 2, D])
                st = sb(c, "stF", [P, S, 2, 6])
                mv = sb(c, "mvF", [P, S, 2, 2])
                ve = sb(c, "veF", [P, S, 2, 2])
                rstd = sb(c, "rstdF", [P, S, 2, 2])
                wo = xin[:, 0:KD]
                psT = ps(c, "psTF", [P, 2, D])
                psX = ps(c, "psXF", [P, 2, D])
                psY = ps(c, "psYF", [P, 3, D])
                psR = ps(c, "psRF", [P, 1, D])
                w_in, wT_turned, wT_ready, sums_ready = sem("w_inF"), sem("wT_turned"), sem("wT_ready"), sem("sums_ready")
                x_in, x_zero, passed = sems("x_inF", S), sem("x_zeroF"), sem("passedF")
                self_added, hh_ready, hT_turned, hT_ready = sems("self_added", S), sems("hh_ready", S), sems("hT_turned", S), sems("hT_ready", S)
                y_summed, y_ready, st_ready, mv_ready = sems("y_summed", S), sems("y_readyF", S), sems("st_readyF", S), sems("mv_readyF", S)
                ve_ready, rstd_ready, norm_steps = sems("ve_readyF", S), sems("rstd_readyF", S), sems("norm_steps", S)
                b_summed, b_ready, b_split, b_in = sem("b_summed"), sem("b_ready"), sem("b_split"), sem("b_in")
                xb_ready, x1_ready, x1b_ready = sems("xb_ready", S), sems("x1_ready", S), sems("x1b_ready", S)
                xl_ready, xl_turned, x2T_ready = sems("xl_readyF", S), sems("xl_turned", S), sems("x2T_ready", S)
                lg_summed, lg_ready, x2T_stored = sems("lg_summed", S), sems("lg_ready", S), sems("x2T_stored", S)
                xl_stored, z_stored = sems("xl_stored", S), sems("z_stored", S)
                LOADS = 8

                def is_last(n, j):
                    return isinstance(n, int) and n * S + j == NT - 1

                with nc.Block() as block:
                    @block.sync
                    def _(sp):
                        sp.dma_start(wo, a["W_out"].rearrange("(k p) i -> p k i", p=P)).then_inc(w_in, 16)
                        for b, bank in enumerate(("sp", "fq")):
                            sp.dma_start(wr[:, :, b * NE:(b + 1) * NE], a["Wr_" + bank].rearrange("(k p) e -> p k e", p=P)).then_inc(w_in, 16)
                        for name, to in row.items():
                            sp.dma_start(to[:], a[name].partition_broadcast(P)).then_inc(w_in, 16)
                        sp.dma_start(bhT[:], a["bias_h"].rearrange("h o -> o h")).then_inc(w_in, 16)
                        sp.dma_start(brow[:], a["b_out"].rearrange("(a o) -> a o", a=1)).then_inc(w_in, 16)

                        sp.wait_ge(wT_turned, KD)

                        def load(n, j):
                            reused(sp, hT_turned[j], n, n)
                            tile = bass.ts(n * S + j, P)
                            sp.dma_start(xp[:, j], xp_d[tile, :]).then_inc(x_in[j], 16)
                            if is_last(n, j):
                                sp.wait_ge(x_zero, 1)
                                sp.dma_start(xin[0:LAST, j], a["x"][(NT - 1) * P:N, :]).then_inc(x_in[j], 16)
                            else:
                                reused(sp, x1b_ready[j], n, n)
                                reused(sp, xl_ready[j], n, n)
                                sp.dma_start(xin[:, j], a["x"][tile, :]).then_inc(x_in[j], 16)

                        def store(n, j):
                            sp.wait_ge(xl_ready[j], n + 1)
                            sp.dma_start(xl_d[bass.ts(n * S + j, P), :], xl[:, j % 3]).then_inc(xl_stored[j], 16)
                            sp.wait_ge(x1b_ready[j], n + 1)
                            sp.dma_start(z_d[bass.ts(n * S + j, P), :], x1b[:, j % 3]).then_inc(z_stored[j], 16)
                        pipeline(sp, S, NT, [(0, load), (S - 1, store)])

                    @block.gpsimd
                    def _(pool):
                        pool.wait_ge(w_in, 16 * LOADS)

                        def add_beta(n, j):
                            if is_last(n, j):
                                pool.wait_ge(x1b_ready[j], n)
                                pool.wait_ge(xl_ready[j], n)
                                nc.gpsimd.memset(xin[:, j], 0.0).then_inc(x_zero, 1)
                            pool.wait_ge(x_in[j], n * 32 + 32)
                            nc.gpsimd.tensor_tensor(xin[:, j], xin[:, j], row["beta"][:], ALU.add).then_inc(xb_ready[j], 1)

                        def deviation(which):
                            def fn(n, j):
                                pool.wait_ge(ve_ready[j], n * 4 + which * 2 + 2)
                                nc.gpsimd.tensor_tensor(rstd[:, j, which, 0:1], ve[:, j, which, 0:1], halfneg[:],
                                                        ALU.pow).then_inc(rstd_ready[j], 1)
                                pool.wait_ge(rstd_ready[j], n * 4 + which * 2 + 1)
                                nc.gpsimd.tensor_tensor(rstd[:, j, which, 1:2], ve[:, j, which, 1:2], rstd[:, j, which, 0:1],
                                                        ALU.mult).then_inc(rstd_ready[j], 1)
                            return fn

                        def add_bs2(n, j):
                            pool.wait_ge(x1_ready[j], n + 1)
                            earlier(pool, z_stored, n, j, 3, each=16)
                            nc.gpsimd.tensor_tensor(x1b[:, j % 3], xin[:, j], row["bs2"][:], ALU.add).then_inc(x1b_ready[j], 1)
                        pipeline(pool, S, NT, [(0, add_beta), (4, deviation(1)), (2, deviation(0)), (4, add_bs2)])

                    @block.vector
                    def _(dve):
                        nc.vector.memset(ones[:], 1.0).then_inc(b_ready, 1)
                        dve.wait_ge(w_in, 16 * LOADS)
                        for k in range(KD):
                            dve.wait_ge(wT_turned, k + 1)
                            nc.vector.tensor_copy(woT[:, k], psT[:, k % 2]).then_inc(wT_ready, 1)
                        nc.vector.tensor_scalar(rsum[:], accs[:, :, 8:9].to_broadcast([P, NT, H]), -1.0, 1.0, ALU.mult, ALU.add).then_inc(sums_ready, 1)
                        dve.wait_ge(sums_ready, 1)
                        nc.vector.tensor_tensor(eself[:], accs[:, :, H:2 * H], rsum[:], ALU.add).then_inc(sums_ready, 1)
                        dve.wait_ge(sums_ready, 2)
                        nc.vector.scalar_tensor_tensor(rsum[:], accs[:, :, 0:H], 1e-16, eself[:], ALU.add, ALU.add).then_inc(sums_ready, 1)
                        dve.wait_ge(sums_ready, 3)
                        nc.vector.reciprocal(rsum[:], rsum[:]).then_inc(sums_ready, 1)
                        dve.wait_ge(sums_ready, 4)

                        dve.wait_ge(b_summed, 1)
                        nc.vector.tensor_tensor(brow[:], psR[0:1, 0], brow[:], ALU.add).then_inc(b_split, 1)
                        for i in range(3):
                            dve.wait_ge(b_split, 2 * i + 1)
                            nc.vector.tensor_copy(bpart[:, i], brow[:]).then_inc(b_split, 1)
                            dve.wait_ge(b_split, 2 * i + 2)
                            if i < 2:
                                nc.vector.tensor_tensor(brow[:], brow[:], bpart[:, i], ALU.subtract).then_inc(b_split, 1)

                        def heads(n, j):
                            t = n * S + j
                            dve.wait_ge(x_in[j], n * 32 + 32)
                            for h in range(H):
                                cols = slice(h * HD, (h + 1) * HD)
                                nc.vector.scalar_tensor_tensor(xp[:, j, cols], xp[:, j, cols], eself[:, bass.ds(t, 1), h],
                                                               acc[:, bass.ds(t, 1), cols].rearrange("p a d -> p (a d)"), ALU.mult, ALU.add
                                                               ).then_inc(self_added[j], 1)

                        def stats(v, which, n, j):
                            nc.vector.bn_stats(st[:, j, which], v).then_inc(st_ready[j], 1)
                            dve.wait_ge(st_ready[j], n * 2 + which + 1)
                            dve.sem_inc(passed, 1)
                            nc.vector.bn_aggr(mv[:, j, which], st[:, j, which]).then_inc(mv_ready[j], 1)
                            dve.wait_ge(mv_ready[j], n * 2 + which + 1)
                            nc.vector.tensor_scalar_add(ve[:, j, which, 0:1], mv[:, j, which, 1:2], EPS).then_inc(ve_ready[j], 1)
                            nc.vector.tensor_scalar_mul(ve[:, j, which, 1:2], mv[:, j, which, 0:1], -1.0).then_inc(ve_ready[j], 1)

                        def stats_out(n, j):
                            dve.wait_ge(y_summed[j], n + 1)
                            dve.sem_inc(passed, 1)
                            stats(psY[:, j % 3], 0, n, j)

                        def residual(n, j):
                            dve.wait_ge(y_ready[j], n + 1)
                            nc.vector.tensor_tensor(y[:, j % 2], y[:, j % 2], row["gamma"][:], ALU.mult).then_inc(norm_steps[j], 1)
                            dve.wait_ge(norm_steps[j], n + 1)
                            dve.wait_ge(xb_ready[j], n + 1)
                            nc.vector.tensor_tensor(xin[:, j], y[:, j % 2], xin[:, j], ALU.add).then_inc(x1_ready[j], 1)
                            dve.wait_ge(x1_ready[j], n + 1)
                            dve.sem_inc(passed, 1)
                            stats(xin[:, j], 1, n, j)
                        pipeline(dve, S, NT, [(4, residual), (2, stats_out), (0, heads)])

                    @block.tensor
                    def _(pe):
                        pe.wait_ge(w_in, 16 * LOADS)
                        for k in range(KD):
                            if k >= 2:
                                pe.wait_ge(wT_ready, k - 1)
                            for o in range(KD):
                                last = nc.tensor.transpose(psT[:, k % 2, o * P:(o + 1) * P], wo[:, o, k * P:(k + 1) * P], ident[:])
                            last.then_inc(wT_turned, 1)
                        pe.wait_ge(wT_ready, KD)
                        for k in range(KD):
                            last = nc.tensor.matmul(psR[0:1, 0], bhT[:, k:k + 1], woT[:, k], start=(k == 0), stop=(k == KD - 1))
                        last.then_inc(b_summed, 1)
                        pe.wait_ge(b_ready, 1)
                        pe.wait_ge(b_in, 16)

                        def turn(to, rows):
                            for k in range(KD):
                                last = nc.tensor.transpose(to[:, k * P:(k + 1) * P], rows[:, k * P:(k + 1) * P], ident[:])
                            return last

                        def turn_heads(n, j):
                            pe.wait_ge(hh_ready[j], n * 4 + 4)
                            earlier(pe, hT_ready, n, j, 2)
                            turn(psT[:, j % 2], xp[:, j]).then_inc(hT_turned[j], 1)

                        def project(n, j):
                            pe.wait_ge(hT_ready[j], n + 1)
                            earlier(pe, y_ready, n, j, 3)
                            nc.tensor.matmul(psY[:, j % 3], ones[:], bparts[:], start=True, stop=False)
                            for k in range(KD):
                                last = nc.tensor.matmul(psY[:, j % 3], rT[:, j % 2, k * P:(k + 1) * P], woT[:, k], start=False, stop=(k == KD - 1))
                            last.then_inc(y_summed[j], 1)

                        def turn_rows(n, j):
                            pe.wait_ge(xl_ready[j], n + 1)
                            earlier(pe, x2T_ready, n, j, 2)
                            turn(psX[:, j % 2], xl[:, j % 3]).then_inc(xl_turned[j], 1)

                        def route(n, j):
                            pe.wait_ge(x2T_ready[j], n + 1)
                            earlier(pe, lg_ready, n, j, 1)
                            for k in range(KD):
                                last = nc.tensor.matmul(psR[:, 0, 0:2 * NE], x2T[:, j % 2, k * P:(k + 1) * P], wr[:, k],
                                                        start=(k == 0), stop=(k == KD - 1))
                            last.then_inc(lg_summed[j], 1)
                        pipeline(pe, S, NT, [(5, turn_rows), (6, route), (1, project), (0, turn_heads)])

                    @block.scalar
                    def _(act):
                        act.wait_ge(b_split, 6)
                        act.dma_start(bparts[:], bpart[:]).then_inc(b_in, 16)

                        def copy_heads(n, j):
                            act.wait_ge(hT_turned[j], n + 1)
                            earlier(act, y_summed, n, j, 2)
                            nc.scalar.copy(rT[:, j % 2], psT[:, j % 2]).then_inc(hT_ready[j], 1)

                        def scale_heads(n, j):
                            act.wait_ge(self_added[j], n * 4 + 4)
                            for h in range(H):
                                cols = slice(h * HD, (h + 1) * HD)
                                nc.scalar.activation(xp[:, j, cols], xp[:, j, cols], ACT.Copy, scale=rsum[:, bass.ds(n * S + j, 1), h]).then_inc(hh_ready[j], 1)

                        def normalise(to, v, which, n, j):
                            act.wait_ge(rstd_ready[j], n * 4 + which * 2 + 2)
                            return nc.scalar.activation(to, v, ACT.Identity, bias=rstd[:, j, which, 1:2], scale=rstd[:, j, which, 0:1])

                        def normalise_out(n, j):
                            earlier(act, x1_ready, n, j, 2)
                            normalise(y[:, j % 2], psY[:, j % 3], 0, n, j).then_inc(y_ready[j], 1)

                        def normalise_residual(n, j):
                            earlier(act, xl_stored, n, j, 3, each=16)
                            earlier(act, xl_turned, n, j, 3)
                            normalise(xl[:, j % 3], xin[:, j], 1, n, j).then_inc(xl_ready[j], 1)

                        def copy_rows(n, j):
                            act.wait_ge(xl_turned[j], n + 1)
                            earlier(act, lg_summed, n, j, 2)
                            earlier(act, x2T_stored, n, j, 2, each=16)
                            nc.scalar.copy(x2T[:, j % 2], psX[:, j % 2]).then_inc(x2T_ready[j], 1)
                            act.wait_ge(x2T_ready[j], n + 1)
                            act.dma_start(x2T_d[bass.ts(n * S + j, P), :], x2T[:, j % 2]).then_inc(x2T_stored[j], 16)

                        def copy_logits(n, j):
                            act.wait_ge(lg_summed[j], n + 1)
                            nc.scalar.copy(lg[:, bass.ds(n * S + j, 1)].rearrange("p a e -> p (a e)"), psR[:, 0, 0:2 * NE]).then_inc(lg_ready[j], 1)

                        pipeline(act, S, NT, [(3, normalise_out), (5, copy_rows), (4, normalise_residual), (6, copy_logits),
                                               (0, scale_heads), (0, copy_heads)])
                        for j in range(S):
                            for stored in (xl_stored, z_stored, x2T_stored):
                                act.wait_ge(stored[j], 16 * ((NT - 1 - j) // S + 1))

        def route():
            B2 = 2 * NE
            with ExitStack() as c:
                iota8 = sb(c, "iota8", [P, B2], I32)
                iota8f = sb(c, "iota8f", [P, B2])
                prow = sb(c, "prow", [P, 1], I32)
                real = sb(c, "real", [P, 1])
                far = sb(c, "far", [P, 1])
                toki = sb(c, "toki", [P, NT], I32)
                jrow = sb(c, "jrow", [1, ET], I32)
                jrowf = sb(c, "jrowf", [1, ET])
                triu = sb(c, "triu", [P, P])
                ones = sb(c, "ones", [P, P])
                mx = sb(c, "mx", [P, 2 * NT])
                br = sb(c, "br", [P, B2])
                br_in = sem("br_in")
                ex = sb(c, "ex", [P, NT, B2])
                oh = sb(c, "oh", [P, NT, B2])
                cum = sb(c, "cum", [P, NT, B2])
                tot = sb(c, "tot", [P, NT, B2])
                pre = sb(c, "pre", [P, NT, B2])
                cnt = sb(c, "cnt", [P, B2], I32)
                nt = sb(c, "nt", [P, B2])
                nti = sb(c, "nti", [P, B2], I32)
                ends = sb(c, "ends", [P, 2, NE])
                base = sb(c, "base", [P, B2])
                slotf = sb(c, "slotf", [P, 2 * NT])
                posf = sb(c, "posf", [P, 2 * NT])
                sci = sb(c, "sci", [P, 2 * NT], I32)
                ecmp = sb(c, "ecmp", [1, 2, ET, NE])
                ef = sb(c, "ef", [1, 2, ET])
                fill = sb(c, "fill", [P, 2 * ET], I32)
                psC = ps(c, "psC", [P, 2, D])
                psN = ps(c, "psN", [P, 2, D])
                S = 6
                idx = sb(c, "idx", [P, S, 2], I32)
                tok = sb(c, "tok", [P, S], I32)
                free = rec[:, NE:].rearrange("p e c -> p (e c)")
                xT, z = free[:, 0:S * D].rearrange("p (s d) -> p s d", d=D), free[:, S * D:2 * S * D].rearrange("p (s d) -> p s d", d=D)
                free = free[:, 2 * S * D:]
                ws1, ws2 = free[:, 0:KD * FF].rearrange("p (k f) -> p k f", f=FF), free[:, KD * FF:KD * FF + FF // P * D].rearrange("p (k o) -> p k o", o=D)
                free = free[:, KD * FF + FF // P * D:]
                ys, free = free[:, 0:2 * D].rearrange("p (s d) -> p s d", d=D), free[:, 2 * D:]
                hsT, bs1 = free[:, 0:2 * FF].rearrange("p (s f) -> p s f", f=FF), free[:, 2 * FF:2 * FF + FF // P]
                psU = ps(c, "psUG", [P, 2, D])
                psD = ps(c, "psDG", [P, 2, D])
                ws_in, xT_in, z_in = sem("ws_in"), sems("xT_inG", S), sems("z_inG", S)
                up_summed, hs_ready, down_summed = sems("up_summedG", S), sems("hs_ready", S), sems("down_summedG", S)
                ys_ready, z_ready, z_stored = sems("ys_ready", S), sems("z_ready", S), sems("z_storedG", S)
                staged, scattered = sems("staged", S), sems("scattered", S)
                g1, gz, g2, g3, g4, filled = sem("g1"), sem("gz"), sem("g2"), sem("g3"), sem("g4"), sem("filled")
                e_ready, e_done, perm_in, passed = sem("e_ready"), sem("e_done"), sem("perm_in"), sem("passedG")
                banks = "p t (b e) -> p (t b) e"
                assert NT // S == NE
                halves = (slice(0, NT // 2), slice(NT // 2, NT))

                def total_on(eng, unit, first):
                    def fn(n, j):
                        if (isinstance(n, int) and n < 2) == first:
                            eng.wait_ge(z_in[j], n * 16 + 16)
                            eng.wait_ge(ys_ready[j], n + 1)
                            unit.tensor_tensor(z[:, j], ys[:, j % 2], z[:, j], ALU.add).then_inc(z_ready[j], 1)
                    return fn

                with nc.Block() as block:
                    @block.gpsimd
                    def _(pool):
                        nc.gpsimd.iota(iota8[:], [[0, 2], [1, NE]], base=0, channel_multiplier=0).then_inc(gz, 1)
                        nc.gpsimd.iota(prow[:], [[0, 1]], base=0, channel_multiplier=1).then_inc(gz, 1)
                        nc.gpsimd.iota(toki[:], [[P, NT]], base=0, channel_multiplier=1).then_inc(gz, 1)
                        nc.gpsimd.iota(jrow[:], [[1, ET]], base=0, channel_multiplier=0).then_inc(gz, 1)
                        nc.gpsimd.memset(ones[:], 1.0).then_inc(gz, 1)
                        nc.gpsimd.memset(fill[:], NP - 1).then_inc(gz, 1)
                        nc.gpsimd.memset(triu[:], 1.0).then_inc(gz, 1)
                        pool.wait_ge(gz, 7)
                        nc.gpsimd.affine_select(out=triu[:], in_=triu[:], compare_op=ALU.is_ge, fill=0.0,
                                                base=0, pattern=[[1, P]], channel_multiplier=-1).then_inc(gz, 1)
                        pool.wait_ge(filled, 16)

                        def scatter(n, j):
                            pool.wait_ge(staged[j], n * 2 + 2)
                            pool.sem_inc(passed, 1)
                            for b in range(2):
                                pool.indirect_dma_start(perm_d, bass.IndirectOffsetOnAxis(ap=idx[:, j, b:b + 1], axis=0),
                                                        tok[:, j:j + 1], None, bounds_check=2 * ET * P - 1,
                                                        oob_is_err=False).then_inc(scattered[j], 16)
                        pipeline(pool, S, NT, [(0, total_on(pool, nc.gpsimd, True)), (4, scatter)])

                    @block.sync
                    def _(sp):
                        for b, bank in enumerate(("sp", "fq")):
                            sp.dma_start(br[:, b * NE:(b + 1) * NE], a["br_" + bank].partition_broadcast(P)).then_inc(br_in, 16)
                        sp.dma_start(ws1, a["Ws1"].rearrange("(k p) f -> p k f", p=P)).then_inc(ws_in, 16)
                        sp.dma_start(ws2, a["Ws2"].rearrange("(k p) o -> p k o", p=P)).then_inc(ws_in, 16)
                        sp.dma_start(bs1, a["bs1"].rearrange("(f p) -> p f", p=P)).then_inc(ws_in, 16)
                        sp.wait_ge(gz, 8)
                        sp.dma_start(perm_d.rearrange("(p j) a -> p (j a)", p=P), fill[:]).then_inc(filled, 16)

                        def load(n, j):
                            tile = bass.ts(n * S + j, P)
                            reused(sp, up_summed[j], n, n)
                            sp.dma_start(xT[:, j], x2T_d[tile, :]).then_inc(xT_in[j], 16)
                            reused(sp, z_stored[j], n * 16, n)
                            sp.dma_start(z[:, j], z_d[tile, :]).then_inc(z_in[j], 16)

                        def load_expert(n, j):
                            if j == S - 1:
                                load_weights(sp, "sp", NE - 1 - n if isinstance(n, int) else n - 2)
                        pipeline(sp, S, NT, [(0, load), (0, load_expert)])
                        for j in range(S):
                            sp.wait_ge(scattered[j], 32 * ((NT - 1 - j) // S + 1))
                        sp.dma_start(perm[:], perm_d.rearrange("(j p) a -> p (j a)", p=P)).then_inc(perm_in, 16)
                        sp.wait_ge(perm_in, 16)

                    @block.scalar
                    def _(act):
                        act.wait_ge(ws_in, 48)

                        def exp(n, j):
                            if isinstance(n, int) and n * S + j == 1:
                                act.wait_ge(e_ready, 1)
                                nc.scalar.activation(ex[:], ex[:], ACT.Exp).then_inc(e_done, 1)

                        def gelu(n, j):
                            act.wait_ge(up_summed[j], n + 1)
                            earlier(act, down_summed, n, j, 2)
                            for f in range(FF // P):
                                cols = slice(f * P, (f + 1) * P)
                                nc.scalar.activation(hsT[:, j % 2, cols], psU[:, j % 2, cols], ACT.Gelu, bias=bs1[:, f:f + 1]).then_inc(hs_ready[j], 1)

                        def copy_down(n, j):
                            act.wait_ge(down_summed[j], n + 1)
                            earlier(act, z_ready, n, j, 2)
                            nc.scalar.copy(ys[:, j % 2], psD[:, j % 2]).then_inc(ys_ready[j], 1)

                        def store(n, j):
                            act.wait_ge(z_ready[j], n + 1)
                            act.dma_start(z_d[bass.ts(n * S + j, P), :], z[:, j]).then_inc(z_stored[j], 16)
                        pipeline(act, S, NT, [(0, gelu), (1, copy_down), (0, exp), (3, store)])
                        for j in range(S):
                            act.wait_ge(z_stored[j], 16 * ((NT - 1 - j) // S + 1))

                    @block.tensor
                    def _(pe):
                        def count(n, j):
                            if not isinstance(n, int) or n * S + j != 3:
                                return
                            pe.wait_ge(gz, 8)
                            pe.wait_ge(g2, 1)
                            for m, w in enumerate(halves):
                                cols = (w.stop - w.start) * B2
                                nc.tensor.matmul(psC[:, m, 0:cols], triu[:], oh[:, w].rearrange("p t e -> p (t e)"), start=True, stop=True)
                                nc.tensor.matmul(psN[:, m, 0:cols], ones[:], oh[:, w].rearrange("p t e -> p (t e)"), start=True, stop=True).then_inc(g3, 1)
                        pe.wait_ge(ws_in, 48)

                        def up(n, j):
                            pe.wait_ge(xT_in[j], n * 16 + 16)
                            earlier(pe, hs_ready, n, j, 2, each=2)
                            for f in range(FF // P):
                                for k in range(KD):
                                    last = nc.tensor.matmul(psU[:, j % 2, f * P:(f + 1) * P], ws1[:, k, f * P:(f + 1) * P],
                                                            xT[:, j, k * P:(k + 1) * P], start=(k == 0), stop=(k == KD - 1))
                            last.then_inc(up_summed[j], 1)

                        def down(n, j):
                            pe.wait_ge(hs_ready[j], n * 2 + 2)
                            earlier(pe, ys_ready, n, j, 2)
                            for f in range(FF // P):
                                last = nc.tensor.matmul(psD[:, j % 2], hsT[:, j % 2, f * P:(f + 1) * P], ws2[:, f], start=(f == 0), stop=(f == FF // P - 1))
                            last.then_inc(down_summed[j], 1)
                        pipeline(pe, S, NT, [(0, count), (0, up), (1, down)])

                    @block.vector
                    def _(dve):
                        count = [0]

                        def link(ins):
                            count[0] += 1
                            ins.then_inc(g1, 1)
                            dve.wait_ge(g1, count[0])

                        dve.wait_ge(gz, 8)
                        link(nc.vector.tensor_copy(iota8f[:], iota8[:]))
                        link(nc.vector.tensor_copy(far[:], prow[:]))
                        link(nc.vector.tensor_scalar(real[:], far[:], float(LAST), None, ALU.is_lt))
                        link(nc.vector.tensor_scalar(far[:], real[:], -30000.0, 30000.0, ALU.mult, ALU.add))
                        lgb, exb, ohb = lg[:].rearrange(banks, b=2), ex[:].rearrange(banks, b=2), oh[:].rearrange(banks, b=2)
                        dve.wait_ge(br_in, 32)
                        link(nc.vector.tensor_tensor(lg[:], lg[:], br[:].unsqueeze(1).to_broadcast([P, NT, B2]), ALU.add))
                        link(nc.vector.tensor_reduce(mx[:], lgb, AX_X, ALU.max))
                        link(nc.vector.tensor_tensor(ohb, lgb, mx[:].unsqueeze(2).to_broadcast([P, 2 * NT, NE]), ALU.subtract))
                        link(nc.vector.tensor_copy(ex[:], oh[:]))
                        nc.vector.memset(slotf[:], 0.0).then_inc(e_ready, 1)
                        link(nc.vector.tensor_scalar(oh[:], oh[:], 0.0, -float(NE), ALU.is_equal, ALU.mult))
                        link(nc.vector.tensor_tensor(oh[:], oh[:], iota8f[:].unsqueeze(1).to_broadcast([P, NT, B2]), ALU.add))
                        link(nc.vector.tensor_reduce(mx[:], ohb, AX_X, ALU.min))
                        link(nc.vector.tensor_tensor(ohb, ohb, mx[:].unsqueeze(2).to_broadcast([P, 2 * NT, NE]), ALU.is_equal))
                        nc.vector.tensor_scalar(oh[:, NT - 1], oh[:, NT - 1], real[:, 0:1], None, ALU.mult).then_inc(g2, 1)
                        dve.wait_ge(e_done, 1)
                        link(nc.vector.tensor_reduce(gate[:], exb, AX_X, ALU.add))
                        link(nc.vector.reciprocal(gate[:], gate[:]))
                        dve.wait_ge(g3, 2)
                        for m, w in enumerate(halves):
                            cols = (w.stop - w.start) * B2
                            link(nc.vector.tensor_copy(cum[:, w].rearrange("p t e -> p (t e)"), psC[:, m, 0:cols]))
                            link(nc.vector.tensor_copy(tot[:, w].rearrange("p t e -> p (t e)"), psN[:, m, 0:cols]))
                        for k in range(B2):
                            link(nc.vector.tensor_tensor_scan(pre[:, :, k], ones[:, 0:NT], tot[:, :, k], 0.0, ALU.mult, ALU.add))
                        link(nc.vector.tensor_scalar(nt[:], pre[:, NT - 1], float(P - 1), None, ALU.add))
                        link(nc.vector.tensor_tensor(cum[:], cum[:], pre[:], ALU.add))
                        link(nc.vector.scalar_tensor_tensor(cum[:], cum[:], -1.0, tot[:], ALU.add, ALU.subtract))
                        link(nc.vector.tensor_copy(cnt[:], nt[:]))
                        link(nc.vector.tensor_scalar(nti[:], cnt[:], 7, None, ALU.arith_shift_right))
                        link(nc.vector.tensor_copy(nt[:], nti[:]))
                        for b in range(2):
                            link(nc.vector.tensor_tensor_scan(ends[:, b], ones[:, 0:NE], nt[:, b * NE:(b + 1) * NE], 0.0, ALU.mult, ALU.add))
                            link(nc.vector.tensor_tensor(base[:, b * NE:(b + 1) * NE], ends[:, b], nt[:, b * NE:(b + 1) * NE], ALU.subtract))
                            link(nc.vector.tensor_scalar(base[:, b * NE:(b + 1) * NE], base[:, b * NE:(b + 1) * NE], float(P), float(b * ET * P),
                                                         ALU.mult, ALU.add))
                        cumb = cum[:].rearrange(banks, b=2)
                        link(nc.vector.tensor_tensor(tot[:], cum[:], oh[:], ALU.mult))
                        link(nc.vector.tensor_reduce(posf[:], tot[:].rearrange(banks, b=2), AX_X, ALU.add))
                        link(nc.vector.tensor_tensor(cum[:], cum[:], base[:].unsqueeze(1).to_broadcast([P, NT, B2]), ALU.add))
                        link(nc.vector.tensor_tensor(cum[:], cum[:], oh[:], ALU.mult))
                        link(nc.vector.tensor_reduce(slotf[:], cumb, AX_X, ALU.add))
                        link(nc.vector.tensor_copy(slot[:].rearrange("p t b -> p (t b)"), slotf[:]))
                        link(nc.vector.tensor_scalar(slotf[:, 2 * NT - 2:2 * NT], slotf[:, 2 * NT - 2:2 * NT], far[:, 0:1], None, ALU.add))
                        link(nc.vector.tensor_copy(sci[:], slotf[:]))
                        link(nc.vector.scalar_tensor_tensor(gate[:], posf[:], float(CAP), gate[:], ALU.is_lt, ALU.mult))
                        link(nc.vector.tensor_copy(jrowf[:], jrow[:]))
                        for b in range(2):
                            link(nc.vector.tensor_tensor(ecmp[:, b], ends[0:1, b].unsqueeze(1).to_broadcast([1, ET, NE]),
                                                         jrowf[:].unsqueeze(2).to_broadcast([1, ET, NE]), ALU.is_le))
                            link(nc.vector.tensor_reduce(ef[:, b], ecmp[:, b], AX_X, ALU.add))
                            link(nc.vector.tensor_scalar(ef[:, b], ef[:, b], float(NE - 1), float(b * NE), ALU.min, ALU.add))
                        link(nc.vector.tensor_copy(erow[0:1, 4:], ef[:].rearrange("a b j -> a (b j)")))

                        def stage(n, j):
                            reused(dve, scattered[j], n * 32, n)
                            nc.vector.tensor_copy(idx[:, j], sci[:, bass.ds((n * S + j) * 2, 2)]).then_inc(staged[j], 1)
                            nc.vector.tensor_copy(tok[:, j:j + 1], toki[:, bass.ds(n * S + j, 1)]).then_inc(staged[j], 1)
                        pipeline(dve, S, NT, [(0, total_on(dve, nc.vector, False)), (0, stage)])

        def experts():
            S = 4
            UP, DOWN = 1, 3
            with ExitStack() as c:
                ix = sb(c, "ixH", [P, S], I32)
                xr = sb(c, "xr", [P, S, D])
                xT = sb(c, "xTH", [P, 2, D])
                hp = sb(c, "hp", [P, 2, FF])
                hr = sb(c, "hr", [P, 2, FF])
                hT = sb(c, "hT", [P, 2, FF])
                y = sb(c, "yH", [P, 2, D])
                psT = ps(c, "psTH", [P, 2, D])
                psU = ps(c, "psUH", [P, 2, D])
                psH = ps(c, "psHH", [P, 2, D])
                psD = ps(c, "psDH", [P, 2, D])
                ix_in, x_in, x_turned, xT_ready = sems("ix_inH", S), sems("x_inH", S), sems("x_turnedH", S), sems("xT_readyH", S)
                up_summed, h_biased, h_ready, h_turned = sems("up_summedH", S), sems("h_biased", S), sems("h_readyH", S), sems("h_turned", S)
                hT_ready, down_summed, y_ready, y_stored = sems("hT_readyH", S), sems("down_summedH", S), sems("y_readyH", S), sems("y_storedH", S)
                passed, second_in = sem("passedH"), sem("second_in")

                def experts_of(eng):
                    window = []

                    def load(first, count):
                        return nc.values_load_multi_w_load_instructions(
                            erow[0:1, bass.ds(first, count)], [eng.engine], min_val=0, max_val=2 * NE - 1,
                            skip_runtime_bounds_check_because="a count of ends, held to the bank's experts")[1]

                    def load_round(n, j):
                        if j == 0 and not isinstance(n, int):
                            window[:] = load(n * S, 2 * S)

                    def expert(n, j, lag):
                        if isinstance(n, int):
                            return load(S + n * S + j, 1)[0]
                        return window[S + j] if j + lag < S else window[j]
                    return load_round, expert

                ROUNDS, FIRST = 2 * ET // S, 2 * ET // S - SUMMED // S
                free = rec[:, 0:NE].rearrange("p e c -> p (e c)")
                part_y = free[:, SUMMED * D:(SUMMED + S) * D].rearrange("p (s d) -> p s d", d=D)
                part_ix = sb(c, "part_ix", [P, S], I32)
                part_ix_in, part_y_in, part_z_in = sems("part_ix_in", S), sems("part_y_in", S), sems("part_z_in", S)
                part_ready = sems("part_ready", S)
                assert ET % S == 0 and SUMMED % S == 0 and FIRST >= ET // S + 2 and SUMMED < NT

                def nothing():
                    pass

                def first_bank(eng):
                    eng.wait_ge(banks_in, 64 * NE)
                    return [(ET // S, (), lambda: eng.wait_ge(second_in, 64 * NE))]

                def with_parts(part, before=nothing):
                    return [(FIRST, (), before), (FIRST + 1, [(0, lambda n, j: part(True, n, j))], nothing),
                            (ROUNDS, [(0, lambda n, j: part(False, n, j))], nothing)]

                with nc.Block() as block:
                    @block.sync
                    def _(sp):
                        def load_expert(n, j):
                            if j == 0:
                                load_weights(sp, "fq", n - 2, second_in)

                        def indices(n, j):
                            reused(sp, x_in[j], n * 16, n)
                            sp.dma_start(ix[:, j:j + 1], perm[:, bass.ds(n * S + j, 1)]).then_inc(ix_in[j], 16)
                        
                        def load_part(first, n, j):
                            if not first:
                                sp.wait_ge(part_y_in[j], (n - FIRST) * 16)
                            sp.dma_start(part_ix[:, j:j + 1], slot[:, bass.ds((n - FIRST) * S + j, 1), 0]).then_inc(part_ix_in[j], 16)
                            if not first:
                                sp.wait_ge(part_ready[j], n - FIRST)
                            sp.dma_start(sums_z[:, bass.ds((n - FIRST) * S + j, 1)].rearrange("p a d -> p (a d)"),
                                         z_d[bass.ts((n - FIRST) * S + j, P), :]).then_inc(part_z_in[j], 16)

                        pipeline(sp, S, 2 * ET, [(0, indices)], [
                            (2 + NE, [(0, load_expert)], nothing),
                            *with_parts(load_part, lambda: sp.wait_ge(y_ready[S - 1], ET // S))])

                    @block.gpsimd
                    def _(pool):
                        def gather(n, j):
                            pool.wait_ge(ix_in[j], n * 16 + 16)
                            reused(pool, x_turned[j], n, n)
                            pool.sem_inc(passed, 1)
                            pool.indirect_dma_start(xr[:, j], None, xl_d, bass.IndirectOffsetOnAxis(ap=ix[:, j:j + 1], axis=0)
                                                    ).then_inc(x_in[j], 16)

                        def gather_part(first, n, j):
                            pool.wait_ge(part_ix_in[j], (n - FIRST + 1) * 16)
                            if not first:
                                pool.wait_ge(part_ready[j], n - FIRST)
                            pool.sem_inc(passed, 1)
                            pool.indirect_dma_start(part_y[:, j], None, y_d[0:ET * P, :], bass.IndirectOffsetOnAxis(ap=part_ix[:, j:j + 1], axis=0)
                                                    ).then_inc(part_y_in[j], 16)

                        def outputs_stored():
                            for j in range(S):
                                pool.wait_ge(y_stored[j], ET // S * 16)
                        pipeline(pool, S, 2 * ET, [(0, gather)], with_parts(gather_part, outputs_stored))

                    @block.tensor
                    def _(pe):
                        second_bank = first_bank(pe)
                        load_round, expert = experts_of(pe)

                        def turn_rows(n, j):
                            pe.wait_ge(x_in[j], n * 16 + 16)
                            earlier(pe, xT_ready, n, j, 2)
                            for k in range(KD):
                                last = nc.tensor.transpose(psT[:, j % 2, k * P:(k + 1) * P], xr[:, j, k * P:(k + 1) * P], ident[:])
                            last.then_inc(x_turned[j], 1)

                        def up(n, j):
                            e = expert(n, j, UP)
                            pe.wait_ge(xT_ready[j], n + 1)
                            earlier(pe, h_biased, n, j, 2)
                            for k in range(KD):
                                last = nc.tensor.matmul(psU[:, j % 2, 0:FF], xT[:, j % 2, k * P:(k + 1) * P], w1[:, e, k],
                                                        start=(k == 0), stop=(k == KD - 1))
                            last.then_inc(up_summed[j], 1)

                        def turn_hidden(n, j):
                            pe.wait_ge(h_ready[j], n + 1)
                            earlier(pe, hT_ready, n, j, 2)
                            for f in range(FF // P):
                                last = nc.tensor.transpose(psH[:, j % 2, f * P:(f + 1) * P], hr[:, j % 2, f * P:(f + 1) * P], ident[:])
                            last.then_inc(h_turned[j], 1)

                        def down(n, j):
                            e = expert(n, j, DOWN)
                            pe.wait_ge(hT_ready[j], n + 1)
                            earlier(pe, y_ready, n, j, 2)
                            for f in range(FF // P):
                                last = nc.tensor.matmul(psD[:, j % 2], hT[:, j % 2, f * P:(f + 1) * P], w2[:, e, f],
                                                        start=(f == 0), stop=(f == FF // P - 1))
                            last.then_inc(down_summed[j], 1)
                        pipeline(pe, S, 2 * ET, [(0, load_round), (0, turn_rows), (UP, up), (2, turn_hidden), (DOWN, down)], second_bank)

                    @block.scalar
                    def _(act):
                        def copy_rows(n, j):
                            act.wait_ge(x_turned[j], n + 1)
                            earlier(act, up_summed, n, j, 2)
                            nc.scalar.copy(xT[:, j % 2], psT[:, j % 2]).then_inc(xT_ready[j], 1)

                        def gelu(n, j):
                            act.wait_ge(h_biased[j], n + 1)
                            earlier(act, h_turned, n, j, 2)
                            nc.scalar.activation(hr[:, j % 2], hp[:, j % 2], ACT.Gelu).then_inc(h_ready[j], 1)

                        def store(n, j):
                            act.wait_ge(y_ready[j], n + 1)
                            act.dma_start(y_d[bass.ts(n * S + j, P), :], y[:, j % 2]).then_inc(y_stored[j], 16)
                        pipeline(act, S, 2 * ET, [(0, copy_rows), (UP, gelu), (DOWN, store)])
                        for j in range(S):
                            act.wait_ge(y_stored[j], 16 * (2 * ET // S))

                    @block.vector
                    def _(dve):
                        second_bank = first_bank(dve)
                        load_round, expert = experts_of(dve)

                        def bias_up(n, j):
                            e = expert(n, j, UP)
                            dve.wait_ge(up_summed[j], n + 1)
                            earlier(dve, h_ready, n, j, 2)
                            nc.vector.tensor_tensor(hp[:, j % 2], psU[:, j % 2, 0:FF], b1[:, e], ALU.add).then_inc(h_biased[j], 1)

                        def copy_hidden(n, j):
                            dve.wait_ge(h_turned[j], n + 1)
                            earlier(dve, down_summed, n, j, 2)
                            nc.vector.tensor_copy(hT[:, j % 2], psH[:, j % 2, 0:FF]).then_inc(hT_ready[j], 1)

                        def bias_down(n, j):
                            e = expert(n, j, DOWN)
                            dve.wait_ge(down_summed[j], n + 1)
                            earlier(dve, y_stored, n, j, 2, each=16)
                            nc.vector.tensor_tensor(y[:, j % 2], psD[:, j % 2], b2[:, e], ALU.add).then_inc(y_ready[j], 1)

                        def add_part(first, n, j):
                            dve.wait_ge(part_z_in[j], (n - FIRST + 1) * 16)
                            dve.wait_ge(part_y_in[j], (n - FIRST + 1) * 16)
                            total = sums_z[:, bass.ds((n - FIRST) * S + j, 1)].rearrange("p a d -> p (a d)")
                            nc.vector.scalar_tensor_tensor(total, part_y[:, j], gate[:, bass.ds(((n - FIRST) * S + j) * 2, 1)], total,
                                                           ALU.mult, ALU.add).then_inc(part_ready[j], 1)
                        pipeline(dve, S, 2 * ET, [(0, load_round), (UP, bias_up), (2, copy_hidden), (DOWN, bias_down)],
                                 second_bank + with_parts(add_part))

        def combine():
            S, REST = 6, NT - SUMMED
            assert REST <= 2 * S
            with ExitStack() as c:
                ix = sb(c, "ixI", [P, S], I32)
                free = rec[:, NE:].rearrange("p e c -> p (e c)")
                yb, y0, zr = (free[:, k * D:(k + m) * D].rearrange("p (s d) -> p s d", d=D)
                              for k, m in ((0, S), (S, REST), (S + REST, REST)))
                ix_in, y_in, y0_in, z_in = sems("ix_inI", S), sems("y_inI", S), sems("y0_inI", REST), sem("z_inI")
                part, o_ready, stored, passed = sem("partI"), sems("o_ready", S), sems("storedI", S), sem("passedI")

                def tile_at(n, s):
                    q = n * S + s
                    return (SUMMED + q, True) if isinstance(q, int) and q < REST else (q - REST, False)

                def total_of(n, s):
                    t, rest = tile_at(n, s)
                    return zr[:, t - SUMMED] if rest else sums_z[:, bass.ds(t, 1)].rearrange("p a d -> p (a d)")

                with nc.Block() as block:
                    @block.sync
                    def _(sp):
                        sp.dma_start(zr, z_d[SUMMED * P:, :].rearrange("(t p) d -> p t d", p=P)).then_inc(z_in, 16)

                        def load(n, s):
                            reused(sp, y_in[s], n * 16, n)
                            t, _ = tile_at(n, s)
                            sp.dma_start(ix[:, s:s + 1], slot[:, bass.ds(t, 1), 1]).then_inc(ix_in[s], 16)
                        pipeline(sp, S, NT, [(0, load)])

                    @block.gpsimd
                    def _(pool):
                        def gather(n, s):
                            t, rest = tile_at(n, s)
                            if rest:
                                pool.indirect_dma_start(y0[:, t - SUMMED], None, y_d, bass.IndirectOffsetOnAxis(ap=slot[:, t, 0:1], axis=0)
                                                        ).then_inc(y0_in[t - SUMMED], 16)
                            pool.wait_ge(ix_in[s], n * 16 + 16)
                            reused(pool, o_ready[s], n, n)
                            pool.sem_inc(passed, 1)
                            pool.indirect_dma_start(yb[:, s], None, y_d, bass.IndirectOffsetOnAxis(ap=ix[:, s:s + 1], axis=0)
                                                    ).then_inc(y_in[s], 16)
                        pipeline(pool, S, NT, [(0, gather)])

                    @block.vector
                    def _(dve):
                        dve.wait_ge(z_in, 16)

                        def add(n, s):
                            t, rest = tile_at(n, s)
                            total = total_of(n, s)
                            first, second = (gate[:, bass.ds(t * 2 + b, 1)] for b in range(2))
                            if rest:
                                dve.wait_ge(y0_in[t - SUMMED], 16)
                                nc.vector.scalar_tensor_tensor(total, y0[:, t - SUMMED], first, total, ALU.mult, ALU.add).then_inc(part, 1)
                                dve.wait_ge(part, t - SUMMED + 1)
                            dve.wait_ge(y_in[s], n * 16 + 16)
                            nc.vector.scalar_tensor_tensor(total, yb[:, s], second, total, ALU.mult, ALU.add).then_inc(o_ready[s], 1)
                        pipeline(dve, S, NT, [(0, add)])

                    @block.scalar
                    def _(act):
                        def store(n, s):
                            act.wait_ge(o_ready[s], n + 1)
                            t, _ = tile_at(n, s)
                            if isinstance(t, int) and t == NT - 1:
                                act.dma_start(out[(NT - 1) * P:N, :], total_of(n, s)[0:LAST]).then_inc(stored[s], 16)
                            else:
                                act.dma_start(out[bass.ts(t, P), :], total_of(n, s)).then_inc(stored[s], 16)
                        pipeline(act, S, NT, [(0, store)])
                        for s in range(S):
                            act.wait_ge(stored[s], 16 * ((NT - 1 - s) // S + 1))

        phase(constants)
        aN = sb(edges, "aN", [P, NT, 2 * H])
        phase(project_nodes)
        if phases >= 2:
            with ExitStack() as soft:
                dstR = sb(soft, "dstR", [CP, NC, GE])
                dlR = sb(soft, "dlR", [CP, NC, GE])
                tbase = sb(soft, "tbase", [CP, NC])
                with ExitStack() as raw:
                    srcR = sb(raw, "srcR", [CP, NC, GE])
                    hiR = sb(raw, "hiR", [CP, NC, GE])
                    srcRi = sb(raw, "srcRi", [CP, NC, GE], I32)
                    dstRi = sb(raw, "dstRi", [CP, NC, GE], I32)
                    phase(plan_units)
                    phase(rows_to_edges, ((srcR, srcE[:]), (hiR, hiE[:]), (dlR, dlE[:])), "B")
                aR, rest = acc[0:CP, 0:3 * H * NC * GE], acc[0:CP, 3 * H * NC * GE:]
                aR = aR.rearrange("p (j q e) -> p j q e", j=3 * H, q=NC)
                aE = acc[:, 3 * H * NC * GE:3 * H * NC * GE + TU * 3 * H].rearrange("p (t j) -> p t j", t=TU)
                phase(gather_logits)
                phase(edges_to_rows)
                parts = rest[:, 0:12 * NC * GE].rearrange("p (j q e) -> p j q e", j=12, q=NC)
                fwd, bwd, penv, last1, penf, penb = parts[:, 0:H], parts[:, H:2 * H], parts[:, 8], parts[:, 9], parts[:, 10], parts[:, 11]
                phase(edge_softmax)
                col = 3 * H * NC * GE + 9 * NC * GE
                KEPT = (2 * H * NC * GE // D, col // D, (col + NC * GE) // D)
                assert col % D == 0
                phase(rows_to_edges, [(aR[:, h], x9E[:, :, h]) for h in range(2 * H)] + [(last1, x9E[:, :, 8])], "D",
                      (acc[:, 3 * H * NC * GE:col], acc[:, KEPT[0] * D:3 * H * NC * GE], acc[:, KEPT[2] * D:NT * D]))
                if scratch != "Internal" and phases == 2:
                    x9_d = dram("x9_d", [P, TU, 9])
                    with nc.Block() as block:
                        @block.sync
                        def _(sp):
                            x9o = sem("x9o")
                            sp.dma_start(x9_d, x9E[:]).then_inc(x9o, 16)
                            sp.wait_ge(x9o, 16)
        if phases >= 3:
            xl_d = dram("xl_d", [NP, D])
            x2T_d = dram("x2T_d", [NP, D])
            z_d = dram("z_d", [NP, D])
            y_d = dram("y_d", [2 * ET * P, D])
            perm_d = dram("perm_d", [2 * ET * P, 1], I32)
            with sums:
                with edges:
                    acc = acc[:].rearrange("p (t d) -> p t d", d=D)
                    phase(aggregate)
                if scratch != "Internal" and phases == 3:
                    acc_d, accs_d = dram("acc_d", [P, NT, D]), dram("accs_d", [P, NT, 9])
                    with nc.Block() as block:
                        @block.sync
                        def _(sp):
                            x9o = sem("x9o")
                            sp.dma_start(acc_d, acc).then_inc(x9o, 16)
                            sp.dma_start(accs_d, accs[:]).then_inc(x9o, 16)
                            sp.wait_ge(x9o, 32)
                if phases > 3:
                    phase(finish_nodes)
            if phases > 4:
                gate = sb(ctx, "gate", [P, 2 * NT])
                slot = sb(ctx, "slot", [P, NT, 2], I32)
                perm = sb(ctx, "perm", [P, 2 * ET], I32)
                erow = sb(ctx, "erow", [1, 4 + 2 * ET], I32)
                with ExitStack() as weights:
                    rec = sb(weights, "rec", [P, 2 * NE, KD * FF + FF // P * D + FF + D])
                    W2, B1, B2 = KD * FF, KD * FF + FF // P * D, KD * FF + FF // P * D + FF
                    w1 = rec[:, :, 0:W2].rearrange("p e (k f) -> p e k f", f=FF)
                    w2 = rec[:, :, W2:B1].rearrange("p e (k o) -> p e k o", o=D)
                    b1, b2 = rec[:, :, B1:B2], rec[:, :, B2:]
                    banks_in = ctx.enter_context(nc.semaphore("banks_in"))

                    def load_weights(eng, bank, e, signal=banks_in):
                        to, e = bass.ds(e + NE * (bank == "fq"), 1), bass.ds(e, 1)
                        for rows, k in ((w1, "W1_"), (w2, "W2_")):
                            eng.dma_start(rows[:, to].rearrange("p e k f -> p (e k) f"), a[k + bank][e].rearrange("e (k p) f -> p (e k) f", p=P)
                                          ).then_inc(signal, 16)
                        for rows, k in ((b1, "b1_"), (b2, "b2_")):
                            eng.dma_start(rows[:, to].rearrange("p e f -> p (e f)"), a[k + bank][e].rearrange("e f -> (e f)").partition_broadcast(P)
                                          ).then_inc(signal, 16)
                    phase(route)
                    sums_z = rec[:, 0:NE].rearrange("p e c -> p (e c)")[:, 0:SUMMED * D].rearrange("p (t d) -> p t d", d=D)
                    phase(experts)
                    phase(combine)


_INS = {"x": "x", "src": "src", "dst": "dst", "Wh": "L0_gnn_Wh", "att_src": "L0_gnn_att_src", "att_dst": "L0_gnn_att_dst",
        "bias_h": "L0_gnn_bias_h", "W_out": "L0_gnn_W_out", "b_out": "L0_gnn_b_out", "gamma": "L0_gnn_gamma",
        "beta": "L0_gnn_beta", "Wr_sp": "L0_ffn_Wr_sp", "br_sp": "L0_ffn_br_sp", "Wr_fq": "L0_ffn_Wr_fq",
        "br_fq": "L0_ffn_br_fq", "Ws1": "L0_ffn_Ws1", "bs1": "L0_ffn_bs1", "Ws2": "L0_ffn_Ws2", "bs2": "L0_ffn_bs2",
        "W1_sp": "L0_ffn_W1_sp", "b1_sp": "L0_ffn_b1_sp", "W2_sp": "L0_ffn_W2_sp", "b2_sp": "L0_ffn_b2_sp",
        "W1_fq": "L0_ffn_W1_fq", "b1_fq": "L0_ffn_b1_fq", "W2_fq": "L0_ffn_W2_fq", "b2_fq": "L0_ffn_b2_fq"}
SCRATCH, PHASES = "Internal", 9


def kernel(**inputs):
    import numpy as np
    import concourse.bacc as bacc
    from concourse.bass_utils import run_bass_kernel_spmd as run

    nc = bacc.Bacc("TRN2", target_bir_lowering=False, num_devices=1)
    arrays, aps = {}, {}
    for short, name in _INS.items():
        arrays["in_" + short] = v = np.ascontiguousarray(inputs[name])
        aps[short] = nc.dram_tensor("in_" + short, v.shape, mybir.dt.from_np(v.dtype), kind="ExternalInput").ap()
    out = nc.dram_tensor("out_x", (N, D), F32, kind="ExternalOutput").ap()
    build(nc, aps, out, SCRATCH, PHASES)
    r = run(nc, [arrays], core_ids=[0])
    return r.results[0]["out_x"]
```
